# Optimizing a Trainium2 kernel written in Bass

```python
import numpy as np
import jax
import jax.numpy as jnp

def _softmax(x, axis=-1):
    return jax.nn.softmax(x, axis=axis)

def _gelu(x):
    return jax.nn.gelu(x, approximate=True)

def _silu(x):
    return jax.nn.silu(x)

def _sigmoid(x):
    return jax.nn.sigmoid(x)

def _layernorm(x, axis=-1, eps=1e-05):
    m = jnp.mean(x, axis=axis, keepdims=True)
    v = jnp.var(x, axis=axis, keepdims=True)
    return (x - m) / jnp.sqrt(v + eps)

def _scatter_add(tgt, idx, src, axis=0):
    return tgt.at[idx].add(src)

def _segment_sum(src, seg, n):
    return jax.ops.segment_sum(src, seg, n)
kernel_name = 'mk_perceiver_d2_seqx_r4_5ff718'

def setup_inputs(seed: int=0):
    np.random.seed(seed)
    _w = jnp.asarray

    def _rec_inputs():
        import jax
        import jax.numpy as jnp
        _rk = jax.random.key(seed)
        x = -0.0002928 + 1 * jax.random.normal(jax.random.fold_in(_rk, 1), (8, 64, 256), jnp.float32)
        _lenS = 64 - jax.random.randint(jax.random.fold_in(_rk, 7), (8,), 0, max(1, 64 // 4) + 1, jnp.int32)
        _lenS2 = 1601 - jax.random.randint(jax.random.fold_in(_rk, 8), (8,), 0, max(1, 1601 // 4) + 1, jnp.int32)
        _ctx_512P = jax.random.normal(jax.random.fold_in(_rk, 11), (8, 16, 128), jnp.float32)
        _ctx_512c = jax.random.dirichlet(jax.random.fold_in(_rk, 511), 0.3 * jnp.ones((16,), jnp.float32), (8, 1601))
        _ctx_512t = jnp.einsum('bsk,bkd->bsd', _ctx_512c, _ctx_512P)
        _ctx_512t = _ctx_512t * jax.lax.rsqrt(jnp.mean(jnp.square(_ctx_512t)) + 1e-12) * 0.953939
        ctx_512 = 0.00222621 + 0.99962 * (_ctx_512t + 0.3 * jax.random.normal(jax.random.fold_in(_rk, 611), (8, 1601, 128), jnp.float32))
        return (x, ctx_512)
    x, ctx_512 = _rec_inputs()

    def _L0_xattn_setup():
        import jax, jax.numpy as jnp
        import numpy as np
        H, D, C1, C2, S, M, B, W = (16, 32, 256, 128, 512, 128, 2, 4)

        def _ln(x, g, b):
            m = jnp.mean(x, -1, keepdims=True)
            v = jnp.var(x, -1, keepdims=True)
            return (x - m) * jax.lax.rsqrt(v + 1e-05) * g + b

        def _mha(x, y, wq, wk, wv, li1_w, li1_b, lnx_g, lnx_b, lny_g, lny_b, ln3_g, ln3_b, li2_w, li2_b, li3_w, li3_b, causal):
            xn = _ln(x, lnx_g, lnx_b)
            yn = _ln(y, lny_g, lny_b)
            q = jnp.einsum('bsc,hcd->bhsd', xn, wq)
            k = jnp.einsum('btc,hcd->bhtd', yn, wk)
            v = jnp.einsum('btc,hcd->bhtd', yn, wv)
            a = jax.nn.softmax(jnp.einsum('bhsd,bhtd->bhst', q, k) * D ** (-0.5), axis=-1)
            if causal:
                s, t = (a.shape[-2], a.shape[-1])
                mask = (jnp.arange(t)[None, :] > jnp.arange(s)[:, None]).astype(a.dtype)
                a = a * mask
            o = jnp.einsum('bhst,bhtd->bhsd', a, v)
            o = o.transpose(0, 2, 1, 3).reshape(x.shape[0], x.shape[1], H * D)
            x_out = x + o @ li1_w + li1_b
            h = jax.nn.gelu(_ln(x_out, ln3_g, ln3_b) @ li2_w + li2_b, approximate=False)
            return x_out + h @ li3_w + li3_b
        key = jax.random.key(seed)
        ks = iter(jax.random.split(key, 64))

        def w(shape, scale=0.02):
            return jax.random.normal(next(ks), shape, jnp.float32) * scale
        inp = {'xx': jax.random.normal(next(ks), (B, S, C1), jnp.float32), 'ee': jax.random.normal(next(ks), (B, M, C2), jnp.float32), 'ln1_g': jnp.ones(C1, jnp.float32), 'ln1_b': jnp.zeros(C1, jnp.float32), 'ln2_g': jnp.ones(C1, jnp.float32), 'ln2_b': jnp.zeros(C1, jnp.float32)}
        for pfx, cy in (('a1', C1), ('a2', C2)):
            inp[pfx + '_wq'] = w((H, C1, D))
            inp[pfx + '_wk'] = w((H, cy, D))
            inp[pfx + '_wv'] = w((H, cy, D))
            inp[pfx + '_li1_w'] = w((H * D, C1))
            inp[pfx + '_li1_b'] = jnp.zeros(C1, jnp.float32)
            inp[pfx + '_lnx_g'] = jnp.ones(C1, jnp.float32)
            inp[pfx + '_lnx_b'] = jnp.zeros(C1, jnp.float32)
            inp[pfx + '_lny_g'] = jnp.ones(cy, jnp.float32)
            inp[pfx + '_lny_b'] = jnp.zeros(cy, jnp.float32)
            inp[pfx + '_ln3_g'] = jnp.ones(C1, jnp.float32)
            inp[pfx + '_ln3_b'] = jnp.zeros(C1, jnp.float32)
            inp[pfx + '_li2_w'] = w((C1, C1 * W))
            inp[pfx + '_li2_b'] = jnp.zeros(C1 * W, jnp.float32)
            inp[pfx + '_li3_w'] = w((C1 * W, C1))
            inp[pfx + '_li3_b'] = jnp.zeros(C1, jnp.float32)
        inp['training'] = 0
        return inp
    _L0_xattn_all = _L0_xattn_setup()
    _L0_xattn_in = {k: v for k, v in _L0_xattn_all.items() if k in ('ln1_g', 'ln1_b', 'ln2_g', 'ln2_b', 'a1_wq', 'a1_wk', 'a1_wv', 'a1_li1_w', 'a1_li1_b', 'a1_lnx_g', 'a1_lnx_b', 'a1_lny_g', 'a1_lny_b', 'a1_ln3_g', 'a1_ln3_b', 'a1_li2_w', 'a1_li2_b', 'a1_li3_w', 'a1_li3_b', 'a2_wq', 'a2_wk', 'a2_wv', 'a2_li1_w', 'a2_li1_b', 'a2_lnx_g', 'a2_lnx_b', 'a2_lny_g', 'a2_lny_b', 'a2_ln3_g', 'a2_ln3_b', 'a2_li2_w', 'a2_li2_b', 'a2_li3_w', 'a2_li3_b')}
    del _L0_xattn_all

    def _L0_attn_setup():
        import jax, jax.numpy as jnp
        import numpy as np
        B, N, D = (2, 2048, 256)
        H, Dh = (16, 64)
        P = H * Dh
        EPS = 1e-06
        DECAY_BIAS_SHIFT = 2.0

        def _elu_plus_one(x):
            return jax.nn.elu(x) + 1.0

        def _ssd_scan(q, k, v, a, eps):
            qT = jnp.moveaxis(q, 2, 0)
            kT = jnp.moveaxis(k, 2, 0)
            vT = jnp.moveaxis(v, 2, 0)
            aT = jnp.moveaxis(a, 2, 0)
            Bb, Hh, _, Dk = q.shape
            Dv = v.shape[-1]
            S0 = jnp.zeros((Bb, Hh, Dk, Dv), q.dtype)
            z0 = jnp.zeros((Bb, Hh, Dk), q.dtype)

            def step(carry, inp):
                S, z = carry
                qt, kt, vt, at = inp
                S = at[..., None, None] * S + kt[..., :, None] * vt[..., None, :]
                z = at[..., None] * z + kt
                num = jnp.einsum('bhk,bhkv->bhv', qt, S)
                den = jnp.einsum('bhk,bhk->bh', qt, z) + eps
                return ((S, z), num / den[..., None])
            _, outT = jax.lax.scan(step, (S0, z0), (qT, kT, vT, aT))
            return jnp.moveaxis(outT, 0, 2)
        key = jax.random.key(seed)
        ks = jax.random.split(key, 7)
        s_in = 1.0 / np.sqrt(D)
        s_out = 1.0 / np.sqrt(P)
        return {'x': jax.random.normal(ks[0], (B, N, D), jnp.float32), 'Wq': jax.random.normal(ks[1], (D, P), jnp.float32) * s_in, 'Wk': jax.random.normal(ks[2], (D, P), jnp.float32) * s_in, 'Wv': jax.random.normal(ks[3], (D, P), jnp.float32) * s_in, 'Wo': jax.random.normal(ks[4], (P, D), jnp.float32) * s_out, 'Wa': jax.random.normal(ks[5], (D, H), jnp.float32) * s_in, 'ba': jnp.zeros((H,), jnp.float32)}
    _L0_attn_all = _L0_attn_setup()
    _L0_attn_in = {k: v for k, v in _L0_attn_all.items() if k in ('Wq', 'Wk', 'Wv', 'Wo', 'Wa', 'ba')}
    del _L0_attn_all

    def _L0_ffn_setup():
        import jax, jax.numpy as jnp
        import numpy as np
        from functools import partial
        HEADS = 16
        EPS = 1e-12

        def _l2_normalize(z):
            n = jnp.linalg.norm(z, axis=-1, keepdims=True)
            return z / jnp.maximum(n, EPS)
        key = jax.random.key(seed)
        kx, kq, kk, kv, ko, kf = jax.random.split(key, 6)
        B, S, D, L = (2, 512, 256, 256)
        scale = 0.02
        return {'x': jax.random.normal(kx, (B, S, D), dtype=jnp.float32), 'Wq': jax.random.normal(kq, (D, L), dtype=jnp.float32) * scale, 'Wk': jax.random.normal(kk, (D, L), dtype=jnp.float32) * scale, 'Wv': jax.random.normal(kv, (D, L), dtype=jnp.float32) * scale, 'Wo': jax.random.normal(ko, (L, D), dtype=jnp.float32) * scale, 'Wff': jax.random.normal(kf, (D, D), dtype=jnp.float32) * scale}
    _L0_ffn_all = _L0_ffn_setup()
    _L0_ffn_in = {k: v for k, v in _L0_ffn_all.items() if k in ('Wq', 'Wk', 'Wv', 'Wo', 'Wff')}
    del _L0_ffn_all

    def _L1_xattn_setup():
        import jax, jax.numpy as jnp
        import numpy as np
        NUM_HEADS = 16
        HEAD_DIM = 64
        Q_DIM = 256
        KV_DIM = 128
        INNER = NUM_HEADS * HEAD_DIM
        key = jax.random.key(seed)
        ks = jax.random.split(key, 7)
        B, N, M = (32, 128, 512)
        q = jax.random.normal(ks[0], (B, N, Q_DIM), dtype=jnp.float32)
        kv = jax.random.normal(ks[1], (B, M, KV_DIM), dtype=jnp.float32)
        Wq = jax.random.normal(ks[2], (Q_DIM, INNER), dtype=jnp.float32) / np.sqrt(Q_DIM)
        Wk = jax.random.normal(ks[3], (KV_DIM, INNER), dtype=jnp.float32) / np.sqrt(KV_DIM)
        Wv = jax.random.normal(ks[4], (KV_DIM, INNER), dtype=jnp.float32) / np.sqrt(KV_DIM)
        Wo = jax.random.normal(ks[5], (INNER, Q_DIM), dtype=jnp.float32) / np.sqrt(INNER)
        bo = jax.random.normal(ks[6], (Q_DIM,), dtype=jnp.float32) * 0.01
        return {'q': q, 'kv': kv, 'Wq': Wq, 'Wk': Wk, 'Wv': Wv, 'Wo': Wo, 'bo': bo}
    _L1_xattn_all = _L1_xattn_setup()
    _L1_xattn_in = {k: v for k, v in _L1_xattn_all.items() if k in ('Wq', 'Wk', 'Wv', 'Wo', 'bo')}
    del _L1_xattn_all

    def _L1_attn_setup():
        import jax, jax.numpy as jnp
        import numpy as np
        H_HEADS = 16
        DECAY_C = 0.7408182206817179

        def _gelu(x):
            return jax.nn.gelu(x, approximate=False)

        def _mlp(x, W1, b1, W2, b2):
            return _gelu(x @ W1 + b1) @ W2 + b2

        def _forward(queries, mu_r, mu_k, mu_v, mu_g, mu_a, mu_d, dA, dB, db, aA, aB, ab, gA, gB, rW1, rb1, rW2, rb2, kW1, kb1, kW2, kb2, vW1, vb1, vW2, vb2, oW1, ob1, oW2, ob2, rem_mult, iclr_mix, bonus_mult, ln_g, ln_b):
            B, T, C = queries.shape
            H = H_HEADS
            N = C // H
            r = _mlp(queries + mu_r, rW1, rb1, rW2, rb2)
            k = _mlp(queries + mu_k, kW1, kb1, kW2, kb2)
            v = _mlp(queries + mu_v, vW1, vb1, vW2, vb2)
            gate = jax.nn.sigmoid((queries + mu_g) @ gA @ gB)
            iclr = jax.nn.sigmoid((queries + mu_a) @ aA @ ab + (queries + mu_a) @ aA @ aB) if False else jax.nn.sigmoid((queries + mu_a) @ aA @ aB + ab)
            decay = jnp.exp(-DECAY_C * jax.nn.sigmoid(jnp.tanh((queries + mu_d) @ dA @ dB + db)))
            removal_k = k * rem_mult
            replacement_k = k * (1.0 + (iclr - 1.0) * iclr_mix)
            rh = r.reshape(B, T, H, N)
            rkh = replacement_k.reshape(B, T, H, N)
            vh = v.reshape(B, T, H, N)
            dh = decay.reshape(B, T, H, N)
            ah = iclr.reshape(B, T, H, N)
            rmh = removal_k.reshape(B, T, H, N)
            kn = rmh / jnp.maximum(jnp.linalg.norm(rmh, axis=-1, keepdims=True), 1e-12)
            xs = tuple((jnp.swapaxes(a, 0, 1) for a in (dh, ah, kn, rkh, vh, rh)))

            def step(wkv, x):
                d, a, knt, rk, vt, rt = x
                tmp = jnp.einsum('bhj,bhjk->bhk', a * knt, wkv)
                wkv = d[..., None] * wkv - knt[..., None] * tmp[:, :, None, :] + vt[..., None] * rk[:, :, None, :]
                return (wkv, jnp.einsum('bhij,bhj->bhi', wkv, rt))
            wkv0 = jnp.zeros((B, H, N, N), queries.dtype)
            _, out_t = jax.lax.scan(step, wkv0, xs)
            out = jnp.swapaxes(out_t, 0, 1)
            bonus = jnp.sum(rh * rkh, -1, keepdims=True) * 0.2 * vh * bonus_mult.reshape(1, 1, H, N)
            out = (out + bonus).reshape(B, T, C)
            mu = jnp.mean(out, -1, keepdims=True)
            var = jnp.mean((out - mu) ** 2, -1, keepdims=True)
            out = (out - mu) / jnp.sqrt(var + 1e-06) * ln_g + ln_b
            out = out * gate
            out = _mlp(out, oW1, ob1, oW2, ob2)
            return out
        B, T, C = (4, 512, 256)
        L = max(64, C // 8)
        E = int(C * 1.2)
        key = jax.random.key(seed)
        ctr = [0]

        def rn(shape, s=0.02):
            ctr[0] += 1
            return jax.random.normal(jax.random.fold_in(key, ctr[0]), shape, jnp.float32) * s
        z = lambda *s: jnp.zeros(s, jnp.float32)
        inp = {'queries': rn((B, T, C), 1.0), 'keys': rn((B, T, C), 1.0), 'values': rn((B, T, C), 1.0), 'attn_mask': jnp.ones((B, T), dtype=bool), 'mu_r': rn((C,)), 'mu_k': rn((C,)), 'mu_v': rn((C,)), 'mu_g': rn((C,)), 'mu_a': rn((C,)), 'mu_d': rn((C,)), 'dA': rn((C, L)), 'dB': rn((L, C)), 'db': z(C), 'aA': rn((C, L)), 'aB': rn((L, C)), 'ab': z(C), 'gA': rn((C, L)), 'gB': rn((L, C)), 'rW1': rn((C, E)), 'rb1': z(E), 'rW2': rn((E, C)), 'rb2': z(C), 'kW1': rn((C, E)), 'kb1': z(E), 'kW2': rn((E, C)), 'kb2': z(C), 'vW1': rn((C, E)), 'vb1': z(E), 'vW2': rn((E, C)), 'vb2': z(C), 'oW1': rn((C, E)), 'ob1': z(E), 'oW2': rn((E, C)), 'ob2': z(C), 'rem_mult': rn((C,), 0.05), 'iclr_mix': jnp.full((C,), 0.7, jnp.float32), 'bonus_mult': jnp.full((C,), 1.2, jnp.float32), 'ln_g': jnp.ones((C,), jnp.float32), 'ln_b': z(C)}
        return inp
    _L1_attn_all = _L1_attn_setup()
    _L1_attn_in = {k: v for k, v in _L1_attn_all.items() if k in ('keys', 'values', 'attn_mask', 'mu_r', 'mu_k', 'mu_v', 'mu_g', 'mu_a', 'mu_d', 'dA', 'dB', 'db', 'aA', 'aB', 'ab', 'gA', 'gB', 'rW1', 'rb1', 'rW2', 'rb2', 'kW1', 'kb1', 'kW2', 'kb2', 'vW1', 'vb1', 'vW2', 'vb2', 'oW1', 'ob1', 'oW2', 'ob2', 'rem_mult', 'iclr_mix', 'bonus_mult', 'ln_g', 'ln_b')}
    del _L1_attn_all

    def _L1_ffn_setup():
        import jax, jax.numpy as jnp
        import numpy as np
        B, P, D, D_MLP, E, K = (2, 512, 256, 1024, 8, 2)
        key = jax.random.key(seed)
        k_x, k_g, k_in, k_out = jax.random.split(key, 4)
        s_in = 1.0 / np.sqrt(D).astype(np.float32)
        s_out = 1.0 / np.sqrt(D_MLP).astype(np.float32)
        return {'x': jax.random.normal(k_x, (B, P, D), dtype=jnp.float32), 'W_gate': jax.random.normal(k_g, (D, E), dtype=jnp.float32) * s_in, 'W_in': jax.random.normal(k_in, (E, D, D_MLP), dtype=jnp.float32) * s_in, 'b_in': jnp.zeros((E, D_MLP), dtype=jnp.float32), 'W_out': jax.random.normal(k_out, (E, D_MLP, D), dtype=jnp.float32) * s_out, 'b_out': jnp.zeros((E, D), dtype=jnp.float32)}
    _L1_ffn_all = _L1_ffn_setup()
    _L1_ffn_in = {k: v for k, v in _L1_ffn_all.items() if k in ('W_gate', 'W_in', 'b_in', 'W_out', 'b_out')}
    del _L1_ffn_all
    return {'x': x, 'ctx_512': ctx_512, 'L0_xattn_ln1_g': _L0_xattn_in['ln1_g'], 'L0_xattn_ln1_b': _L0_xattn_in['ln1_b'], 'L0_xattn_ln2_g': _L0_xattn_in['ln2_g'], 'L0_xattn_ln2_b': _L0_xattn_in['ln2_b'], 'L0_xattn_a1_wq': _L0_xattn_in['a1_wq'], 'L0_xattn_a1_wk': _L0_xattn_in['a1_wk'], 'L0_xattn_a1_wv': _L0_xattn_in['a1_wv'], 'L0_xattn_a1_li1_w': _L0_xattn_in['a1_li1_w'], 'L0_xattn_a1_li1_b': _L0_xattn_in['a1_li1_b'], 'L0_xattn_a1_lnx_g': _L0_xattn_in['a1_lnx_g'], 'L0_xattn_a1_lnx_b': _L0_xattn_in['a1_lnx_b'], 'L0_xattn_a1_lny_g': _L0_xattn_in['a1_lny_g'], 'L0_xattn_a1_lny_b': _L0_xattn_in['a1_lny_b'], 'L0_xattn_a1_ln3_g': _L0_xattn_in['a1_ln3_g'], 'L0_xattn_a1_ln3_b': _L0_xattn_in['a1_ln3_b'], 'L0_xattn_a1_li2_w': _L0_xattn_in['a1_li2_w'], 'L0_xattn_a1_li2_b': _L0_xattn_in['a1_li2_b'], 'L0_xattn_a1_li3_w': _L0_xattn_in['a1_li3_w'], 'L0_xattn_a1_li3_b': _L0_xattn_in['a1_li3_b'], 'L0_xattn_a2_wq': _L0_xattn_in['a2_wq'], 'L0_xattn_a2_wk': _L0_xattn_in['a2_wk'], 'L0_xattn_a2_wv': _L0_xattn_in['a2_wv'], 'L0_xattn_a2_li1_w': _L0_xattn_in['a2_li1_w'], 'L0_xattn_a2_li1_b': _L0_xattn_in['a2_li1_b'], 'L0_xattn_a2_lnx_g': _L0_xattn_in['a2_lnx_g'], 'L0_xattn_a2_lnx_b': _L0_xattn_in['a2_lnx_b'], 'L0_xattn_a2_lny_g': _L0_xattn_in['a2_lny_g'], 'L0_xattn_a2_lny_b': _L0_xattn_in['a2_lny_b'], 'L0_xattn_a2_ln3_g': _L0_xattn_in['a2_ln3_g'], 'L0_xattn_a2_ln3_b': _L0_xattn_in['a2_ln3_b'], 'L0_xattn_a2_li2_w': _L0_xattn_in['a2_li2_w'], 'L0_xattn_a2_li2_b': _L0_xattn_in['a2_li2_b'], 'L0_xattn_a2_li3_w': _L0_xattn_in['a2_li3_w'], 'L0_xattn_a2_li3_b': _L0_xattn_in['a2_li3_b'], 'L0_attn_Wq': _L0_attn_in['Wq'], 'L0_attn_Wk': _L0_attn_in['Wk'], 'L0_attn_Wv': _L0_attn_in['Wv'], 'L0_attn_Wo': _L0_attn_in['Wo'], 'L0_attn_Wa': _L0_attn_in['Wa'], 'L0_attn_ba': _L0_attn_in['ba'], 'L0_ffn_Wq': _L0_ffn_in['Wq'], 'L0_ffn_Wk': _L0_ffn_in['Wk'], 'L0_ffn_Wv': _L0_ffn_in['Wv'], 'L0_ffn_Wo': _L0_ffn_in['Wo'], 'L0_ffn_Wff': _L0_ffn_in['Wff'], 'L1_xattn_Wq': _L1_xattn_in['Wq'], 'L1_xattn_Wk': _L1_xattn_in['Wk'], 'L1_xattn_Wv': _L1_xattn_in['Wv'], 'L1_xattn_Wo': _L1_xattn_in['Wo'], 'L1_xattn_bo': _L1_xattn_in['bo'], 'L1_attn_keys': _L1_attn_in['keys'], 'L1_attn_values': _L1_attn_in['values'], 'L1_attn_attn_mask': _L1_attn_in['attn_mask'], 'L1_attn_mu_r': _L1_attn_in['mu_r'], 'L1_attn_mu_k': _L1_attn_in['mu_k'], 'L1_attn_mu_v': _L1_attn_in['mu_v'], 'L1_attn_mu_g': _L1_attn_in['mu_g'], 'L1_attn_mu_a': _L1_attn_in['mu_a'], 'L1_attn_mu_d': _L1_attn_in['mu_d'], 'L1_attn_dA': _L1_attn_in['dA'], 'L1_attn_dB': _L1_attn_in['dB'], 'L1_attn_db': _L1_attn_in['db'], 'L1_attn_aA': _L1_attn_in['aA'], 'L1_attn_aB': _L1_attn_in['aB'], 'L1_attn_ab': _L1_attn_in['ab'], 'L1_attn_gA': _L1_attn_in['gA'], 'L1_attn_gB': _L1_attn_in['gB'], 'L1_attn_rW1': _L1_attn_in['rW1'], 'L1_attn_rb1': _L1_attn_in['rb1'], 'L1_attn_rW2': _L1_attn_in['rW2'], 'L1_attn_rb2': _L1_attn_in['rb2'], 'L1_attn_kW1': _L1_attn_in['kW1'], 'L1_attn_kb1': _L1_attn_in['kb1'], 'L1_attn_kW2': _L1_attn_in['kW2'], 'L1_attn_kb2': _L1_attn_in['kb2'], 'L1_attn_vW1': _L1_attn_in['vW1'], 'L1_attn_vb1': _L1_attn_in['vb1'], 'L1_attn_vW2': _L1_attn_in['vW2'], 'L1_attn_vb2': _L1_attn_in['vb2'], 'L1_attn_oW1': _L1_attn_in['oW1'], 'L1_attn_ob1': _L1_attn_in['ob1'], 'L1_attn_oW2': _L1_attn_in['oW2'], 'L1_attn_ob2': _L1_attn_in['ob2'], 'L1_attn_rem_mult': _L1_attn_in['rem_mult'], 'L1_attn_iclr_mix': _L1_attn_in['iclr_mix'], 'L1_attn_bonus_mult': _L1_attn_in['bonus_mult'], 'L1_attn_ln_g': _L1_attn_in['ln_g'], 'L1_attn_ln_b': _L1_attn_in['ln_b'], 'L1_ffn_W_gate': _L1_ffn_in['W_gate'], 'L1_ffn_W_in': _L1_ffn_in['W_in'], 'L1_ffn_b_in': _L1_ffn_in['b_in'], 'L1_ffn_W_out': _L1_ffn_in['W_out'], 'L1_ffn_b_out': _L1_ffn_in['b_out']}

def reference(x, ctx_512, L0_xattn_ln1_g, L0_xattn_ln1_b, L0_xattn_ln2_g, L0_xattn_ln2_b, L0_xattn_a1_wq, L0_xattn_a1_wk, L0_xattn_a1_wv, L0_xattn_a1_li1_w, L0_xattn_a1_li1_b, L0_xattn_a1_lnx_g, L0_xattn_a1_lnx_b, L0_xattn_a1_lny_g, L0_xattn_a1_lny_b, L0_xattn_a1_ln3_g, L0_xattn_a1_ln3_b, L0_xattn_a1_li2_w, L0_xattn_a1_li2_b, L0_xattn_a1_li3_w, L0_xattn_a1_li3_b, L0_xattn_a2_wq, L0_xattn_a2_wk, L0_xattn_a2_wv, L0_xattn_a2_li1_w, L0_xattn_a2_li1_b, L0_xattn_a2_lnx_g, L0_xattn_a2_lnx_b, L0_xattn_a2_lny_g, L0_xattn_a2_lny_b, L0_xattn_a2_ln3_g, L0_xattn_a2_ln3_b, L0_xattn_a2_li2_w, L0_xattn_a2_li2_b, L0_xattn_a2_li3_w, L0_xattn_a2_li3_b, L0_attn_Wq, L0_attn_Wk, L0_attn_Wv, L0_attn_Wo, L0_attn_Wa, L0_attn_ba, L0_ffn_Wq, L0_ffn_Wk, L0_ffn_Wv, L0_ffn_Wo, L0_ffn_Wff, L1_xattn_Wq, L1_xattn_Wk, L1_xattn_Wv, L1_xattn_Wo, L1_xattn_bo, L1_attn_keys, L1_attn_values, L1_attn_attn_mask, L1_attn_mu_r, L1_attn_mu_k, L1_attn_mu_v, L1_attn_mu_g, L1_attn_mu_a, L1_attn_mu_d, L1_attn_dA, L1_attn_dB, L1_attn_db, L1_attn_aA, L1_attn_aB, L1_attn_ab, L1_attn_gA, L1_attn_gB, L1_attn_rW1, L1_attn_rb1, L1_attn_rW2, L1_attn_rb2, L1_attn_kW1, L1_attn_kb1, L1_attn_kW2, L1_attn_kb2, L1_attn_vW1, L1_attn_vb1, L1_attn_vW2, L1_attn_vb2, L1_attn_oW1, L1_attn_ob1, L1_attn_oW2, L1_attn_ob2, L1_attn_rem_mult, L1_attn_iclr_mix, L1_attn_bonus_mult, L1_attn_ln_g, L1_attn_ln_b, L1_ffn_W_gate, L1_ffn_W_in, L1_ffn_b_in, L1_ffn_W_out, L1_ffn_b_out):
    import jax
    import jax.numpy as jnp

    def _L0_xattn_ref(xx, ee, ln1_g, ln1_b, ln2_g, ln2_b, a1_wq, a1_wk, a1_wv, a1_li1_w, a1_li1_b, a1_lnx_g, a1_lnx_b, a1_lny_g, a1_lny_b, a1_ln3_g, a1_ln3_b, a1_li2_w, a1_li2_b, a1_li3_w, a1_li3_b, a2_wq, a2_wk, a2_wv, a2_li1_w, a2_li1_b, a2_lnx_g, a2_lnx_b, a2_lny_g, a2_lny_b, a2_ln3_g, a2_ln3_b, a2_li2_w, a2_li2_b, a2_li3_w, a2_li3_b, training):
        import jax, jax.numpy as jnp
        import numpy as np
        H, D, C1, C2, S, M, B, W = (16, 32, 256, 128, 512, 128, 2, 4)

        def _ln(x, g, b):
            m = jnp.mean(x, -1, keepdims=True)
            v = jnp.var(x, -1, keepdims=True)
            return (x - m) * jax.lax.rsqrt(v + 1e-05) * g + b

        def _mha(x, y, wq, wk, wv, li1_w, li1_b, lnx_g, lnx_b, lny_g, lny_b, ln3_g, ln3_b, li2_w, li2_b, li3_w, li3_b, causal):
            xn = _ln(x, lnx_g, lnx_b)
            yn = _ln(y, lny_g, lny_b)
            q = jnp.einsum('bsc,hcd->bhsd', xn, wq)
            k = jnp.einsum('btc,hcd->bhtd', yn, wk)
            v = jnp.einsum('btc,hcd->bhtd', yn, wv)
            a = jax.nn.softmax(jnp.einsum('bhsd,bhtd->bhst', q, k) * D ** (-0.5), axis=-1)
            if causal:
                s, t = (a.shape[-2], a.shape[-1])
                mask = (jnp.arange(t)[None, :] > jnp.arange(s)[:, None]).astype(a.dtype)
                a = a * mask
            o = jnp.einsum('bhst,bhtd->bhsd', a, v)
            o = o.transpose(0, 2, 1, 3).reshape(x.shape[0], x.shape[1], H * D)
            x_out = x + o @ li1_w + li1_b
            h = jax.nn.gelu(_ln(x_out, ln3_g, ln3_b) @ li2_w + li2_b, approximate=False)
            return x_out + h @ li3_w + li3_b
        x = _ln(xx, ln1_g, ln1_b)
        x = x + _mha(x, x, a1_wq, a1_wk, a1_wv, a1_li1_w, a1_li1_b, a1_lnx_g, a1_lnx_b, a1_lny_g, a1_lny_b, a1_ln3_g, a1_ln3_b, a1_li2_w, a1_li2_b, a1_li3_w, a1_li3_b, causal=True)
        x = _ln(x, ln2_g, ln2_b)
        return x + _mha(x, ee, a2_wq, a2_wk, a2_wv, a2_li1_w, a2_li1_b, a2_lnx_g, a2_lnx_b, a2_lny_g, a2_lny_b, a2_ln3_g, a2_ln3_b, a2_li2_w, a2_li2_b, a2_li3_w, a2_li3_b, causal=False)

    def _L0_attn_ref(x, Wq, Wk, Wv, Wo, Wa, ba):
        import jax, jax.numpy as jnp
        import numpy as np
        B, N, D = (2, 2048, 256)
        H, Dh = (16, 64)
        P = H * Dh
        EPS = 1e-06
        DECAY_BIAS_SHIFT = 2.0

        def _elu_plus_one(x):
            return jax.nn.elu(x) + 1.0

        def _ssd_scan(q, k, v, a, eps):
            qT = jnp.moveaxis(q, 2, 0)
            kT = jnp.moveaxis(k, 2, 0)
            vT = jnp.moveaxis(v, 2, 0)
            aT = jnp.moveaxis(a, 2, 0)
            Bb, Hh, _, Dk = q.shape
            Dv = v.shape[-1]
            S0 = jnp.zeros((Bb, Hh, Dk, Dv), q.dtype)
            z0 = jnp.zeros((Bb, Hh, Dk), q.dtype)

            def step(carry, inp):
                S, z = carry
                qt, kt, vt, at = inp
                S = at[..., None, None] * S + kt[..., :, None] * vt[..., None, :]
                z = at[..., None] * z + kt
                num = jnp.einsum('bhk,bhkv->bhv', qt, S)
                den = jnp.einsum('bhk,bhk->bh', qt, z) + eps
                return ((S, z), num / den[..., None])
            _, outT = jax.lax.scan(step, (S0, z0), (qT, kT, vT, aT))
            return jnp.moveaxis(outT, 0, 2)
        b, n, _ = x.shape
        q = (x @ Wq).reshape(b, n, H, Dh).transpose(0, 2, 1, 3)
        k = (x @ Wk).reshape(b, n, H, Dh).transpose(0, 2, 1, 3)
        v = (x @ Wv).reshape(b, n, H, Dh).transpose(0, 2, 1, 3)
        q = _elu_plus_one(q)
        k = _elu_plus_one(k)
        a = jax.nn.sigmoid(x @ Wa + ba + DECAY_BIAS_SHIFT)
        a = a.transpose(0, 2, 1)
        out = _ssd_scan(q, k, v, a, EPS)
        out = out.transpose(0, 2, 1, 3).reshape(b, n, P)
        return out @ Wo

    def _L0_ffn_ref(x, Wq, Wk, Wv, Wo, Wff):
        import jax, jax.numpy as jnp
        import numpy as np
        from functools import partial
        HEADS = 16
        EPS = 1e-12

        def _l2_normalize(z):
            n = jnp.linalg.norm(z, axis=-1, keepdims=True)
            return z / jnp.maximum(n, EPS)
        B, S, D = x.shape
        H = HEADS
        L = Wq.shape[1]
        dh = L // H

        def split_heads(t):
            return t.reshape(B, S, H, dh).transpose(0, 2, 1, 3).reshape(B * H, S, dh)
        q = split_heads(x @ Wq)
        k = split_heads(x @ Wk)
        v = split_heads(x @ Wv)
        scores = jnp.einsum('bqd,bkd->bkq', q, k) / jnp.sqrt(jnp.asarray(D, x.dtype))
        attn = jax.nn.softmax(scores, axis=-1)
        out = jnp.einsum('bkq,bkv->bqv', attn, v)
        z = out.reshape(B, H, S, dh).transpose(0, 2, 1, 3).reshape(B, S, L)
        z = z @ Wo
        z = _l2_normalize(z)
        z = z @ Wff
        z = _l2_normalize(z)
        z = jax.nn.gelu(z, approximate=False)
        return z

    def _L1_xattn_ref(q, kv, Wq, Wk, Wv, Wo, bo):
        import jax, jax.numpy as jnp
        import numpy as np
        NUM_HEADS = 16
        HEAD_DIM = 64
        Q_DIM = 256
        KV_DIM = 128
        INNER = NUM_HEADS * HEAD_DIM
        B, N, _ = q.shape
        M = kv.shape[1]
        scale = HEAD_DIM ** (-0.5)
        qh = (q @ Wq).reshape(B, N, NUM_HEADS, HEAD_DIM).transpose(0, 2, 1, 3)
        kh = (kv @ Wk).reshape(B, M, NUM_HEADS, HEAD_DIM).transpose(0, 2, 1, 3)
        vh = (kv @ Wv).reshape(B, M, NUM_HEADS, HEAD_DIM).transpose(0, 2, 1, 3)
        scores = jnp.einsum('bhnd,bhmd->bhnm', qh, kh) * scale
        attn = jax.nn.softmax(scores, axis=-1)
        out = jnp.einsum('bhnm,bhmd->bhnd', attn, vh)
        out = out.transpose(0, 2, 1, 3).reshape(B, N, INNER)
        return out @ Wo + bo

    def _L1_attn_ref(queries, keys, values, attn_mask, mu_r, mu_k, mu_v, mu_g, mu_a, mu_d, dA, dB, db, aA, aB, ab, gA, gB, rW1, rb1, rW2, rb2, kW1, kb1, kW2, kb2, vW1, vb1, vW2, vb2, oW1, ob1, oW2, ob2, rem_mult, iclr_mix, bonus_mult, ln_g, ln_b):
        import jax, jax.numpy as jnp
        import numpy as np
        H_HEADS = 16
        DECAY_C = 0.7408182206817179

        def _gelu(x):
            return jax.nn.gelu(x, approximate=False)

        def _mlp(x, W1, b1, W2, b2):
            return _gelu(x @ W1 + b1) @ W2 + b2

        def _forward(queries, mu_r, mu_k, mu_v, mu_g, mu_a, mu_d, dA, dB, db, aA, aB, ab, gA, gB, rW1, rb1, rW2, rb2, kW1, kb1, kW2, kb2, vW1, vb1, vW2, vb2, oW1, ob1, oW2, ob2, rem_mult, iclr_mix, bonus_mult, ln_g, ln_b):
            B, T, C = queries.shape
            H = H_HEADS
            N = C // H
            r = _mlp(queries + mu_r, rW1, rb1, rW2, rb2)
            k = _mlp(queries + mu_k, kW1, kb1, kW2, kb2)
            v = _mlp(queries + mu_v, vW1, vb1, vW2, vb2)
            gate = jax.nn.sigmoid((queries + mu_g) @ gA @ gB)
            iclr = jax.nn.sigmoid((queries + mu_a) @ aA @ ab + (queries + mu_a) @ aA @ aB) if False else jax.nn.sigmoid((queries + mu_a) @ aA @ aB + ab)
            decay = jnp.exp(-DECAY_C * jax.nn.sigmoid(jnp.tanh((queries + mu_d) @ dA @ dB + db)))
            removal_k = k * rem_mult
            replacement_k = k * (1.0 + (iclr - 1.0) * iclr_mix)
            rh = r.reshape(B, T, H, N)
            rkh = replacement_k.reshape(B, T, H, N)
            vh = v.reshape(B, T, H, N)
            dh = decay.reshape(B, T, H, N)
            ah = iclr.reshape(B, T, H, N)
            rmh = removal_k.reshape(B, T, H, N)
            kn = rmh / jnp.maximum(jnp.linalg.norm(rmh, axis=-1, keepdims=True), 1e-12)
            xs = tuple((jnp.swapaxes(a, 0, 1) for a in (dh, ah, kn, rkh, vh, rh)))

            def step(wkv, x):
                d, a, knt, rk, vt, rt = x
                tmp = jnp.einsum('bhj,bhjk->bhk', a * knt, wkv)
                wkv = d[..., None] * wkv - knt[..., None] * tmp[:, :, None, :] + vt[..., None] * rk[:, :, None, :]
                return (wkv, jnp.einsum('bhij,bhj->bhi', wkv, rt))
            wkv0 = jnp.zeros((B, H, N, N), queries.dtype)
            _, out_t = jax.lax.scan(step, wkv0, xs)
            out = jnp.swapaxes(out_t, 0, 1)
            bonus = jnp.sum(rh * rkh, -1, keepdims=True) * 0.2 * vh * bonus_mult.reshape(1, 1, H, N)
            out = (out + bonus).reshape(B, T, C)
            mu = jnp.mean(out, -1, keepdims=True)
            var = jnp.mean((out - mu) ** 2, -1, keepdims=True)
            out = (out - mu) / jnp.sqrt(var + 1e-06) * ln_g + ln_b
            out = out * gate
            out = _mlp(out, oW1, ob1, oW2, ob2)
            return out
        del keys, values, attn_mask
        return _forward(queries, mu_r, mu_k, mu_v, mu_g, mu_a, mu_d, dA, dB, db, aA, aB, ab, gA, gB, rW1, rb1, rW2, rb2, kW1, kb1, kW2, kb2, vW1, vb1, vW2, vb2, oW1, ob1, oW2, ob2, rem_mult, iclr_mix, bonus_mult, ln_g, ln_b)

    def _L1_ffn_ref(x, W_gate, W_in, b_in, W_out, b_out):
        import jax, jax.numpy as jnp
        import numpy as np
        B, P, D, D_MLP, E, K = (2, 512, 256, 1024, 8, 2)
        gate_logits = jnp.einsum('bpd,de->bpe', x, W_gate)
        top_w, top_idx = jax.lax.top_k(gate_logits, K)
        top_w = jax.nn.softmax(top_w, axis=-1)
        combine = jnp.einsum('bpke,bpk->bpe', jax.nn.one_hot(top_idx, E, dtype=x.dtype), top_w)
        out = jnp.zeros_like(x)
        for e in range(E):
            h = jax.nn.gelu(jnp.einsum('bpd,dm->bpm', x, W_in[e]) + b_in[e], approximate=False)
            y = jnp.einsum('bpm,md->bpd', h, W_out[e]) + b_out[e]
            out = out + combine[..., e, None] * y
        return out
    x = x + _L0_xattn_ref(_layernorm(x, axis=-1), ctx_512, L0_xattn_ln1_g, L0_xattn_ln1_b, L0_xattn_ln2_g, L0_xattn_ln2_b, L0_xattn_a1_wq, L0_xattn_a1_wk, L0_xattn_a1_wv, L0_xattn_a1_li1_w, L0_xattn_a1_li1_b, L0_xattn_a1_lnx_g, L0_xattn_a1_lnx_b, L0_xattn_a1_lny_g, L0_xattn_a1_lny_b, L0_xattn_a1_ln3_g, L0_xattn_a1_ln3_b, L0_xattn_a1_li2_w, L0_xattn_a1_li2_b, L0_xattn_a1_li3_w, L0_xattn_a1_li3_b, L0_xattn_a2_wq, L0_xattn_a2_wk, L0_xattn_a2_wv, L0_xattn_a2_li1_w, L0_xattn_a2_li1_b, L0_xattn_a2_lnx_g, L0_xattn_a2_lnx_b, L0_xattn_a2_lny_g, L0_xattn_a2_lny_b, L0_xattn_a2_ln3_g, L0_xattn_a2_ln3_b, L0_xattn_a2_li2_w, L0_xattn_a2_li2_b, L0_xattn_a2_li3_w, L0_xattn_a2_li3_b, 0)
    x = x + _L0_attn_ref(_layernorm(x, axis=-1), L0_attn_Wq, L0_attn_Wk, L0_attn_Wv, L0_attn_Wo, L0_attn_Wa, L0_attn_ba)
    x = x + _L0_ffn_ref(_layernorm(x, axis=-1), L0_ffn_Wq, L0_ffn_Wk, L0_ffn_Wv, L0_ffn_Wo, L0_ffn_Wff)
    x = x + _L1_xattn_ref(_layernorm(x, axis=-1), ctx_512, L1_xattn_Wq, L1_xattn_Wk, L1_xattn_Wv, L1_xattn_Wo, L1_xattn_bo)
    x = x + _L1_attn_ref(_layernorm(x, axis=-1), L1_attn_keys, L1_attn_values, L1_attn_attn_mask, L1_attn_mu_r, L1_attn_mu_k, L1_attn_mu_v, L1_attn_mu_g, L1_attn_mu_a, L1_attn_mu_d, L1_attn_dA, L1_attn_dB, L1_attn_db, L1_attn_aA, L1_attn_aB, L1_attn_ab, L1_attn_gA, L1_attn_gB, L1_attn_rW1, L1_attn_rb1, L1_attn_rW2, L1_attn_rb2, L1_attn_kW1, L1_attn_kb1, L1_attn_kW2, L1_attn_kb2, L1_attn_vW1, L1_attn_vb1, L1_attn_vW2, L1_attn_vb2, L1_attn_oW1, L1_attn_ob1, L1_attn_oW2, L1_attn_ob2, L1_attn_rem_mult, L1_attn_iclr_mix, L1_attn_bonus_mult, L1_attn_ln_g, L1_attn_ln_b)
    x = x + _L1_ffn_ref(_layernorm(x, axis=-1), L1_ffn_W_gate, L1_ffn_W_in, L1_ffn_b_in, L1_ffn_W_out, L1_ffn_b_out)
    return x

_drawn_inputs = setup_inputs


def setup_inputs(seed=0):
    import zlib

    import numpy as np

    out = dict(_drawn_inputs(seed))
    spreads = {'L0_xattn_ln1_g': (1.0, 0.2),
     'L0_xattn_ln1_b': (0.0, 0.1),
     'L0_xattn_ln2_g': (1.0, 0.2),
     'L0_xattn_ln2_b': (0.0, 0.1),
     'L0_xattn_a1_li1_b': (0.0, 0.1),
     'L0_xattn_a1_lnx_g': (1.0, 0.6),
     'L0_xattn_a1_lnx_b': (0.0, 0.8),
     'L0_xattn_a1_lny_g': (1.0, 0.6),
     'L0_xattn_a1_lny_b': (0.0, 0.8),
     'L0_xattn_a1_ln3_g': (1.0, 0.6),
     'L0_xattn_a1_ln3_b': (0.0, 2.0),
     'L0_xattn_a1_li2_b': (0.0, 0.423),
     'L0_xattn_a1_li3_b': (0.0, 0.1),
     'L0_xattn_a2_li1_b': (0.0, 0.1),
     'L0_xattn_a2_lnx_g': (1.0, 0.6),
     'L0_xattn_a2_lnx_b': (0.0, 0.8),
     'L0_xattn_a2_lny_g': (1.0, 0.6),
     'L0_xattn_a2_lny_b': (0.0, 0.8),
     'L0_xattn_a2_ln3_g': (1.0, 0.6),
     'L0_xattn_a2_ln3_b': (0.0, 0.8),
     'L0_xattn_a2_li2_b': (0.0, 0.536),
     'L0_xattn_a2_li3_b': (0.0, 0.1),
     'L0_attn_ba': (0.0, 0.755),
     'L1_attn_db': (0.0, 0.8),
     'L1_attn_ab': (0.0, 0.8),
     'L1_attn_rb1': (0.0, 0.8),
     'L1_attn_rb2': (0.0, 0.52),
     'L1_attn_kb1': (0.0, 0.8),
     'L1_attn_kb2': (0.0, 0.458),
     'L1_attn_vb1': (0.0, 0.8),
     'L1_attn_vb2': (0.0, 0.44),
     'L1_attn_ob1': (0.0, 0.56),
     'L1_attn_ob2': (0.0, 0.1),
     'L1_attn_iclr_mix': (0.699999988079071, 0.6),
     'L1_attn_bonus_mult': (1.2000000476837158, 0.6),
     'L1_attn_ln_g': (1.0, 0.6),
     'L1_attn_ln_b': (0.0, 0.8),
     'L1_ffn_b_in': (0.0, 0.505),
     'L1_ffn_b_out': (0.0, 0.343)}
    factors = {'L0_xattn_a1_wq': 8.0,
     'L0_xattn_a1_wk': 8.0,
     'L0_xattn_a1_wv': 7.268,
     'L0_xattn_a1_li1_w': 6.461,
     'L0_xattn_a2_wq': 8.0,
     'L0_xattn_a2_wk': 8.0,
     'L0_attn_Wq': 6.218,
     'L0_attn_Wk': 3.89,
     'L0_ffn_Wq': 28.647,
     'L0_ffn_Wk': 26.934,
     'L0_ffn_Wv': 9.24,
     'L0_ffn_Wo': 10.83,
     'L0_ffn_Wff': 11.92,
     'L1_xattn_bo': 7.643,
     'L1_attn_mu_r': 8.0,
     'L1_attn_mu_k': 8.0,
     'L1_attn_mu_v': 8.0,
     'L1_attn_mu_g': 8.0,
     'L1_attn_mu_a': 8.0,
     'L1_attn_mu_d': 8.0,
     'L1_attn_dA': 8.0,
     'L1_attn_dB': 8.0,
     'L1_attn_aA': 8.0,
     'L1_attn_aB': 8.0,
     'L1_attn_gA': 8.0,
     'L1_attn_gB': 8.0,
     'L1_attn_rW1': 7.041,
     'L1_attn_rW2': 5.438,
     'L1_attn_kW1': 7.206,
     'L1_attn_kW2': 6.757,
     'L1_attn_vW1': 7.157,
     'L1_attn_vW2': 8.0,
     'L1_attn_oW1': 3.503,
     'L1_attn_oW2': 3.243,
     'L1_attn_rem_mult': 8.0}
    for name, (base, spread) in spreads.items():
        noise = np.random.default_rng([zlib.crc32(name.encode()), seed]).standard_normal(out[name].shape)
        drawn = base * np.exp(spread * noise) if base else spread * noise
        out[name] = jnp.asarray(drawn.astype(out[name].dtype))
    for name, factor in factors.items():
        out[name] = (out[name] * factor).astype(out[name].dtype)
    return out
```

```python
from contextlib import ExitStack, contextmanager

import concourse.bass as bass
from concourse import mybir

F32 = mybir.dt.float32
U32 = mybir.dt.uint32
ALU = mybir.AluOpType
ACT = mybir.ActivationFunctionType
AX = mybir.AxisListType.X
ds = bass.ds

P = 128
NB, T, C = 8, 64, 256
TOK = NB * T
KC = C // P
PAIRS = NB // 2
H = 16
S_CTX, CC = 1601, 128
NT = -(-S_CTX // P)
TAIL = S_CTX - (NT - 1) * P
HID = 1024
MC = HID // P
E1 = 307
EC = [(0, 128), (128, 128), (256, E1 - 256)]
LORA = 64
NE = 8
BANK = 512
DECAY_C = 0.7408182206817179
EPS = 1e-5

ROWS = [("L0_xattn_" + n, 1) for n in (
    "ln1_g", "ln1_b", "ln2_g", "ln2_b", "a1_li1_b", "a1_lnx_g", "a1_lnx_b", "a1_lny_g", "a1_lny_b", "a1_ln3_g",
    "a1_ln3_b", "a1_li3_b", "a2_li1_b", "a2_lnx_g", "a2_lnx_b", "a2_ln3_g", "a2_ln3_b", "a2_li3_b")]
ROWS += [("L0_xattn_a1_li2_b", 4), ("L0_xattn_a2_li2_b", 4), ("L1_xattn_bo", 1)]
ROWS += [("L1_attn_" + n, 1) for n in ("mu_r", "mu_k", "mu_v", "mu_g", "mu_a", "mu_d", "ob2", "ln_g", "ln_b")]
ROWS += [("L1_ffn_b_in", 32)]
NROW = sum(n for _, n in ROWS)
ROW_AT = {name: sum(n for _, n in ROWS[:i]) for i, (name, _) in enumerate(ROWS)}
EROWS = ["L1_attn_rb1", "L1_attn_kb1", "L1_attn_vb1", "L1_attn_ob1"]
HEADROWS = ["rem_mult", "iclr_mix", "bonus_mult", "rb2", "kb2", "vb2", "ab", "db"]

NORMS = ["x", "h", "a1_x", "a1_m", "mid", "a2_x", "a2_m", "lin", "ffn", "x1", "rw", "rw_o", "moe"]
NORM = {n: i for i, n in enumerate(NORMS)}

SCALAR_GROUPS = [("x_in", 2), ("params", 4), ("a1_q", 4), ("a1_v", 8), ("a1_h", 8),
                 ("a2_wkT", 1), ("a2_q", 4), ("a2_qp", 16), ("a2_o", 4), ("a2_h", 8),
                 ("lin_v", 16), ("ffn_q", 4), ("ffn_v", 4),
                 ("x1_wkT", 2), ("x1_q", 8), ("x1_qp", 16), ("x1_o", 8),
                 ("rw_r", 3), ("rw_k", 3), ("rw_v", 3), ("rw_g", 3), ("rw_a", 1), ("rw_d", 1), ("rw_back", 2),
                 ("rw_h", 3), ("moe_ct", 1), ("moe_h", NE * MC)]
VECTOR_GROUPS = [("a1_k", 4), ("a1_li1", 2), ("a1_li3", 2), ("a2_li1", 2), ("a2_li3", 2),
                 ("lin_q", 8), ("lin_k", 8), ("lin_a", 1), ("lin_o", 2), ("ffn_k", 4), ("ffn_o", 2), ("ffn_f", 2),
                 ("x1_out", 2), ("rw_heads", 1), ("rw_r2", 4), ("rw_k2", 4), ("rw_v2", 4), ("rw_a2", 4), ("rw_d2", 4),
                 ("rw_out", 2), ("moe_logits", 1), ("moe_xT", 4), ("moe_b", 4), ("moe_y", NE * PAIRS)]


def after(groups, name):
    n = 0
    for layer, count in groups:
        n += count
        if layer == name:
            return n
    raise KeyError(name)


def s_done(name):
    return after(SCALAR_GROUPS, name)


def v_done(name):
    return after(VECTOR_GROUPS, name)


class Count:

    def __init__(self):
        self.base, self.k, self.index = 0, 0, 0

    def step(self):
        self.k += 1
        self.index += 1

    @property
    def value(self):
        return self.base + self.k


class Settle:

    def __init__(self, eng):
        self.eng, self.zero = eng, eng.alloc_register("settled")
        eng.reg_mov(self.zero, 0)

    def __call__(self):
        self.eng.reg_add(self.zero, self.zero, self.zero)

    def finish(self, done):
        self.eng.wait_ge(done, self.zero)


@contextmanager
def loop(eng, start, end, *counts, settle=None):
    before = [(c.base, c.k, c.index) for c, _ in counts]
    if settle is not None:
        settle()
    with eng.Fori(start, end) as it:
        for (c, per), (base, k, _) in zip(counts, before):
            c.base, c.k = (it - start) * per + (base + k), 0
        yield it
        for c, per in counts:
            assert c.k == per, (c.k, per)
    for (c, per), (base, k, index) in zip(counts, before):
        c.base, c.k, c.index = base, k + per * (end - start), index + per * (end - start)


class Chain:

    def __init__(self, eng, sem):
        self.eng, self.sem, self.count = eng, sem, Count()

    def __call__(self, ins):
        ins.then_inc(self.sem, 1)
        self.count.step()
        self.eng.wait_ge(self.sem, self.count.value)


class Groups:

    def __init__(self, eng, banks, filled, emptied, plan):
        self.eng, self.banks, self.filled, self.emptied, self.plan = eng, banks, filled, emptied, list(plan)
        self.count, self.left = Count(), 0

    def layer(self, name):
        assert self.left == 0 and self.plan[0][0] == name, (name, self.plan[0], self.left)
        self.left = self.plan.pop(0)[1]

    def fill(self, emit):
        if self.count.index >= 2:
            self.eng.wait_ge(self.emptied, self.count.value - 1)
        bank = self.banks[self.count.index % 2]
        self.count.step()
        self.left -= 1
        emit(bank).then_inc(self.filled, 1)

    def take(self):
        bank = self.banks[self.count.index % 2]
        self.count.step()
        self.left -= 1
        self.eng.wait_ge(self.filled, self.count.value)
        return bank

    def release(self, ins, taken_since=0):
        ins.then_inc(self.emptied, 1)
        self.eng.wait_ge(self.emptied, self.count.value - taken_since)


class Region:

    def __init__(self, tensor, at=0):
        self.tensor, self.at = tensor, at

    def take(self, *shape, parts=P):
        n = 1
        for s in shape:
            n *= s
        view = self.tensor[0:parts, self.at:self.at + n]
        self.at += n
        assert self.at <= self.tensor.shape[1], (self.at, self.tensor.shape)
        if len(shape) == 2:
            view = view.rearrange("p (a b) -> p a b", b=shape[1])
        elif len(shape) == 3:
            view = view.rearrange("p (a b c) -> p a b c", b=shape[1], c=shape[2])
        return view


def perceiver_kernel(nc, io, out):
    ctx = ExitStack()
    with ctx:
        def sb(name, shape, dt=F32):
            return ctx.enter_context(nc.sbuf_tensor(name, shape, dt))

        sems = {}

        def sem(name):
            if name not in sems:
                sems[name] = ctx.enter_context(nc.semaphore(name))
            return sems[name]

        psum = ctx.enter_context(nc.psum_tensor("psum", [P, 8 * BANK], F32))

        def bank(i, n=1):
            return psum[:, i * BANK:(i + n) * BANK]

        X = sb("X", [P, KC, TOK])
        xc = sb("xc", [P, KC, TOK])
        sq = sb("sq", [P, KC, TOK])
        std = sb("std", [P, TOK])
        rstd = sb("rstd", [P, TOK])
        ident = sb("ident", [P, P])
        meanw = sb("meanw", [P, P])
        tri = sb("tri", [P, P])
        after_s = sb("after_s", [P, T])
        upto_t = sb("upto_t", [P, T])
        above_q = sb("above_q", [P, T])
        par = sb("par", [P, KC * NROW])
        epar = sb("epar", [P, 3 * len(EROWS)])
        small = sb("small", [P, 256])
        rep = sb("rep", [H, P])
        headrows = sb("headrows", [H, len(HEADROWS) * 16])
        headpar = sb("headpar", [P, len(HEADROWS), 16])
        weights = [sb("weights0", [P, 8224]), sb("weights1", [P, 7168])]
        work = sb("work", [P, 30720])

        cst = small[:, 0:4]
        mx16, sum16, rec16 = small[:, 16:32], small[:, 32:48], small[:, 48:64]
        ctx_sum, ctx_mean, ctx_var = small[:, 64:64 + NT], small[:, 80:80 + NT], small[:, 96:96 + NT]
        ctx_std, ctx_rstd = small[:, 112:112 + NT], small[:, 128:128 + NT]
        u_max, u_bias, u_sum, u_rec = (small[:, 144 + i:145 + i] for i in range(4))

        def col(name, i=0):
            at = (i % KC) * NROW + ROW_AT[name] + i // KC
            return par[:, at:at + 1]

        W = {}
        r = Region(weights[0])
        W["a1"] = dict(wq=r.take(KC, 512), wk=r.take(KC, 512), wv=r.take(KC, 512), li1=r.take(4, C),
                       li2=r.take(KC, HID), li3=r.take(MC, C))
        r = Region(weights[1])
        W["a2"] = dict(wq=r.take(KC, 512), wk=r.take(512), wv=r.take(512), li1=r.take(4, C),
                       li2=r.take(KC, HID), li3=r.take(MC, C))
        r = Region(weights[0])
        W["lin"] = dict(wq=r.take(KC, 1024), wk=r.take(KC, 1024), wv=r.take(KC, 1024), wo=r.take(8, C), wa=r.take(KC, H))
        r = Region(weights[1])
        W["ffn"] = dict(wq=r.take(KC, 512), wk=r.take(KC, 512), wv=r.take(KC, 512), wo=r.take(4, C), wff=r.take(KC, C))
        r = Region(weights[0])
        W["x1"] = dict(wq=r.take(KC, 1024), wk=r.take(1024), wv=r.take(1024), wo=r.take(8, C))
        r = Region(weights[1])
        W["rw"] = {n + "W1": r.take(KC, E1) for n in "rkvo"}
        W["rw"].update({n + "W2": r.take(3, C) for n in "rkvo"})
        W["rw"].update({n + "A": r.take(KC, LORA) for n in "gad"})
        W["rw"].update({n + "B": r.take(C, parts=LORA) for n in "gad"})
        r = Region(weights[0])
        W["moe"] = [dict(w_in=r.take(KC, HID), w_out=r.take(MC, C)) for _ in range(2)]
        r = Region(weights[1])
        W["gate"] = dict(wg=r.take(KC, NE), b_out=r.take(C, parts=NE))

        r = Region(work, 16384)
        x_rows = r.take(4, C)
        par_rows = r.take(C)
        epar_rows = r.take(E1)
        r = Region(work)
        h_in = r.take(KC, TOK)
        hq = r.take(KC, TOK)
        hk = r.take(KC, TOK)
        x_mid = r.take(KC, TOK)
        a1 = dict(QT=r.take(4, TOK), KT=r.take(4, TOK), V=r.take(NB, 512, parts=T), OT=r.take(4, TOK),
                  QS=r.take(4, P), KS=r.take(4, P), VS=r.take(2, 512, parts=T), prob=r.take(H, T), probT=r.take(H, P, parts=T))
        a1["HT"] = Region(work, 4096).take(MC, TOK)
        r = Region(work)
        w_in2 = r.take(KC, TOK)
        x_mid2 = r.take(KC, TOK)
        QP = r.take(H, TOK)
        z_at = r.at
        ZT = r.take(H, TOK)
        raw_at = r.at
        r.at += 2 * NT * CC
        Y = r.take(NT, CC)
        YT = r.take(S_CTX)
        r.at += NT * CC - S_CTX
        prob = r.take(NT * P)
        probT = r.take(NT, P)
        q_stage = r.take(P)
        z_stage = r.take(P)
        rz = Region(work, z_at)
        x_QT = rz.take(8, TOK)
        x_WkT = rz.take(8, P)
        x_xn = rz.take(KC, TOK)
        ro = Region(work, 2048)
        x_OT = ro.take(8, TOK)
        x_HT = ro.take(MC, TOK)
        x_m = Region(work, z_at + 8192).take(KC, TOK)
        ctx_g, ctx_b = r.take(CC), r.take(CC)
        r = Region(work)
        lin = dict(xn=r.take(KC, TOK), QT=r.take(8, TOK), KT=r.take(8, TOK), V=r.take(NB, 1024, parts=T), OT=r.take(8, TOK),
                   la=r.take(PAIRS, H), z=r.take(PAIRS, H), ba=r.take(H), QS=r.take(8, P), KS=r.take(8, P),
                   VS=r.take(2, 1024, parts=T), decay=r.take(H, T), prob=r.take(H, T))
        elu_at = r.at
        lin["probT"] = r.take(H, P, parts=T)
        elu = Region(work, elu_at).take(2, TOK)
        r = Region(work)
        ffn = dict(xn=r.take(KC, TOK), QT=r.take(4, TOK), KT=r.take(4, TOK), V=r.take(PAIRS, 512), OT=r.take(4, TOK),
                   QS=r.take(4, P), KS=r.take(4, P), VS=r.take(512), prob=r.take(H, T), z=r.take(KC, TOK), z2=r.take(KC, TOK))
        r = Region(work)
        hd = {n: r.take(T, 16) for n in ("r", "k", "v", "a", "d", "kn", "akn", "rk", "bonus")}
        gate = r.take(KC, TOK)
        s_tmp = r.take(16, 16)
        s_keep = r.take(16, 16)
        s_new = r.take(16, 16)
        s_row = r.take(16)
        nrm = r.take(T)
        nrm2 = r.take(T)
        hist_at = r.at
        hist = r.take(T + 1, 16, 16)
        r = Region(work, hist_at)
        rw_xn = r.take(KC, TOK)
        rw_in = r.take(KC, TOK)
        rw_HT = r.take(3, TOK)
        rw_lo = r.take(TOK, parts=LORA)
        rw_tm = r.take(2, 4 * C)
        r = Region(work)
        moe_xn = r.take(KC, TOK)
        moe_HT = [r.take(MC, TOK) for _ in range(2)]
        acc = r.take(4, C)
        logits = r.take(4, NE)
        comb = r.take(4, NE)
        combT = r.take(TOK, parts=NE)
        iota8 = r.take(NE)
        top8 = r.take(4, 8)
        topf = r.take(4, 8)
        hot = r.take(NE)
        hot2 = r.take(NE)
        dlt = r.take(8)
        topi = sb("topi", [P, 4, 8], U32)

        scratch = {n: nc.dram_tensor("scratch_" + n, (TOK, C), F32, kind="Internal").ap() for n in ("r", "k", "v", "a", "d", "o")}

        def place(h, per):
            return (h % per) * (H // per) + h // per

        def bc(ap, shape):
            return ap.to_broadcast(shape)

        block = ctx.enter_context(nc.Block())

        @block.sync
        def _(sp):
            def load(dst, src, name):
                sp.dma_start(dst, src).then_inc(sem(name), 16)

            def heads(ap):
                return ap.rearrange("h (k p) d -> p k h d", p=P)

            def rows(ap):
                return ap.rearrange("(k p) n -> p k n", p=P)

            load(x_rows, io["x"].rearrange("b t c -> (b t) c").rearrange("(n p) c -> p n c", p=P), "x_loaded")
            for name, n in ROWS:
                a = io[name]
                a = a.rearrange("e (k c) -> (e k) c", c=C) if name == "L1_ffn_b_in" else a.rearrange("(k c) -> k c", c=C)
                load(par_rows[ROW_AT[name]:ROW_AT[name] + n, :], a, "rows_loaded")
            for i, name in enumerate(EROWS):
                load(epar_rows[i:i + 1, :], io[name].rearrange("(a c) -> a c", a=1), "rows_loaded")

            def stage_heads(w, dst, src):
                for k in range(KC):
                    load(dst[:, k, :].rearrange("p (h d) -> p h d", h=H), src[:, k * P:(k + 1) * P, :].rearrange("h p d -> p h d"), w)

            a = "L0_xattn_a1_"
            stage_heads("a1_weights", W["a1"]["wq"], io[a + "wq"])
            stage_heads("a1_weights", W["a1"]["wk"], io[a + "wk"])
            stage_heads("a1_weights", W["a1"]["wv"], io[a + "wv"])
            load(W["a1"]["li1"], rows(io[a + "li1_w"]), "a1_weights")
            load(W["a1"]["li2"], rows(io[a + "li2_w"]), "a1_weights")
            load(W["a1"]["li3"], rows(io[a + "li3_w"]), "a1_weights")
            a = "L0_xattn_a2_"
            stage_heads("a2_weights", W["a2"]["wq"], io[a + "wq"])
            load(W["a2"]["wk"].rearrange("p (h d) -> p h d", h=H), io[a + "wk"].rearrange("h c d -> c h d"), "a2_weights")
            load(W["a2"]["wv"].rearrange("p (h d) -> p h d", h=H), io[a + "wv"].rearrange("h c d -> c h d"), "a2_weights")
            load(W["a2"]["li1"], rows(io[a + "li1_w"]), "a2_weights")
            load(W["a2"]["li2"], rows(io[a + "li2_w"]), "a2_weights")
            load(W["a2"]["li3"], rows(io[a + "li3_w"]), "a2_weights")
            for i, name in enumerate(HEADROWS):
                load(headrows[:, i * 16:(i + 1) * 16], io["L1_attn_" + name].rearrange("(h n) -> h n", h=H), "headrows_loaded")

            def load_batch(b):
                half = (b % 2) * (NT * CC)
                dst = work[:, ds(half + raw_at, (NT - 1) * CC)].rearrange("p (n c) -> p n c", c=CC)
                load(dst, io["ctx_512"][ds(b, 1), 0:(NT - 1) * P, :].rearrange("o (p n) c -> p (o n) c", p=P), "ctx_loaded")
                dst = work[0:TAIL, ds(half + (raw_at + (NT - 1) * CC), CC)]
                load(dst, io["ctx_512"][ds(b, 1), (NT - 1) * P:S_CTX, :].rearrange("o p c -> p (o c)"), "ctx_loaded")

            def load_context(which):
                sp.wait_ge(sem("tails_zeroed"), which + 1)
                load_batch(0)
                sp.wait_ge(sem("ctx_loaded"), which * NB * 32 + 32)
                load_batch(1)
                first = which * NB
                with loop(sp, first + 1, first + NB - 1) as taken:
                    sp.wait_ge(sem("ctx_loaded"), taken * 32 + 32)
                    sp.wait_ge(sem("ctx_centered" if which == 0 else "keys_made"), taken)
                    load_batch(taken - (first - 1))

            sp.wait_ge(sem("norm_out"), NORM["mid"] + 1)
            load(ctx_g, io["L0_xattn_a2_lny_g"].rearrange("(a c) -> a c", a=1).to_broadcast([P, CC]), "ctx_affine")
            load(ctx_b, io["L0_xattn_a2_lny_b"].rearrange("(a c) -> a c", a=1).to_broadcast([P, CC]), "ctx_affine")
            sp.wait_ge(sem("v_emptied"), v_done("a1_li3"))
            load(W["lin"]["wq"], rows(io["L0_attn_Wq"]), "lin_weights")
            load(W["lin"]["wk"], rows(io["L0_attn_Wk"]), "lin_weights")
            load(W["lin"]["wv"], rows(io["L0_attn_Wv"]), "lin_weights")
            load(W["lin"]["wo"], rows(io["L0_attn_Wo"]), "lin_weights")
            load(W["lin"]["wa"], rows(io["L0_attn_Wa"]), "lin_weights")
            load_context(0)

            sp.wait_ge(sem("ffn_zeroed"), 1)
            load(lin["ba"], io["L0_attn_ba"].rearrange("(a c) -> a c", a=1).to_broadcast([P, H]), "lin_bias")
            for k in range(KC):
                for n in ("q", "k", "v"):
                    load(W["ffn"]["w" + n][:, k, :].rearrange("p (h d) -> p h d", h=H)[:, :, 0:16],
                         io["L0_ffn_W" + n][k * P:(k + 1) * P, :].rearrange("p (h d) -> p h d", h=H), "ffn_weights")
            for m in range(4):
                for j in range(4):
                    hh = 4 * m + j
                    load(W["ffn"]["wo"][32 * j:32 * j + 16, m, :], io["L0_ffn_Wo"][hh * 16:(hh + 1) * 16, :], "ffn_weights")
            load(W["ffn"]["wff"], rows(io["L0_ffn_Wff"]), "ffn_weights")

            sp.wait_ge(sem("v_emptied"), v_done("lin_o"))
            load(W["x1"]["wq"], rows(io["L1_xattn_Wq"]), "x1_weights")
            load(W["x1"]["wk"], io["L1_xattn_Wk"], "x1_weights")
            load(W["x1"]["wv"], io["L1_xattn_Wv"], "x1_weights")
            load(W["x1"]["wo"], rows(io["L1_xattn_Wo"]), "x1_weights")
            sp.wait_ge(sem("ffn_added"), 1)
            for n in "rkvo":
                load(W["rw"][n + "W1"], rows(io[f"L1_attn_{n}W1"]), "rw_weights")
                for m, (e0, en) in enumerate(EC):
                    load(W["rw"][n + "W2"][0:en, m, :], io[f"L1_attn_{n}W2"][e0:e0 + en, :], "rw_weights")
            for n in "gad":
                load(W["rw"][n + "A"], rows(io[f"L1_attn_{n}A"]), "rw_weights")
                load(W["rw"][n + "B"], io[f"L1_attn_{n}B"], "rw_weights")
            load_context(1)

            def load_expert(e, slot):
                w = W["moe"][slot]
                load(w["w_in"], io["L1_ffn_W_in"][ds(e, 1), :, :].rearrange("o (k p) n -> p (o k) n", p=P), f"expert_loaded{slot}")
                load(w["w_out"], io["L1_ffn_W_out"][ds(e, 1), :, :].rearrange("o (k p) n -> p (o k) n", p=P), f"expert_loaded{slot}")

            sp.wait_ge(sem("v_emptied"), v_done("x1_out"))
            load_expert(0, 0)
            load_expert(1, 1)
            for i, n in enumerate("rkvad"):
                sp.wait_ge(sem("v_emptied"), v_done("rw_" + n + "2"))
                sp.dma_start(scratch[n].rearrange("(n p) c -> p n c", p=P),
                             rw_tm[:, i % 2, :].rearrange("p (n c) -> p n c", c=C)).then_inc(sem("scratch_written"), 16)
                sp.wait_ge(sem("scratch_written"), 16 * (i + 1))
                for b in range(NB):
                    load(hd[n][b * H:(b + 1) * H, :, :],
                         scratch[n][b * T:(b + 1) * T, :].rearrange("t (h n) -> h t n", h=H), "heads_loaded")
            sp.wait_ge(sem("rw_summed"), 1)
            for b in range(NB):
                sp.dma_start(scratch["o"][b * T:(b + 1) * T, :].rearrange("t (h n) -> h t n", h=H),
                             hd["v"][b * H:(b + 1) * H, :, :]).then_inc(sem("out_scratched"), 16)
            sp.wait_ge(sem("out_scratched"), 16 * NB)
            load(rw_tm[:, 0, :].rearrange("p (n c) -> p n c", c=C), scratch["o"].rearrange("(n p) c -> p n c", p=P), "rw_back_loaded")
            sp.wait_ge(sem("v_emptied"), v_done("rw_out"))
            load(W["gate"]["wg"], rows(io["L1_ffn_W_gate"]), "gate_weights")
            load(W["gate"]["b_out"], io["L1_ffn_b_out"], "gate_weights")
            with loop(sp, 1, NE // 2) as i:
                for slot in range(2):
                    sp.wait_ge(sem("v_emptied"), (i - 1) * (2 * PAIRS) + (v_done("moe_b") + (slot + 1) * PAIRS))
                    load_expert(i * 2 + slot, slot)
            sp.wait_ge(sem("v_emptied"), v_done("moe_y"))
            sp.dma_start(out.rearrange("b t c -> (b t) c").rearrange("(n p) c -> p n c", p=P), acc).then_inc(sem("stored"), 16)
            sp.wait_ge(sem("stored"), 16)

        @block.gpsimd
        def _(pool):
            settle = Settle(pool)
            chain = Chain(pool, sem("pool_order"))
            g = nc.gpsimd
            chain(g.memset(ident[:], 0.0))
            chain(g.affine_select(out=ident[:], in_=ident[:], compare_op=ALU.not_equal, fill=1.0, base=0,
                                  pattern=[[-1, P]], channel_multiplier=1))
            chain(g.memset(meanw[:], 1.0 / C))
            chain(g.memset(cst[:, 0:1], EPS))
            g.memset(cst[:, 1:2], 1e-6).then_inc(sem("constants"), 1)
            chain(g.memset(tri[:], 1.0))
            chain(g.memset(after_s[:], 1.0))
            chain(g.memset(upto_t[:], 1.0))
            chain(g.memset(above_q[:], 1.0))
            for b in range(2):
                q = slice(b * T, (b + 1) * T)
                chain(g.memset(tri[q, (1 - b) * T:(2 - b) * T], 0.0))
                chain(g.affine_select(out=tri[q, q], in_=tri[q, q], compare_op=ALU.is_ge, fill=0.0, base=0,
                                      pattern=[[1, T]], channel_multiplier=-1))
                chain(g.affine_select(out=after_s[q, :], in_=after_s[q, :], compare_op=ALU.is_ge, fill=0.0, base=-1,
                                      pattern=[[-1, T]], channel_multiplier=1))
                chain(g.affine_select(out=upto_t[q, :], in_=upto_t[q, :], compare_op=ALU.is_ge, fill=0.0, base=0,
                                      pattern=[[-1, T]], channel_multiplier=1))
                chain(g.affine_select(out=above_q[q, :], in_=above_q[q, :], compare_op=ALU.is_ge, fill=0.0, base=-1,
                                      pattern=[[1, T]], channel_multiplier=-1))
            chain(g.memset(rep[:], 0.0))
            rep3 = rep[:].rearrange("k (b h) -> k b h", h=H)
            g.affine_select(out=rep3, in_=rep3, compare_op=ALU.not_equal, fill=1.0, base=0,
                            pattern=[[0, NB], [-1, H]], channel_multiplier=1).then_inc(sem("masks"), 1)

            def stage_pairs(which, d):
                with loop(pool, 0, PAIRS, (chain.count, 2)) as p:
                    pool.wait_ge(sem("core_scores"), p + which * PAIRS)
                    chain(g.tensor_copy(d["QS"], d["QT"][:, :, ds(p * P, P)]))
                    chain(g.tensor_copy(d["KS"], d["KT"][:, :, ds(p * P, P)]))
                    pool.wait_ge(sem("core_o"), p + which * PAIRS)
                    src = d["V"][:, ds(p, 1), :].rearrange("p o n -> p (o n)") if which == 2 else d["V"][:, ds(p * 2, 2), :]
                    g.tensor_copy(d["VS"], src).then_inc(sem("core_staged"), 1)
                    pool.wait_ge(sem("core_staged"), p + (which * PAIRS + 1))

            pool.wait_ge(sem("s_emptied"), s_done("a1_v"))
            pool.wait_ge(sem("v_emptied"), v_done("a1_k"))
            stage_pairs(0, a1)

            def cross(which):
                name = ("a2", "x1")[which]
                pool.wait_ge(sem("s_emptied"), s_done(name + "_qp"))
                with loop(pool, 0, NB) as b:
                    if which == 1:
                        pool.wait_ge(sem("ctx_loaded"), b * 32 + (32 * NB + 32))
                        pool.wait_ge(sem("z_ready"), b * 8 + 64)
                        src = work[:, ds((b % 2) * (NT * CC) + raw_at, NT * CC)].rearrange("p (n c) -> p n c", c=CC)
                        g.tensor_copy(Y, src).then_inc(sem("keys_made"), 1)
                        pool.wait_ge(sem("keys_made"), b + (NB + 1))
                    with loop(pool, 0, 8, settle=settle) as hp:
                        pool.wait_ge(sem("u_scores"), b * 8 + hp + 64 * which)
                        g.tensor_copy(q_stage.rearrange("p (h t) -> p h t", h=2),
                                      QP[:, ds(hp * 2, 2), ds(b * T, T)]).then_inc(sem("u_staged"), 1)
                        pool.wait_ge(sem("u_staged"), b * 8 + hp + (64 * which + 1))

            pool.wait_ge(sem("norm_out"), NORM["a1_m"] + 1)
            chain(g.memset(work[:, raw_at + (NT - 1) * CC:raw_at + NT * CC], 0.0))
            g.memset(work[:, raw_at + (2 * NT - 1) * CC:raw_at + 2 * NT * CC], 0.0).then_inc(sem("tails_zeroed"), 1)
            cross(0)
            pool.wait_ge(sem("norm_out"), NORM["lin"] + 1)
            for n in ("wq", "wk", "wv"):
                chain(g.memset(W["ffn"][n], 0.0))
            g.memset(W["ffn"]["wo"], 0.0).then_inc(sem("ffn_zeroed"), 1)
            pool.wait_ge(sem("s_emptied"), s_done("lin_v"))
            pool.wait_ge(sem("v_emptied"), v_done("lin_k"))
            stage_pairs(1, lin)
            pool.wait_ge(sem("s_emptied"), s_done("ffn_v"))
            pool.wait_ge(sem("v_emptied"), v_done("ffn_k"))
            stage_pairs(2, ffn)
            pool.wait_ge(sem("ffn_added"), 1)
            chain(g.memset(work[:, raw_at + (NT - 1) * CC:raw_at + NT * CC], 0.0))
            g.memset(work[:, raw_at + (2 * NT - 1) * CC:raw_at + 2 * NT * CC], 0.0).then_inc(sem("tails_zeroed"), 1)
            cross(1)
            pool.wait_ge(sem("state"), 1)
            with loop(pool, 0, T, (chain.count, 2)) as t:
                v_j = hd["v"][:, ds(t, 1), :].rearrange("p o j -> p j o")
                rk_k = hd["rk"][:, ds(t, 1), :]
                d_j = hd["d"][:, ds(t, 1), :].rearrange("p o j -> p j o")
                w = hist[:, ds(t, 1), :, :].rearrange("p o j k -> p (o j) k")
                chain(g.tensor_tensor(s_new, bc(v_j, [P, 16, 16]), bc(rk_k, [P, 16, 16]), ALU.mult))
                pool.wait_ge(sem("state"), t + 1)
                chain(g.tensor_tensor(s_keep, w, bc(d_j, [P, 16, 16]), ALU.mult))
                g.tensor_tensor(s_keep, s_keep, s_new, ALU.add).then_inc(sem("state_kept"), 1)
                pool.wait_ge(sem("state_kept"), t + 1)
            pool.wait_ge(sem("norm_out"), NORM["moe"] + 1)
            g.iota(iota8, pattern=[[1, NE]], base=0, channel_multiplier=0, allow_small_or_imprecise_dtypes=True).then_inc(sem("iota"), 1)
            settle.finish(sem("constants"))

        @block.tensor
        def _(pe):
            settle = Settle(pe)
            mm, tr = nc.tensor.matmul, nc.tensor.transpose
            sg = Groups(pe, (bank(0), bank(1)), sem("s_filled"), sem("s_emptied"), SCALAR_GROUPS)
            vg = Groups(pe, (bank(2), bank(3)), sem("v_filled"), sem("v_emptied"), VECTOR_GROUPS)

            def product(groups, name, n, lhs, rhs, k, outs=None):
                groups.layer(name)
                for i in range(n):
                    def emit(b):
                        for j in range(k):
                            left, right = lhs(i, j), rhs(i, j)
                            o = b[0:left.shape[-1], 0:right.shape[-1]]
                            ins = mm(o, lhsT=left, rhs=right, start=(j == 0), stop=(j == k - 1))
                        return ins
                    groups.fill(emit)

            def norm(name, src):
                i = NORM[name]
                for k in range(KC):
                    ins = mm(bank(4), lhsT=meanw[:], rhs=src[:, k, :], start=(k == 0), stop=(k == KC - 1))
                ins.then_inc(sem("norm_mean"), 1)
                pe.wait_ge(sem("norm_squared"), i + 1)
                for k in range(KC):
                    ins = mm(bank(5), lhsT=meanw[:], rhs=sq[:, k, :], start=(k == 0), stop=(k == KC - 1))
                ins.then_inc(sem("norm_var"), 1)

            def core(which, d, dk, dv):
                pe.wait_ge(sem("masks"), 1)
                with loop(pe, 0, PAIRS) as p:
                    done = p + which * PAIRS
                    left, right = (d["KS"], d["QS"]) if which == 2 else (d["QS"], d["KS"])
                    per = P // dk
                    pe.wait_ge(sem("core_staged"), done + 1)
                    settle()
                    for h in range(H):
                        rows = slice((h % per) * dk, (h % per + 1) * dk)
                        for b in range(2):
                            ins = mm(bank(h % per)[b * T:(b + 1) * T, (h // per) * T:(h // per + 1) * T],
                                     lhsT=left[rows, h // per, b * T:(b + 1) * T],
                                     rhs=right[rows, h // per, b * T:(b + 1) * T], start=True, stop=True)
                    ins.then_inc(sem("core_scores"), 1)
                    if which == 1:
                        pe.wait_ge(sem("lin_spread"), p + 1)
                        for i in range(2):
                            ins = mm(bank(2 + i), lhsT=tri[:],
                                     rhs=d["decay"][:, 8 * i:8 * i + 8, :].rearrange("p h s -> p (h s)"), start=True, stop=True)
                        ins.then_inc(sem("lin_sums"), 1)
                    pe.wait_ge(sem("core_probs"), done + 1)
                    settle()
                    if which < 2:
                        for h in range(H):
                            ins = tr(bank(2 + h // 4)[0:T, (h % 4) * P:(h % 4 + 1) * P], d["prob"][:, h, :], ident[:])
                        ins.then_inc(sem("core_pT"), 1)
                        pe.wait_ge(sem("core_pT_s"), done + 1)
                        pe.wait_ge(sem("core_pT_v"), done + 1)
                        settle()
                    pe.wait_ge(sem("core_stored"), done)
                    settle()
                    perv = P // dv
                    for h in range(H):
                        for b in range(2):
                            q = slice(b * T, (b + 1) * T)
                            c0 = (h // perv) * P + b * T if which < 2 else b * BANK + (h // perv) * T
                            o = bank(6, 2)[(h % perv) * dv:(h % perv + 1) * dv, c0:c0 + T]
                            j = place(h, per)
                            if which == 2:
                                ins = mm(o, lhsT=d["VS"][q, h * dv:(h + 1) * dv], rhs=d["prob"][q, j, :], start=True, stop=True)
                            else:
                                ins = mm(o, lhsT=d["VS"][:, b, h * dv:(h + 1) * dv], rhs=d["probT"][:, j, q], start=True, stop=True)
                    ins.then_inc(sem("core_o"), 1)

            def cross(which, name, wk, n_chunk):
                D = n_chunk * P // H
                per = P // D
                sg.layer(name + "_wkT")
                for i in range(n_chunk // 4):
                    def emit(b):
                        for j in range(4):
                            c0 = (4 * i + j) * P
                            ins = tr(b[:, j * P:(j + 1) * P], wk[:, c0:c0 + P], ident[:])
                        return ins
                    sg.fill(emit)
                pe.wait_ge(sem("norm_out"), NORM["a2_x" if which == 0 else "x1"] + 1)
                product(sg, name + "_q", n_chunk, lambda i, j: W[name]["wq"][:, j, i * P:(i + 1) * P],
                        lambda i, j: x_xn[:, j, :], KC)
                pe.wait_ge(sem("s_emptied"), s_done(name + "_q"))

                def rows(h):
                    return slice((h % per) * D, (h % per + 1) * D)

                product(sg, name + "_qp", H, lambda h, j: x_WkT[rows(h), h // per, :],
                        lambda h, j: x_QT[rows(h), h // per, :], 1)
                pe.wait_ge(sem("s_emptied"), s_done(name + "_qp"))

                def scores(b, hp):
                    u = b * 8 + hp + 64 * which
                    pe.wait_ge(sem("u_staged"), u + 1)
                    pe.wait_ge(sem("u_exp"), u)
                    for i in range(4):
                        n = min(BANK, S_CTX - i * BANK)
                        ins = mm(bank(i)[:, 0:n], lhsT=q_stage, rhs=YT[:, i * BANK:i * BANK + n], start=True, stop=True)
                    ins.then_inc(sem("u_scores"), 1)

                def turn_z(b, hp):
                    u = b * 8 + hp + 64 * which
                    pe.wait_ge(sem("z_scaled"), u + 1)
                    pe.wait_ge(sem("zT_stored"), u)
                    tr(bank(7)[:, 0:P], z_stage, ident[:]).then_inc(sem("zT_ready"), 1)

                def weigh(b, hp):
                    u = b * 8 + hp + 64 * which
                    pe.wait_ge(sem("u_exp"), u + 1)

                    def turn(i):
                        side = "sv"[i % 2]
                        pe.wait_ge(sem("turned_out_" + side), u * 2 + i // 2)
                        for j in range(min(4, NT - 4 * i)):
                            t = 4 * i + j
                            n = min(P, S_CTX - t * P)
                            ins = tr(bank(4 + i % 2)[0:n, j * P:(j + 1) * P], prob[:, t * P:t * P + n], ident[:])
                        ins.then_inc(sem("turned_" + side), 1)

                    def add(i):
                        side = "sv"[i % 2]
                        pe.wait_ge(sem("turned_out_" + side), u * 2 + (i // 2 + 1))
                        for j in range(min(4, NT - 4 * i)):
                            t = 4 * i + j
                            n = min(P, S_CTX - t * P)
                            ins = mm(bank(6)[:, 0:CC], lhsT=probT[0:n, t, :], rhs=Y[0:n, t, :], start=(t == 0), stop=(t == NT - 1))
                        return ins

                    turn(0)
                    turn(1)
                    pe.wait_ge(sem("z_scaled"), u)
                    add(0)
                    turn(2)
                    add(1)
                    turn(3)
                    add(2)
                    add(3).then_inc(sem("z_ready"), 1)

                with loop(pe, 0, NB) as b:
                    nb = b + which * NB
                    pe.wait_ge(sem("keys_made"), nb + 1)
                    for t in range(NT):
                        n = min(P, S_CTX - t * P)
                        ins = tr(bank(t // 4)[:, (t % 4) * P:(t % 4) * P + n], Y[0:n, t, :], ident[0:n, 0:n])
                    ins.then_inc(sem("keys_turned"), 1)
                    pe.wait_ge(sem("keysT_s"), nb + 1)
                    pe.wait_ge(sem("keysT_v"), nb + 1)
                    scores(b, 0)
                    scores(b, 1)
                    weigh(b, 0)
                    with loop(pe, 2, 8, settle=settle) as hp:
                        scores(b, hp)
                        turn_z(b, hp - 2)
                        weigh(b, hp - 1)
                    turn_z(b, 6)
                    weigh(b, 7)
                    turn_z(b, 7)
                pe.wait_ge(sem("zT_stored"), 64 * (which + 1))
                sg.layer(name + "_o")
                for m in range(n_chunk):
                    def emit(b):
                        for j in range(per):
                            hh = m * per + j
                            ins = mm(b[j * D:(j + 1) * D, :], lhsT=W[name]["wv"][:, hh * D:(hh + 1) * D], rhs=ZT[:, hh, :],
                                     start=True, stop=True)
                        return ins
                    sg.fill(emit)
                pe.wait_ge(sem("s_emptied"), s_done(name + "_o"))

            def mlp(name, src, hT):
                w = W[name]
                pe.wait_ge(sem("norm_out"), NORM[name + "_m"] + 1)
                product(sg, name + "_h", MC, lambda i, j: w["li2"][:, j, i * P:(i + 1) * P], lambda i, j: src[:, j, :], KC)
                pe.wait_ge(sem("s_emptied"), s_done(name + "_h"))
                product(vg, name + "_li3", KC, lambda i, j: w["li3"][:, j, i * P:(i + 1) * P], lambda i, j: hT[:, j, :], MC)

            pe.wait_ge(sem("constants"), 1)
            pe.wait_ge(sem("x_loaded"), 16)
            sg.layer("x_in")
            for k in range(KC):
                def emit(b):
                    for n in range(4):
                        ins = tr(b[:, n * P:(n + 1) * P], x_rows[:, n, k * P:(k + 1) * P], ident[:])
                    return ins
                sg.fill(emit)
            pe.wait_ge(sem("rows_loaded"), 16 * (len(ROWS) + len(EROWS)))
            sg.layer("params")

            def emit(b):
                for k in range(KC):
                    ins = tr(b[:, k * NROW:(k + 1) * NROW], par_rows[0:NROW, k * P:(k + 1) * P], ident[0:NROW, 0:NROW])
                return ins
            sg.fill(emit)
            ne = len(EROWS)
            for m, (e0, en) in enumerate(EC):
                sg.fill(lambda b: tr(b[0:en, 0:ne], epar_rows[0:ne, e0:e0 + en], ident[0:ne, 0:ne]))
            pe.wait_ge(sem("s_emptied"), s_done("params"))
            norm("x", X)
            pe.wait_ge(sem("norm_out"), NORM["x"] + 1)
            norm("h", hq)
            pe.wait_ge(sem("norm_out"), NORM["h"] + 1)
            norm("a1_x", h_in)
            pe.wait_ge(sem("norm_out"), NORM["a1_x"] + 1)
            pe.wait_ge(sem("a1_weights"), 16 * 9)
            w = W["a1"]
            product(sg, "a1_q", 4, lambda i, j: w["wq"][:, j, i * P:(i + 1) * P], lambda i, j: hq[:, j, :], KC)
            product(vg, "a1_k", 4, lambda i, j: w["wk"][:, j, i * P:(i + 1) * P], lambda i, j: hk[:, j, :], KC)
            product(sg, "a1_v", NB, lambda i, j: hk[:, j, i * T:(i + 1) * T], lambda i, j: w["wv"][:, j, :], KC)
            pe.wait_ge(sem("s_emptied"), s_done("a1_v"))
            pe.wait_ge(sem("v_emptied"), v_done("a1_k"))
            core(0, a1, 32, 32)
            pe.wait_ge(sem("core_stored"), PAIRS)
            product(vg, "a1_li1", KC, lambda i, j: w["li1"][:, j, i * P:(i + 1) * P], lambda i, j: a1["OT"][:, j, :], 4)
            pe.wait_ge(sem("v_emptied"), v_done("a1_li1"))
            norm("a1_m", x_mid)
            mlp("a1", hq, a1["HT"])
            pe.wait_ge(sem("mid_ready"), 1)
            norm("mid", x_mid)
            pe.wait_ge(sem("norm_out"), NORM["mid"] + 1)
            norm("a2_x", w_in2)
            pe.wait_ge(sem("a2_weights"), 16 * 7)
            cross(0, "a2", W["a2"]["wk"], 4)
            w2 = W["a2"]
            product(vg, "a2_li1", KC, lambda i, j: w2["li1"][:, j, i * P:(i + 1) * P], lambda i, j: x_OT[:, j, :], 4)
            pe.wait_ge(sem("v_emptied"), v_done("a2_li1"))
            norm("a2_m", x_mid2)
            mlp("a2", x_m, x_HT)

            pe.wait_ge(sem("a2_added"), 1)
            norm("lin", X)
            pe.wait_ge(sem("norm_out"), NORM["lin"] + 1)
            pe.wait_ge(sem("lin_weights"), 16 * 5)
            wl = W["lin"]
            xn = lin["xn"]
            product(vg, "lin_q", 8, lambda i, j: wl["wq"][:, j, i * P:(i + 1) * P], lambda i, j: xn[:, j, :], KC)
            product(sg, "lin_v", 16, lambda i, j: xn[:, j, (i // 2) * T:(i // 2 + 1) * T],
                    lambda i, j: wl["wv"][:, j, (i % 2) * BANK:(i % 2 + 1) * BANK], KC)
            product(vg, "lin_k", 8, lambda i, j: wl["wk"][:, j, i * P:(i + 1) * P], lambda i, j: xn[:, j, :], KC)
            vg.layer("lin_a")

            def emit(b):
                for p in range(PAIRS):
                    for j in range(KC):
                        ins = mm(b[:, p * H:(p + 1) * H], lhsT=xn[:, j, p * P:(p + 1) * P], rhs=wl["wa"][:, j, :],
                                 start=(j == 0), stop=(j == KC - 1))
                return ins
            vg.fill(emit)
            pe.wait_ge(sem("s_emptied"), s_done("lin_v"))
            pe.wait_ge(sem("v_emptied"), v_done("lin_a"))
            core(1, lin, 64, 64)
            pe.wait_ge(sem("core_stored"), 2 * PAIRS)
            product(vg, "lin_o", KC, lambda i, j: wl["wo"][:, j, i * P:(i + 1) * P], lambda i, j: lin["OT"][:, j, :], 8)

            pe.wait_ge(sem("v_emptied"), v_done("lin_o"))
            norm("ffn", X)
            pe.wait_ge(sem("norm_out"), NORM["ffn"] + 1)
            pe.wait_ge(sem("ffn_weights"), 16 * (3 * KC + 16 + 1))
            wf = W["ffn"]
            xf = ffn["xn"]
            product(sg, "ffn_q", 4, lambda i, j: wf["wq"][:, j, i * P:(i + 1) * P], lambda i, j: xf[:, j, :], KC)
            product(vg, "ffn_k", 4, lambda i, j: wf["wk"][:, j, i * P:(i + 1) * P], lambda i, j: xf[:, j, :], KC)
            product(sg, "ffn_v", PAIRS, lambda i, j: xf[:, j, i * P:(i + 1) * P], lambda i, j: wf["wv"][:, j, :], KC)
            pe.wait_ge(sem("s_emptied"), s_done("ffn_v"))
            pe.wait_ge(sem("v_emptied"), v_done("ffn_k"))
            core(2, ffn, 32, 32)
            pe.wait_ge(sem("core_stored"), 3 * PAIRS)
            product(vg, "ffn_o", KC, lambda i, j: wf["wo"][:, j, i * P:(i + 1) * P], lambda i, j: ffn["OT"][:, j, :], 4)
            pe.wait_ge(sem("l2_squared"), 1)
            for k in range(KC):
                ins = mm(bank(4), lhsT=meanw[:], rhs=sq[:, k, :], start=(k == 0), stop=(k == KC - 1))
            ins.then_inc(sem("l2_sum"), 1)
            pe.wait_ge(sem("l2_out"), 1)
            product(vg, "ffn_f", KC, lambda i, j: wf["wff"][:, j, i * P:(i + 1) * P], lambda i, j: ffn["z"][:, j, :], KC)
            pe.wait_ge(sem("l2_squared"), 2)
            for k in range(KC):
                ins = mm(bank(4), lhsT=meanw[:], rhs=sq[:, k, :], start=(k == 0), stop=(k == KC - 1))
            ins.then_inc(sem("l2_sum"), 1)

            pe.wait_ge(sem("ffn_added"), 1)
            norm("x1", X)
            pe.wait_ge(sem("x1_weights"), 16 * 4)
            cross(1, "x1", W["x1"]["wk"], 8)
            product(vg, "x1_out", KC, lambda i, j: W["x1"]["wo"][:, j, i * P:(i + 1) * P], lambda i, j: x_OT[:, j, :], 8)

            settle.finish(sem("constants"))
            wr = W["rw"]
            pe.wait_ge(sem("v_emptied"), v_done("x1_out"))
            norm("rw", X)
            pe.wait_ge(sem("rw_weights"), 16 * (4 * 4 + 6))
            pe.wait_ge(sem("headrows_loaded"), 16 * len(HEADROWS))
            product(vg, "rw_heads", 1, lambda i, j: rep[:], lambda i, j: headrows[:], 1)
            for i, n in enumerate("rkv"):
                pe.wait_ge(sem("rw_shifted"), i + 1)
                sg.layer("rw_" + n)
                for m, (e0, en) in enumerate(EC):
                    def emit(b):
                        for j in range(KC):
                            ins = mm(b[0:en, :], lhsT=wr[n + "W1"][:, j, e0:e0 + en], rhs=rw_in[:, j, :], start=(j == 0), stop=(j == KC - 1))
                        return ins
                    sg.fill(emit)
                pe.wait_ge(sem("s_emptied"), s_done("rw_" + n))
                vg.layer("rw_" + n + "2")
                for p in range(4):
                    def emit(b):
                        for m, (e0, en) in enumerate(EC):
                            ins = mm(b[:, 0:C], lhsT=rw_HT[0:en, m, p * P:(p + 1) * P], rhs=wr[n + "W2"][0:en, m, :],
                                     start=(m == 0), stop=(m == 2))
                        return ins
                    vg.fill(emit)
            for i, n in enumerate("gad"):
                pe.wait_ge(sem("rw_shifted"), i + 4)
                sg.layer("rw_" + n)

                def emit(b):
                    for j in range(KC):
                        ins = mm(b[0:LORA, :], lhsT=wr[n + "A"][:, j, :], rhs=rw_in[:, j, :], start=(j == 0), stop=(j == KC - 1))
                    return ins
                sg.fill(emit)
                pe.wait_ge(sem("s_emptied"), s_done("rw_v") + 1 + (0, 3, 4)[i])
                if n == "g":
                    for m in range(KC):
                        sg.fill(lambda b: mm(b, lhsT=wr["gB"][:, m * P:(m + 1) * P], rhs=rw_lo, start=True, stop=True))
                else:
                    vg.layer("rw_" + n + "2")
                    for p in range(4):
                        vg.fill(lambda b: mm(b[:, 0:C], lhsT=rw_lo[:, p * P:(p + 1) * P], rhs=wr[n + "B"], start=True, stop=True))
            pe.wait_ge(sem("rw_back_loaded"), 16)
            sg.layer("rw_back")
            back = rw_tm[:, 0, :].rearrange("p (n c) -> p n c", c=C)
            for k in range(KC):
                def emit(b):
                    for n in range(4):
                        ins = tr(b[:, n * P:(n + 1) * P], back[:, n, k * P:(k + 1) * P], ident[:])
                    return ins
                sg.fill(emit)
            pe.wait_ge(sem("s_emptied"), s_done("rw_back"))
            norm("rw_o", rw_xn)
            pe.wait_ge(sem("rw_gated"), 1)
            sg.layer("rw_h")
            for m, (e0, en) in enumerate(EC):
                def emit(b):
                    for j in range(KC):
                        ins = mm(b[0:en, :], lhsT=wr["oW1"][:, j, e0:e0 + en], rhs=rw_in[:, j, :], start=(j == 0), stop=(j == KC - 1))
                    return ins
                sg.fill(emit)
            pe.wait_ge(sem("s_emptied"), s_done("rw_h"))
            vg.layer("rw_out")
            for i in range(KC):
                def emit(b):
                    for m, (e0, en) in enumerate(EC):
                        ins = mm(b, lhsT=wr["oW2"][0:en, m, i * P:(i + 1) * P], rhs=rw_HT[0:en, m, :], start=(m == 0), stop=(m == 2))
                    return ins
                vg.fill(emit)

            pe.wait_ge(sem("v_emptied"), v_done("rw_out"))
            norm("moe", X)
            pe.wait_ge(sem("norm_out"), NORM["moe"] + 1)
            pe.wait_ge(sem("gate_weights"), 32)
            vg.layer("moe_logits")

            def emit(b):
                for p in range(4):
                    for j in range(KC):
                        ins = mm(b[:, p * NE:(p + 1) * NE], lhsT=moe_xn[:, j, p * P:(p + 1) * P], rhs=W["gate"]["wg"][:, j, :],
                                 start=(j == 0), stop=(j == KC - 1))
                return ins
            vg.fill(emit)
            vg.layer("moe_xT")
            for p in range(4):
                def emit(b):
                    for k in range(KC):
                        ins = tr(b[:, k * P:(k + 1) * P], X[:, k, p * P:(p + 1) * P], ident[:])
                    return ins
                vg.fill(emit)
            pe.wait_ge(sem("combined"), 1)
            sg.layer("moe_ct")

            def emit(b):
                for p in range(4):
                    ins = tr(b[0:NE, p * P:(p + 1) * P], comb[:, p, :], ident[:])
                return ins
            sg.fill(emit)
            pe.wait_ge(sem("s_emptied"), s_done("moe_ct"))
            product(vg, "moe_b", 4, lambda i, j: combT[:, i * P:(i + 1) * P], lambda i, j: W["gate"]["b_out"], 1)
            sg.layer("moe_h")
            vg.layer("moe_y")
            with loop(pe, 0, NE // 2, (sg.count, 2 * MC), (vg.count, 2 * PAIRS)) as i:
                for slot in range(2):
                    w = W["moe"][slot]
                    pe.wait_ge(sem(f"expert_loaded{slot}"), i * 32 + 32)
                    for m in range(MC):
                        def emit(b):
                            for j in range(KC):
                                ins = mm(b, lhsT=w["w_in"][:, j, m * P:(m + 1) * P], rhs=moe_xn[:, j, :], start=(j == 0), stop=(j == KC - 1))
                            return ins
                        sg.fill(emit)
                    pe.wait_ge(sem("s_emptied"), sg.count.value)
                    for p in range(PAIRS):
                        def emit(b):
                            for m in range(MC):
                                ins = mm(b[:, 0:C], lhsT=moe_HT[slot][:, m, p * P:(p + 1) * P], rhs=w["w_out"][:, m, :],
                                         start=(m == 0), stop=(m == MC - 1))
                            return ins
                        vg.fill(emit)

        @block.scalar
        def _(act):
            chain = Chain(act, sem("scalar_order"))
            f = nc.scalar.activation
            sg = Groups(act, (bank(0), bank(1)), sem("s_filled"), sem("s_emptied"), SCALAR_GROUPS)

            def norm(name, eps=0):
                i = NORM[name]
                act.wait_ge(sem("norm_centered"), i + 1)
                f(sq[:], xc[:], ACT.Square).then_inc(sem("norm_squared"), 1)
                act.wait_ge(sem("norm_squared"), i + 1)
                act.wait_ge(sem("norm_var"), i + 1)
                f(std[:], bank(5), ACT.Sqrt, bias=cst[:, eps:eps + 1]).then_inc(sem("norm_std"), 1)
                act.wait_ge(sem("norm_std"), i + 1)

            def copies(name, n, dst, func=ACT.Copy, bias=None, rows=slice(0, P), cols=slice(0, BANK)):
                sg.layer(name)
                for i in range(n):
                    b = sg.take()
                    if bias is None:
                        sg.release(f(dst(i), b[rows, cols], func))
                    else:
                        sg.release(f(dst(i), b[rows, cols], func, bias=bias(i)))

            def core(which, d, scale, nch):
                with loop(act, 0, PAIRS) as p:
                    done = p + which * PAIRS
                    if which == 1:
                        act.wait_ge(sem("lin_sums"), p + 1)
                        f(d["decay"], bank(2, 2).rearrange("p (h s) -> p h s", h=H), ACT.Exp).then_inc(sem("core_exp"), 1)
                    else:
                        act.wait_ge(sem("core_shifted"), p + (which // 2) * PAIRS + 1)
                        f(d["prob"], d["prob"], ACT.Exp, scale=scale).then_inc(sem("core_exp"), 1)
                    act.wait_ge(sem("core_exp"), done + 1)
                    if which < 2:
                        act.wait_ge(sem("core_pT"), done + 1)
                        f(d["probT"][:, 0:8, :], bank(2, 2)[0:T, :].rearrange("p (h s) -> p h s", h=8), ACT.Copy).then_inc(sem("core_pT_s"), 1)
                        act.wait_ge(sem("core_pT_s"), done + 1)
                    act.wait_ge(sem("core_o"), done + 1)
                    o = bank(6, 2)[:, 0:nch * P].rearrange("p (m t) -> p m t", t=P)
                    dst = d["OT"][:, :, ds(p * P, P)]
                    if which == 2:
                        o = bank(6, 2).rearrange("p (b m t) -> p b m t", b=2, t=T)[:, :, 0:nch, :]
                        dst = dst.rearrange("p m (b t) -> p b m t", b=2)
                    f(dst, o, ACT.Copy).then_inc(sem("core_stored"), 1)
                    act.wait_ge(sem("core_stored"), done + 1)

            def cross(which, name, n_chunk, scale):
                sg.layer(name + "_wkT")
                for i in range(n_chunk // 4):
                    b = sg.take()
                    sg.release(f(x_WkT[:, 4 * i:4 * i + 4, :], b.rearrange("p (m c) -> p m c", c=P), ACT.Copy))
                copies(name + "_q", n_chunk, lambda i: x_QT[:, i, :])
                copies(name + "_qp", H, lambda i: QP[:, i, :])

                def spread(b, hp):
                    u = b * 8 + hp + 64 * which
                    act.wait_ge(sem("u_bias"), u + 1)
                    act.wait_ge(sem("turned_v"), u * 2)
                    act.wait_ge(sem("u_rec"), u)
                    f(prob[:, 0:S_CTX], bank(0, 4)[:, 0:S_CTX], ACT.Exp, bias=u_bias, scale=scale,
                      accum_out=u_sum).then_inc(sem("u_exp"), 1)
                    act.wait_ge(sem("u_exp"), u + 1)

                def turned(b, hp):
                    u = b * 8 + hp + 64 * which
                    for i in (0, 2):
                        act.wait_ge(sem("turned_s"), u * 2 + (i // 2 + 1))
                        f(probT[:, 4 * i:4 * i + 4, :], bank(4).rearrange("p (n c) -> p n c", c=P), ACT.Copy).then_inc(sem("turned_out_s"), 1)
                        act.wait_ge(sem("turned_out_s"), u * 2 + (i // 2 + 1))

                def z_out(b, hp):
                    u = b * 8 + hp + 64 * which
                    act.wait_ge(sem("zT_ready"), u + 1)
                    f(ZT[:, ds(hp * 2, 2), ds(b * T, T)], bank(7)[:, 0:P].rearrange("p (h t) -> p h t", h=2),
                      ACT.Copy).then_inc(sem("zT_stored"), 1)
                    act.wait_ge(sem("zT_stored"), u + 1)

                with loop(act, 0, NB) as b:
                    nb = b + which * NB
                    if which == 0:
                        act.wait_ge(sem("ctx_centered"), b + 1)
                        f(probT.rearrange("p n c -> p (n c)"), Y.rearrange("p n c -> p (n c)"), ACT.Square).then_inc(sem("ctx_squared"), 1)
                        act.wait_ge(sem("ctx_squared"), b + 1)
                        act.wait_ge(sem("ctx_vars"), b + 1)
                        f(ctx_std, ctx_var, ACT.Sqrt, bias=cst[:, 0:1], scale=1.0 / CC).then_inc(sem("ctx_stds"), 1)
                        act.wait_ge(sem("ctx_stds"), b + 1)
                    act.wait_ge(sem("keys_turned"), nb + 1)
                    f(YT[:, 0:2 * BANK], bank(0, 2), ACT.Copy).then_inc(sem("keysT_s"), 1)
                    act.wait_ge(sem("keysT_s"), nb + 1)
                    spread(b, 0)
                    turned(b, 0)
                    spread(b, 1)
                    with loop(act, 2, 8) as hp:
                        z_out(b, hp - 2)
                        turned(b, hp - 1)
                        spread(b, hp)
                    z_out(b, 6)
                    turned(b, 7)
                    z_out(b, 7)
                copies(name + "_o", n_chunk, lambda i: x_OT[:, i, :])

            copies("x_in", 2, lambda i: X[:, i, :])
            sg.layer("params")
            b = sg.take()
            sg.release(f(par[:], b[:, 0:KC * NROW], ACT.Copy))
            ne = len(EROWS)
            for m, (e0, en) in enumerate(EC):
                b = sg.take()
                sg.release(f(epar[0:en, m * ne:(m + 1) * ne], b[0:en, 0:ne], ACT.Copy))
            act.wait_ge(sem("constants"), 1)
            norm("x")
            norm("h")
            norm("a1_x")
            copies("a1_q", 4, lambda i: a1["QT"][:, i, :])
            copies("a1_v", NB, lambda i: a1["V"][:, i, :], rows=slice(0, T))
            core(0, a1, 32 ** -0.5, 4)
            norm("a1_m")
            copies("a1_h", MC, lambda i: a1["HT"][:, i, :], ACT.Gelu, lambda i: col("L0_xattn_a1_li2_b", i))
            norm("mid")
            norm("a2_x")
            cross(0, "a2", 4, 32 ** -0.5)
            norm("a2_m")
            copies("a2_h", MC, lambda i: x_HT[:, i, :], ACT.Gelu, lambda i: col("L0_xattn_a2_li2_b", i))
            norm("lin")

            def elus(which, n):
                for i in range(n):
                    act.wait_ge(sem("elu_clamped"), which * 8 + i + 1)
                    f(elu[:, i % 2, :], elu[:, i % 2, :], ACT.Exp).then_inc(sem("elu_exp"), 1)
                    act.wait_ge(sem("elu_exp"), which * 8 + i + 1)

            elus(0, 8)
            copies("lin_v", 16, lambda i: lin["V"][:, i // 2, (i % 2) * BANK:(i % 2 + 1) * BANK], rows=slice(0, T))
            elus(1, 8)
            act.wait_ge(sem("lin_abs"), 1)
            chain(f(lin["la"], lin["la"], ACT.Exp, scale=-1.0))
            f(lin["la"], lin["la"], ACT.Ln, bias=1.0).then_inc(sem("lin_log"), 1)
            act.wait_ge(sem("lin_log"), 1)
            core(1, lin, 1.0, 8)
            norm("ffn")
            copies("ffn_q", 4, lambda i: ffn["QT"][:, i, :])
            copies("ffn_v", PAIRS, lambda i: ffn["V"][:, i, :])
            core(2, ffn, 1.0 / 16, 4)
            for i in range(2):
                act.wait_ge(sem("v_emptied"), v_done(("ffn_o", "ffn_f")[i]))
                f(sq[:], ffn[("z", "z2")[i]], ACT.Square).then_inc(sem("l2_squared"), 1)
                act.wait_ge(sem("l2_squared"), i + 1)
                act.wait_ge(sem("l2_sum"), i + 1)
                f(std[:], bank(4), ACT.Sqrt, scale=float(C)).then_inc(sem("l2_norm"), 1)
                act.wait_ge(sem("l2_norm"), i + 1)
            act.wait_ge(sem("l2_out"), 2)
            f(ffn["z2"], ffn["z2"], ACT.Gelu).then_inc(sem("ffn_gelu"), 1)
            act.wait_ge(sem("ffn_gelu"), 1)
            norm("x1")
            cross(1, "x1", 8, 64 ** -0.5)
            norm("rw")
            for i, n in enumerate("rkv"):
                sg.layer("rw_" + n)
                for m, (e0, en) in enumerate(EC):
                    b = sg.take()
                    j = m * ne + EROWS.index("L1_attn_" + n + "b1")
                    if i and m == 0:
                        act.wait_ge(sem("v_filled"), v_done("rw_" + "rkv"[i - 1] + "2"))
                    sg.release(f(rw_HT[0:en, m, :], b[0:en, :], ACT.Gelu, bias=epar[0:en, j:j + 1]))
            copies("rw_g", 1, lambda i: rw_lo, rows=slice(0, LORA))
            for m in range(KC):
                b = sg.take()
                sg.release(f(gate[:, m, :], b, ACT.Sigmoid))
            for n in "ad":
                if n == "d":
                    act.wait_ge(sem("v_filled"), v_done("rw_a2"))
                copies("rw_" + n, 1, lambda i: rw_lo, rows=slice(0, LORA))
            act.wait_ge(sem("heads_biased"), 1)
            f(hd["a"], hd["a"], ACT.Sigmoid).then_inc(sem("heads_act"), 1)
            chain(f(hd["d"], hd["d"], ACT.Tanh))
            chain(f(hd["d"], hd["d"], ACT.Sigmoid))
            act.wait_ge(sem("heads_biased"), 2)
            f(nrm, nrm, ACT.Sqrt).then_inc(sem("heads_act"), 1)
            f(hd["d"], hd["d"], ACT.Exp, scale=-DECAY_C).then_inc(sem("heads_act"), 1)
            act.wait_ge(sem("heads_act"), 3)
            copies("rw_back", KC, lambda i: rw_xn[:, i, :])
            norm("rw_o", 1)
            sg.layer("rw_h")
            for m, (e0, en) in enumerate(EC):
                b = sg.take()
                j = m * ne + EROWS.index("L1_attn_ob1")
                sg.release(f(rw_HT[0:en, m, :], b[0:en, :], ACT.Gelu, bias=epar[0:en, j:j + 1]))
            norm("moe")
            act.wait_ge(sem("top_gap"), 1)
            f(dlt[:, 0:4], dlt[:, 0:4], ACT.Exp).then_inc(sem("top_exp"), 1)
            act.wait_ge(sem("top_exp"), 1)
            copies("moe_ct", 1, lambda i: combT, rows=slice(0, NE))
            sg.layer("moe_h")
            with loop(act, 0, NE // 2, (sg.count, 2 * MC)) as i:
                for slot in range(2):
                    act.wait_ge(sem("v_filled"), i * (2 * PAIRS) + (v_done("moe_b") + (slot - 2) * PAIRS + PAIRS))
                    for m in range(MC):
                        b = sg.take()
                        at = (m % KC) * NROW + ROW_AT["L1_ffn_b_in"] + m // KC + 4 * slot
                        sg.release(f(moe_HT[slot][:, m, :], b, ACT.Gelu, bias=par[:, ds(i * 8 + at, 1)]))

        @block.vector
        def _(dve):
            settle = Settle(dve)
            chain = Chain(dve, sem("vector_order"))
            v = nc.vector
            vg = Groups(dve, (bank(2), bank(3)), sem("v_filled"), sem("v_emptied"), VECTOR_GROUPS)

            def signal(ins, name, value=1):
                ins.then_inc(sem(name), 1)
                dve.wait_ge(sem(name), value)

            def norm(name, src, outs):
                i = NORM[name]
                dve.wait_ge(sem("norm_mean"), i + 1)
                chain(v.tensor_tensor(xc[:, 0, :], src[:, 0, :], bank(4), ALU.subtract))
                signal(v.tensor_tensor(xc[:, 1, :], src[:, 1, :], bank(4), ALU.subtract), "norm_centered", i + 1)
                dve.wait_ge(sem("norm_std"), i + 1)
                chain(v.reciprocal(rstd[:], std[:]))
                for n, (dst, g, b) in enumerate(outs):
                    for k in range(KC):
                        last_one = n == len(outs) - 1 and k == KC - 1
                        ins = v.tensor_tensor(dst[:, k, :], xc[:, k, :], rstd[:], ALU.mult)
                        if g is not None:
                            chain(ins)
                            ins = v.tensor_scalar(dst[:, k, :], dst[:, k, :], col(g, k), col(b, k), ALU.mult, ALU.add)
                        if last_one:
                            signal(ins, "norm_out", i + 1)
                        else:
                            chain(ins)

            def add_into(name, dst, bias, extra):
                vg.layer(name)
                for k in range(KC):
                    b = vg.take()
                    if bias is None:
                        vg.release(v.tensor_tensor(dst[:, k, :], b, extra[:, k, :], ALU.add))
                    else:
                        vg.release(v.scalar_tensor_tensor(out=dst[:, k, :], in0=b, scalar=col(bias, k), in1=extra[:, k, :],
                                                          op0=ALU.add, op1=ALU.add))

            def core(which, d):
                per, nch = (4, 4) if which != 1 else (2, 8)
                full = [P, per, nch, T]
                S = bank(0, per).rearrange("p (g c s) -> p g c s", g=per, s=T)[:, :, 0:nch, :]

                def heads(ap):
                    return ap.rearrange("p (g c) s -> p g c s", g=per)

                def spread(ap):
                    return bc(ap.rearrange("p (g c) -> p g c", g=per).unsqueeze(3), full)

                def over(mask):
                    return bc(mask[:].unsqueeze(1), [P, H, T])

                prob = d["prob"]
                steps = {0: 4, 1: 6, 2: 3}[which]
                with loop(dve, 0, PAIRS, (chain.count, steps)) as p:
                    done = p + which * PAIRS
                    if which == 1:
                        la = d["la"][:, ds(p, 1), :].rearrange("p o (c g) -> p g (o c)", g=per).unsqueeze(3)
                        for g in range(per):
                            ins = v.tensor_tensor(heads(d["decay"])[:, g, :, :], bc(la[:, g, :, :], [P, nch, T]),
                                                  bc(after_s[:].unsqueeze(1), [P, nch, T]), ALU.mult)
                            if g < per - 1:
                                chain(ins)
                        signal(ins, "lin_spread", p + 1)
                        dve.wait_ge(sem("core_scores"), done + 1)
                        dve.wait_ge(sem("core_exp"), done + 1)
                        chain(v.tensor_tensor(heads(prob), S, heads(d["decay"]), ALU.mult))
                        chain(v.tensor_tensor(prob, prob, over(upto_t), ALU.mult))
                        chain(v.tensor_reduce(sum16, prob, AX, ALU.add))
                        chain(v.tensor_scalar(sum16, sum16, 1e-6, None, ALU.add))
                        chain(v.reciprocal(rec16, sum16))
                        signal(v.tensor_tensor(heads(prob), heads(prob), spread(rec16), ALU.mult), "core_probs", done + 1)
                    else:
                        dve.wait_ge(sem("core_scores"), done + 1)
                        chain(v.tensor_reduce(mx16, S, AX, ALU.max))
                        signal(v.tensor_tensor(heads(prob), S, spread(mx16), ALU.subtract), "core_shifted",
                               p + ((which // 2) * PAIRS + 1))
                        dve.wait_ge(sem("core_exp"), done + 1)
                        chain(v.tensor_reduce(sum16, prob, AX, ALU.add))
                        chain(v.reciprocal(rec16, sum16))
                        ins = v.tensor_tensor(heads(prob), heads(prob), spread(rec16), ALU.mult)
                        if which == 0:
                            chain(ins)
                            ins = v.tensor_tensor(prob, prob, over(above_q), ALU.mult)
                        signal(ins, "core_probs", done + 1)
                    if which < 2:
                        dve.wait_ge(sem("core_pT"), done + 1)
                        signal(v.tensor_copy(d["probT"][:, 8:16, :], bank(4, 2)[0:T, :].rearrange("p (h s) -> p h s", h=8)),
                               "core_pT_v", done + 1)

            def cross(which, scale):
                def head_max(b, hp):
                    u = b * 8 + hp + 64 * which
                    dve.wait_ge(sem("u_scores"), u + 1)
                    chain(v.tensor_reduce(u_max, bank(0, 4)[:, 0:S_CTX], AX, ALU.max))
                    signal(v.tensor_scalar(u_bias, u_max, -scale, None, ALU.mult), "u_bias", u + 1)

                def recip(b, hp):
                    u = b * 8 + hp + 64 * which
                    dve.wait_ge(sem("u_exp"), u + 1)
                    signal(v.reciprocal(u_rec, u_sum), "u_rec", u + 1)

                def weigh(b, hp):
                    u = b * 8 + hp + 64 * which
                    for i in (1, 3):
                        n, tiles = (P, 4) if i == 1 else (TAIL, 1)
                        dve.wait_ge(sem("turned_v"), u * 2 + (i // 2 + 1))
                        signal(v.tensor_copy(probT[0:n, 4 * i:4 * i + tiles, :],
                                             bank(5)[0:n, 0:tiles * P].rearrange("p (n c) -> p n c", c=P)),
                               "turned_out_v", u * 2 + (i // 2 + 1))
                    dve.wait_ge(sem("z_ready"), u + 1)
                    signal(v.tensor_scalar(z_stage, bank(6)[:, 0:CC], u_rec, None, ALU.mult), "z_scaled", u + 1)

                full = [P, NT, CC]
                with loop(dve, 0, NB, (chain.count, (5 if which == 0 else 0) + 8)) as b:
                    nb = b + which * NB
                    if which == 0:
                        dve.wait_ge(sem("ctx_loaded"), b * 32 + 32)
                        src = work[:, ds((b % 2) * (NT * CC) + raw_at, NT * CC)].rearrange("p (n c) -> p n c", c=CC)
                        chain(v.tensor_reduce(ctx_sum, src, AX, ALU.add))
                        chain(v.tensor_scalar(ctx_mean, ctx_sum, 1.0 / CC, None, ALU.mult))
                        signal(v.tensor_tensor(Y, src, bc(ctx_mean.unsqueeze(2), full), ALU.subtract), "ctx_centered", b + 1)
                        dve.wait_ge(sem("ctx_squared"), b + 1)
                        signal(v.tensor_reduce(ctx_var, probT, AX, ALU.add), "ctx_vars", b + 1)
                        dve.wait_ge(sem("ctx_stds"), b + 1)
                        chain(v.reciprocal(ctx_rstd, ctx_std))
                        chain(v.tensor_tensor(Y, Y, bc(ctx_rstd.unsqueeze(2), full), ALU.mult))
                        chain(v.tensor_tensor(Y, Y, bc(ctx_g.unsqueeze(1), full), ALU.mult))
                        signal(v.tensor_tensor(Y, Y, bc(ctx_b.unsqueeze(1), full), ALU.add), "keys_made", b + 1)
                    dve.wait_ge(sem("keys_turned"), nb + 1)
                    signal(v.tensor_copy(YT[:, 2 * BANK:S_CTX], bank(2, 2)[:, 0:S_CTX - 2 * BANK]), "keysT_v", nb + 1)
                    head_max(b, 0)
                    recip(b, 0)
                    head_max(b, 1)
                    weigh(b, 0)
                    recip(b, 1)
                    with loop(dve, 2, 8, (chain.count, 1), settle=settle) as hp:
                        head_max(b, hp)
                        weigh(b, hp - 1)
                        recip(b, hp)
                    weigh(b, 7)

            a = "L0_xattn_"
            norm("x", X, [(hq, None, None)])
            norm("h", hq, [(h_in, a + "ln1_g", a + "ln1_b")])
            norm("a1_x", h_in, [(hq, a + "a1_lnx_g", a + "a1_lnx_b"), (hk, a + "a1_lny_g", a + "a1_lny_b")])
            vg.layer("a1_k")
            for i in range(4):
                b = vg.take()
                vg.release(v.tensor_copy(a1["KT"][:, i, :], b))
            dve.wait_ge(sem("masks"), 1)
            core(0, a1)
            add_into("a1_li1", x_mid, a + "a1_li1_b", h_in)
            norm("a1_m", x_mid, [(hq, a + "a1_ln3_g", a + "a1_ln3_b")])
            add_into("a1_li3", x_mid, a + "a1_li3_b", x_mid)
            signal(v.tensor_tensor(x_mid, x_mid, h_in, ALU.add), "mid_ready")
            norm("mid", x_mid, [(w_in2, a + "ln2_g", a + "ln2_b")])
            norm("a2_x", w_in2, [(x_xn, a + "a2_lnx_g", a + "a2_lnx_b")])
            dve.wait_ge(sem("ctx_affine"), 32)
            cross(0, 32 ** -0.5)
            add_into("a2_li1", x_mid2, a + "a2_li1_b", w_in2)
            norm("a2_m", x_mid2, [(x_m, a + "a2_ln3_g", a + "a2_ln3_b")])
            add_into("a2_li3", x_mid2, a + "a2_li3_b", x_mid2)
            chain(v.tensor_tensor(x_mid2, x_mid2, w_in2, ALU.add))
            signal(v.tensor_tensor(X[:], X[:], x_mid2, ALU.add), "a2_added")

            norm("lin", X, [(lin["xn"], None, None)])

            def elus(which, name, dst):
                vg.layer(name)
                banks = {}

                def clamp(i):
                    banks[i] = vg.take()
                    signal(v.tensor_scalar(elu[:, i % 2, :], banks[i], 0.0, None, ALU.min), "elu_clamped", which * 8 + i + 1)

                clamp(0)
                for i in range(8):
                    if i < 7:
                        clamp(i + 1)
                    dve.wait_ge(sem("elu_exp"), which * 8 + i + 1)
                    vg.release(v.scalar_tensor_tensor(out=dst[:, i, :], in0=banks[i], scalar=0.0, in1=elu[:, i % 2, :],
                                                      op0=ALU.max, op1=ALU.add), int(i < 7))

            elus(0, "lin_q", lin["QT"])
            elus(1, "lin_k", lin["KT"])
            vg.layer("lin_a")
            dve.wait_ge(sem("lin_bias"), 16)
            b = vg.take()
            vg.release(v.tensor_tensor(lin["z"], b[:, 0:PAIRS * H].rearrange("p (n h) -> p n h", h=H),
                                       bc(lin["ba"].unsqueeze(1), [P, PAIRS, H]), ALU.add))
            chain(v.tensor_scalar(lin["z"], lin["z"], 2.0, None, ALU.add))
            signal(v.scalar_tensor_tensor(out=lin["la"], in0=lin["z"], scalar=-1.0, in1=lin["z"], op0=ALU.mult, op1=ALU.max), "lin_abs")
            dve.wait_ge(sem("lin_log"), 1)
            chain(v.scalar_tensor_tensor(out=lin["la"], in0=lin["z"], scalar=0.0, in1=lin["la"], op0=ALU.min, op1=ALU.subtract))
            core(1, lin)
            add_into("lin_o", X, None, X)

            norm("ffn", X, [(ffn["xn"], None, None)])
            vg.layer("ffn_k")
            for i in range(4):
                b = vg.take()
                vg.release(v.tensor_copy(ffn["KT"][:, i, :], b))
            core(2, ffn)
            for i in range(2):
                z = ffn[("z", "z2")[i]]
                vg.layer(("ffn_o", "ffn_f")[i])
                for k in range(KC):
                    b = vg.take()
                    vg.release(v.tensor_copy(z[:, k, :], b))
                dve.wait_ge(sem("l2_norm"), i + 1)
                chain(v.tensor_scalar(std[:], std[:], 1e-12, None, ALU.max))
                chain(v.reciprocal(rstd[:], std[:]))
                chain(v.tensor_tensor(z[:, 0, :], z[:, 0, :], rstd[:], ALU.mult))
                signal(v.tensor_tensor(z[:, 1, :], z[:, 1, :], rstd[:], ALU.mult), "l2_out", i + 1)
            dve.wait_ge(sem("ffn_gelu"), 1)
            signal(v.tensor_tensor(X[:], X[:], ffn["z2"], ALU.add), "ffn_added")

            norm("x1", X, [(x_xn, None, None)])
            cross(1, 64 ** -0.5)
            add_into("x1_out", X, "L1_xattn_bo", X)

            settle.finish(sem("constants"))
            norm("rw", X, [(rw_xn, None, None)])
            vg.layer("rw_heads")
            b = vg.take()
            vg.release(v.tensor_copy(headpar[:].rearrange("p i n -> p (i n)"), b[:, 0:P]))
            HP = {n: bc(headpar[:, i:i + 1, :], [P, T, 16]) for i, n in enumerate(HEADROWS)}

            def shift(i):
                n = "rkvgad"[i]
                if i:
                    dve.wait_ge(sem("s_filled"), s_done("rw_" + "rkvgad"[i - 1]) - (2 if i == 4 else 0))
                mu = "L1_attn_mu_" + n
                chain(v.tensor_scalar(rw_in[:, 0, :], rw_xn[:, 0, :], col(mu, 0), None, ALU.add))
                signal(v.tensor_scalar(rw_in[:, 1, :], rw_xn[:, 1, :], col(mu, 1), None, ALU.add), "rw_shifted", i + 1)

            def latents_out(i):
                n = "rkvad"[i]
                if i >= 2:
                    dve.wait_ge(sem("scratch_written"), 16 * (i - 1))
                vg.layer("rw_" + n + "2")
                for p in range(4):
                    b = vg.take()
                    vg.release(v.tensor_copy(rw_tm[:, i % 2, p * C:(p + 1) * C], b[:, 0:C]))

            shift(0)
            shift(1)
            latents_out(0)
            shift(2)
            latents_out(1)
            shift(3)
            latents_out(2)
            shift(4)
            shift(5)
            latents_out(3)
            latents_out(4)
            dve.wait_ge(sem("heads_loaded"), 16 * NB * 5)
            chain(v.tensor_tensor(hd["a"], hd["a"], HP["ab"], ALU.add))
            signal(v.tensor_tensor(hd["d"], hd["d"], HP["db"], ALU.add), "heads_biased", 1)
            for n in "rkv":
                chain(v.tensor_tensor(hd[n], hd[n], HP[n + "b2"], ALU.add))
            chain(v.tensor_tensor(hd["kn"], hd["k"], HP["rem_mult"], ALU.mult))
            chain(v.tensor_tensor(hd["akn"], hd["kn"], hd["kn"], ALU.mult))
            signal(v.tensor_reduce(nrm, hd["akn"], AX, ALU.add), "heads_biased", 2)
            dve.wait_ge(sem("heads_act"), 3)
            chain(v.tensor_scalar(nrm, nrm, 1e-12, None, ALU.max))
            chain(v.reciprocal(nrm2, nrm))
            t16 = [P, T, 16]
            chain(v.tensor_tensor(hd["kn"], hd["kn"], bc(nrm2.unsqueeze(2), t16), ALU.mult))
            chain(v.scalar_tensor_tensor(out=hd["akn"], in0=hd["a"], scalar=-1.0, in1=HP["iclr_mix"], op0=ALU.add, op1=ALU.mult))
            chain(v.scalar_tensor_tensor(out=hd["rk"], in0=hd["akn"], scalar=1.0, in1=hd["k"], op0=ALU.add, op1=ALU.mult))
            chain(v.tensor_tensor(hd["akn"], hd["a"], hd["kn"], ALU.mult))
            chain(v.tensor_tensor(hd["bonus"], hd["r"], hd["rk"], ALU.mult))
            chain(v.tensor_reduce(nrm, hd["bonus"], AX, ALU.add))
            chain(v.tensor_scalar(nrm, nrm, 0.2, None, ALU.mult))
            chain(v.tensor_tensor(hd["bonus"], hd["v"], HP["bonus_mult"], ALU.mult))
            chain(v.tensor_tensor(hd["bonus"], hd["bonus"], bc(nrm.unsqueeze(2), t16), ALU.mult))
            signal(v.memset(hist[:, 0, :, :], 0.0), "state", 1)
            jk = [P, 16, 16]
            with loop(dve, 0, T, (chain.count, 3)) as t:
                wT = hist[:, ds(t, 1), :, :].rearrange("p o j k -> p (o k) j")
                chain(v.tensor_tensor(s_tmp, wT, bc(hd["akn"][:, ds(t, 1), :], jk), ALU.mult))
                chain(v.tensor_reduce(s_row, s_tmp, AX, ALU.add))
                chain(v.tensor_tensor(s_tmp, bc(hd["kn"][:, ds(t, 1), :].rearrange("p o j -> p j o"), jk),
                                      bc(s_row.unsqueeze(1), jk), ALU.mult))
                dve.wait_ge(sem("state_kept"), t + 1)
                signal(v.tensor_tensor(hist[:, ds(t + 1, 1), :, :].rearrange("p o j k -> p (o j) k"), s_keep, s_tmp, ALU.subtract),
                       "state", t + 2)
            chain(v.tensor_tensor(hist[:, 1:T + 1, :, :], hist[:, 1:T + 1, :, :], bc(hd["r"].unsqueeze(2), [P, T, 16, 16]), ALU.mult))
            chain(v.tensor_reduce(hd["v"], hist[:, 1:T + 1, :, :], AX, ALU.add))
            signal(v.tensor_tensor(hd["v"], hd["v"], hd["bonus"], ALU.add), "rw_summed")
            norm("rw_o", rw_xn, [(rw_in, "L1_attn_ln_g", "L1_attn_ln_b")])
            signal(v.tensor_tensor(rw_in, rw_in, gate, ALU.mult), "rw_gated")
            add_into("rw_out", X, "L1_attn_ob2", X)

            norm("moe", X, [(moe_xn, None, None)])
            vg.layer("moe_logits")
            b = vg.take()
            vg.release(v.tensor_copy(logits, b[:, 0:4 * NE].rearrange("p (n e) -> p n e", e=NE)))
            vg.layer("moe_xT")
            for p in range(4):
                b = vg.take()
                vg.release(v.tensor_copy(acc[:, p, :], b[:, 0:C]))
            for p in range(4):
                chain(v.max(top8[:, p, :], logits[:, p, :]))
                chain(v.max_index(topi[:, p, :], top8[:, p, :], logits[:, p, :]))
            chain(v.tensor_copy(topf, topi[:]))
            signal(v.tensor_tensor(dlt[:, 0:4].unsqueeze(2), top8[:, :, 1:2], top8[:, :, 0:1], ALU.subtract), "top_gap")
            dve.wait_ge(sem("top_exp"), 1)
            chain(v.tensor_scalar(dlt[:, 4:8], dlt[:, 0:4], 1.0, None, ALU.add))
            chain(v.reciprocal(dlt[:, 4:8], dlt[:, 4:8]))
            chain(v.tensor_tensor(dlt[:, 0:4], dlt[:, 0:4], dlt[:, 4:8], ALU.mult))
            dve.wait_ge(sem("iota"), 1)
            for p in range(4):
                chain(v.tensor_scalar(hot, iota8, topf[:, p, 0:1], dlt[:, 4 + p:5 + p], ALU.is_equal, ALU.mult))
                chain(v.tensor_scalar(hot2, iota8, topf[:, p, 1:2], dlt[:, p:p + 1], ALU.is_equal, ALU.mult))
                ins = v.tensor_tensor(comb[:, p, :], hot, hot2, ALU.add)
                if p < 3:
                    chain(ins)
                else:
                    signal(ins, "combined")
            vg.layer("moe_b")
            for p in range(4):
                b = vg.take()
                vg.release(v.tensor_tensor(acc[:, p, :], b[:, 0:C], acc[:, p, :], ALU.add))
            vg.layer("moe_y")
            with loop(dve, 0, NE // 2, (vg.count, 2 * PAIRS)) as i:
                for slot in range(2):
                    for p in range(PAIRS):
                        b = vg.take()
                        vg.release(v.scalar_tensor_tensor(out=acc[:, p, :], in0=b[:, 0:C], scalar=comb[:, p, ds(i * 2 + slot, 1)],
                                                          in1=acc[:, p, :], op0=ALU.mult, op1=ALU.add))


_UNUSED = ("L1_attn_keys", "L1_attn_values", "L1_attn_attn_mask")
_OUT = (NB, T, C)


def kernel(**inputs):
    import numpy as _np
    import concourse.bacc as _bacc
    from concourse.bass_utils import run_bass_kernel_spmd as _run

    nc = _bacc.Bacc("TRN2", target_bir_lowering=False, num_devices=1)
    arrays, io = {}, {}
    for name, a in inputs.items():
        if name in _UNUSED:
            continue
        a = _np.ascontiguousarray(a)
        arrays[f"in_{name}"] = a
        io[name] = nc.dram_tensor(f"in_{name}", a.shape, mybir.dt.from_np(a.dtype), kind="ExternalInput").ap()
    out = nc.dram_tensor("out", _OUT, F32, kind="ExternalOutput").ap()
    perceiver_kernel(nc, io, out)
    r = _run(nc, [arrays], core_ids=[0])
    return r.results[0]["out"]
```

```python
from contextlib import ExitStack, contextmanager

import concourse.bass as bass
from concourse import mybir

F32 = mybir.dt.float32
U32 = mybir.dt.uint32
ALU = mybir.AluOpType
ACT = mybir.ActivationFunctionType
AX = mybir.AxisListType.X
ds = bass.ds

P = 128
NB, T, C = 8, 64, 256
TOK = NB * T
KC = C // P
PAIRS = NB // 2
H = 16
S_CTX, CC = 1601, 128
NT = -(-S_CTX // P)
TAIL = S_CTX - (NT - 1) * P
HID = 1024
MC = HID // P
E1 = 307
EC = [(0, 128), (128, 128), (256, E1 - 256)]
LORA = 64
NE = 8
BANK = 512
DECAY_C = 0.7408182206817179
EPS = 1e-5

ROWS = [("L0_xattn_" + n, 1) for n in (
    "ln1_g", "ln1_b", "ln2_g", "ln2_b", "a1_li1_b", "a1_lnx_g", "a1_lnx_b", "a1_lny_g", "a1_lny_b", "a1_ln3_g",
    "a1_ln3_b", "a1_li3_b", "a2_li1_b", "a2_lnx_g", "a2_lnx_b", "a2_ln3_g", "a2_ln3_b", "a2_li3_b")]
ROWS += [("L0_xattn_a1_li2_b", 4), ("L0_xattn_a2_li2_b", 4), ("L1_xattn_bo", 1)]
ROWS += [("L1_attn_" + n, 1) for n in ("mu_r", "mu_k", "mu_v", "mu_g", "mu_a", "mu_d", "ob2", "ln_g", "ln_b")]
ROWS += [("L1_ffn_b_in", 32)]
NROW = sum(n for _, n in ROWS)
ROW_AT = {name: sum(n for _, n in ROWS[:i]) for i, (name, _) in enumerate(ROWS)}
EROWS = ["L1_attn_rb1", "L1_attn_kb1", "L1_attn_vb1", "L1_attn_ob1"]
HEADROWS = ["rem_mult", "iclr_mix", "bonus_mult", "rb2", "kb2", "vb2", "ab", "db"]

NORMS = ["x", "h", "a1_x", "a1_m", "mid", "a2_x", "a2_m", "lin", "ffn", "x1", "rw", "rw_o", "moe"]
NORM = {n: i for i, n in enumerate(NORMS)}

SCALAR_GROUPS = [("x_in", 2), ("params", 4), ("a1_q", 4), ("a1_v", 8), ("a1_h", 8),
                 ("a2_wkT", 1), ("a2_q", 4), ("a2_qp", 16), ("a2_o", 4), ("a2_h", 8),
                 ("lin_v", 16), ("ffn_q", 4), ("ffn_v", 4),
                 ("x1_wkT", 2), ("x1_q", 8), ("x1_qp", 16), ("x1_o", 8),
                 ("rw_r", 3), ("rw_k", 3), ("rw_v", 3), ("rw_g", 3), ("rw_a", 1), ("rw_d", 1), ("rw_back", 2),
                 ("rw_h", 3), ("moe_ct", 1), ("moe_h", NE * MC)]
VECTOR_GROUPS = [("a1_k", 4), ("a1_li1", 2), ("a1_li3", 2), ("a2_li1", 2), ("a2_li3", 2),
                 ("lin_q", 8), ("lin_k", 8), ("lin_a", 1), ("lin_o", 2), ("ffn_k", 4), ("ffn_o", 2), ("ffn_f", 2),
                 ("x1_out", 2), ("rw_heads", 1), ("rw_r2", 4), ("rw_k2", 4), ("rw_v2", 4), ("rw_a2", 4), ("rw_d2", 4),
                 ("rw_out", 2), ("moe_logits", 1), ("moe_xT", 4), ("moe_b", 4), ("moe_y", NE * PAIRS)]


def after(groups, name):
    n = 0
    for layer, count in groups:
        n += count
        if layer == name:
            return n
    raise KeyError(name)


def s_done(name):
    return after(SCALAR_GROUPS, name)


def v_done(name):
    return after(VECTOR_GROUPS, name)


class Count:

    def __init__(self):
        self.base, self.k, self.index = 0, 0, 0

    def step(self):
        self.k += 1
        self.index += 1

    @property
    def value(self):
        return self.base + self.k


class Settle:

    def __init__(self, eng):
        self.eng, self.one = eng, eng.alloc_register("settled")
        eng.reg_mov(self.one, 1)

    def __call__(self):
        self.eng.reg_alu(self.one, self.one, self.one, ALU.bitwise_or)

    def finish(self, done):
        self.eng.wait_ge(done, self.one)


@contextmanager
def loop(eng, start, end, *counts, settle=None):
    before = [(c.base, c.k, c.index) for c, _ in counts]
    if settle is not None:
        settle()
    with eng.Fori(start, end) as it:
        for (c, per), (base, k, _) in zip(counts, before):
            c.base, c.k = (it - start) * per + (base + k), 0
        yield it
        for c, per in counts:
            assert c.k == per, (c.k, per)
    for (c, per), (base, k, index) in zip(counts, before):
        c.base, c.k, c.index = base, k + per * (end - start), index + per * (end - start)


class Chain:

    def __init__(self, eng, sem):
        self.eng, self.sem, self.count = eng, sem, Count()

    def __call__(self, ins):
        ins.then_inc(self.sem, 1)
        self.count.step()
        self.eng.wait_ge(self.sem, self.count.value)


class Groups:

    def __init__(self, eng, banks, filled, emptied, plan):
        self.eng, self.banks, self.filled, self.emptied, self.plan = eng, banks, filled, emptied, list(plan)
        self.count, self.left = Count(), 0

    def layer(self, name):
        assert self.left == 0 and self.plan[0][0] == name, (name, self.plan[0], self.left)
        self.left = self.plan.pop(0)[1]

    def fill(self, emit):
        if self.count.index >= 2:
            self.eng.wait_ge(self.emptied, self.count.value - 1)
        bank = self.banks[self.count.index % 2]
        self.count.step()
        self.left -= 1
        emit(bank).then_inc(self.filled, 1)

    def take(self):
        bank = self.banks[self.count.index % 2]
        self.count.step()
        self.left -= 1
        self.eng.wait_ge(self.filled, self.count.value)
        return bank

    def release(self, ins, taken_since=0):
        ins.then_inc(self.emptied, 1)
        self.eng.wait_ge(self.emptied, self.count.value - taken_since)


class Region:

    def __init__(self, tensor, at=0):
        self.tensor, self.at = tensor, at

    def take(self, *shape, parts=P):
        n = 1
        for s in shape:
            n *= s
        view = self.tensor[0:parts, self.at:self.at + n]
        self.at += n
        assert self.at <= self.tensor.shape[1], (self.at, self.tensor.shape)
        if len(shape) == 2:
            view = view.rearrange("p (a b) -> p a b", b=shape[1])
        elif len(shape) == 3:
            view = view.rearrange("p (a b c) -> p a b c", b=shape[1], c=shape[2])
        return view


def perceiver_kernel(nc, io, out):
    ctx = ExitStack()
    with ctx:
        def sb(name, shape, dt=F32):
            return ctx.enter_context(nc.sbuf_tensor(name, shape, dt))

        sems = {}

        def sem(name):
            if name not in sems:
                sems[name] = ctx.enter_context(nc.semaphore(name))
            return sems[name]

        psum = ctx.enter_context(nc.psum_tensor("psum", [P, 8 * BANK], F32))

        def bank(i, n=1):
            return psum[:, i * BANK:(i + n) * BANK]

        X = sb("X", [P, KC, TOK])
        xc = sb("xc", [P, KC, TOK])
        sq = sb("sq", [P, KC, TOK])
        std = sb("std", [P, TOK])
        rstd = sb("rstd", [P, TOK])
        ident = sb("ident", [P, P])
        meanw = sb("meanw", [P, P])
        tri = sb("tri", [P, P])
        after_s = sb("after_s", [P, T])
        upto_t = sb("upto_t", [P, T])
        above_q = sb("above_q", [P, T])
        par = sb("par", [P, KC * NROW])
        epar = sb("epar", [P, 3 * len(EROWS)])
        small = sb("small", [P, 256])
        rep = sb("rep", [H, P])
        headrows = sb("headrows", [H, len(HEADROWS) * 16])
        headpar = sb("headpar", [P, len(HEADROWS), 16])
        weights = [sb("weights0", [P, 8224]), sb("weights1", [P, 7168])]
        work = sb("work", [P, 30720])

        cst = small[:, 0:4]
        mx16, sum16, rec16 = small[:, 16:32], small[:, 32:48], small[:, 48:64]
        ctx_sum, ctx_mean, ctx_var = small[:, 64:64 + NT], small[:, 80:80 + NT], small[:, 96:96 + NT]
        ctx_std, ctx_rstd = small[:, 112:112 + NT], small[:, 128:128 + NT]
        u_max, u_total, u_rec = small[:, 144:146], small[:, 146:147], small[:, 147:148]
        u_bias = [small[:, 148 + k:149 + k] for k in range(2)]
        u_sum = [small[:, 150 + 2 * k:152 + 2 * k] for k in range(2)]
        ctx_g, ctx_b = small[:, 154:155], small[:, 155:156]

        def col(name, i=0):
            at = (i % KC) * NROW + ROW_AT[name] + i // KC
            return par[:, at:at + 1]

        W = {}
        r = Region(weights[0])
        W["a1"] = dict(wq=r.take(KC, 512), wk=r.take(KC, 512), wv=r.take(KC, 512), li1=r.take(4, C),
                       li2=r.take(KC, HID), li3=r.take(MC, C))
        r = Region(weights[1])
        W["a2"] = dict(wq=r.take(KC, 512), wk=r.take(512), wv=r.take(512), li1=r.take(4, C),
                       li2=r.take(KC, HID), li3=r.take(MC, C))
        r = Region(weights[0])
        W["lin"] = dict(wq=r.take(KC, 1024), wk=r.take(KC, 1024), wv=r.take(KC, 1024), wo=r.take(8, C), wa=r.take(KC, H))
        r = Region(weights[1])
        W["ffn"] = dict(wq=r.take(KC, 512), wk=r.take(KC, 512), wv=r.take(KC, 512), wo=r.take(4, C), wff=r.take(KC, C))
        r = Region(weights[0])
        W["x1"] = dict(wq=r.take(KC, 1024), wk=r.take(1024), wv=r.take(1024), wo=r.take(8, C))
        r = Region(weights[1])
        W["rw"] = {n + "W1": r.take(KC, E1) for n in "rkvo"}
        W["rw"].update({n + "W2": r.take(3, C) for n in "rkvo"})
        W["rw"].update({n + "A": r.take(KC, LORA) for n in "gad"})
        W["rw"].update({n + "B": r.take(C, parts=LORA) for n in "gad"})
        r = Region(weights[0])
        W["moe"] = [dict(w_in=r.take(KC, HID), w_out=r.take(MC, C)) for _ in range(2)]
        r = Region(weights[1])
        W["gate"] = dict(wg=r.take(KC, NE), b_out=r.take(C, parts=NE))

        r = Region(work, 16384)
        x_rows = r.take(4, C)
        par_rows = r.take(C)
        epar_rows = r.take(E1)
        r = Region(work)
        h_in = r.take(KC, TOK)
        hq = r.take(KC, TOK)
        hk = r.take(KC, TOK)
        x_mid = r.take(KC, TOK)
        a1 = dict(QT=r.take(4, TOK), KT=r.take(4, TOK), V=r.take(NB, 512, parts=T), OT=r.take(4, TOK),
                  QS=r.take(4, P), KS=r.take(4, P), VS=r.take(2, 512, parts=T), prob=r.take(H, T), probT=r.take(H, P, parts=T))
        a1["HT"] = Region(work, 4096).take(MC, TOK)
        r = Region(work)
        w_in2 = r.take(KC, TOK)
        x_mid2 = r.take(KC, TOK)
        QZ = r.take(NB * H * T)
        phase_at = r.at
        x_QT = r.take(8, TOK)
        x_WkT = r.take(8, P)
        x_xn = r.take(KC, TOK)
        YT = [Region(work, phase_at + i * (S_CTX + 1)).take(S_CTX) for i in range(2)]
        raw = r.take(NT, CC)
        Y = [r.take(NT, CC) for _ in range(2)]
        prob = [r.take(NT * P) for _ in range(2)]
        probT = r.take(NT, P)
        q_stage = [r.take(P) for _ in range(2)]
        z_stage = r.take(P)
        ctx_sq = r.take(NT, CC)
        ro = Region(work, phase_at)
        x_OT = ro.take(8, TOK)
        x_HT = ro.take(MC, TOK)
        x_m = ro.take(KC, TOK)

        def unit_rows(u):
            return QZ[:, ds(u * P, P)]

        def head_rows(h):
            return QZ.rearrange("p (b h t) -> p b h t", h=H, t=T)[:, :, h, :]

        def units(eng, batch):
            batch(0, 0, True, False)
            with loop(eng, 0, (NB - 2) // 2) as p:
                batch(p * 2 + 1, 1, False, False)
                batch(p * 2 + 2, 0, False, False)
            batch(NB - 1, 1, False, True)

        def pairs(eng, settle, first, n, step):
            if first:
                step(0, 0, True)
                step(1, 1, False)
            with loop(eng, int(first), n, settle=settle) as j:
                step(j * 2, 0, False)
                step(j * 2 + 1, 1, False)
        r = Region(work)
        lin = dict(xn=r.take(KC, TOK), QT=r.take(8, TOK), KT=r.take(8, TOK), V=r.take(NB, 1024, parts=T), OT=r.take(8, TOK),
                   la=r.take(PAIRS, H), z=r.take(PAIRS, H), ba=r.take(H), QS=r.take(8, P), KS=r.take(8, P),
                   VS=r.take(2, 1024, parts=T), decay=r.take(H, T), prob=r.take(H, T))
        elu_at = r.at
        lin["probT"] = r.take(H, P, parts=T)
        elu = Region(work, elu_at).take(2, TOK)
        r = Region(work)
        ffn = dict(xn=r.take(KC, TOK), QT=r.take(4, TOK), KT=r.take(4, TOK), V=r.take(PAIRS, 512), OT=r.take(4, TOK),
                   QS=r.take(4, P), KS=r.take(4, P), VS=r.take(512), prob=r.take(H, T), z=r.take(KC, TOK), z2=r.take(KC, TOK))
        r = Region(work)
        hd = {n: r.take(T, 16) for n in ("r", "k", "v", "a", "d", "kn", "akn", "rk", "bonus")}
        gate = r.take(KC, TOK)
        s_tmp = r.take(16, 16)
        s_keep = r.take(16, 16)
        s_new = r.take(16, 16)
        s_row = r.take(16)
        nrm = r.take(T)
        nrm2 = r.take(T)
        hist_at = r.at
        hist = r.take(T + 1, 16, 16)
        r = Region(work, hist_at)
        rw_xn = r.take(KC, TOK)
        rw_in = r.take(KC, TOK)
        rw_HT = r.take(3, TOK)
        rw_lo = r.take(TOK, parts=LORA)
        rw_tm = r.take(2, 4 * C)
        r = Region(work)
        moe_xn = r.take(KC, TOK)
        moe_HT = [r.take(MC, TOK) for _ in range(2)]
        acc = r.take(4, C)
        logits = r.take(4, NE)
        comb = r.take(4, NE)
        combT = r.take(TOK, parts=NE)
        iota8 = r.take(NE)
        top8 = r.take(4, 8)
        topf = r.take(4, 8)
        hot = r.take(NE)
        hot2 = r.take(NE)
        dlt = r.take(8)
        topi = sb("topi", [P, 4, 8], U32)

        scratch = {n: nc.dram_tensor("scratch_" + n, (TOK, C), F32, kind="Internal").ap() for n in ("r", "k", "v", "a", "d", "o")}

        def place(h, per):
            return (h % per) * (H // per) + h // per

        def bc(ap, shape):
            return ap.to_broadcast(shape)

        block = ctx.enter_context(nc.Block())

        @block.sync
        def _(sp):
            def load(dst, src, name):
                sp.dma_start(dst, src).then_inc(sem(name), 16)

            def heads(ap):
                return ap.rearrange("h (k p) d -> p k h d", p=P)

            def rows(ap):
                return ap.rearrange("(k p) n -> p k n", p=P)

            load(x_rows, io["x"].rearrange("b t c -> (b t) c").rearrange("(n p) c -> p n c", p=P), "x_loaded")
            for name, n in ROWS:
                a = io[name]
                a = a.rearrange("e (k c) -> (e k) c", c=C) if name == "L1_ffn_b_in" else a.rearrange("(k c) -> k c", c=C)
                load(par_rows[ROW_AT[name]:ROW_AT[name] + n, :], a, "rows_loaded")
            for i, name in enumerate(EROWS):
                load(epar_rows[i:i + 1, :], io[name].rearrange("(a c) -> a c", a=1), "rows_loaded")

            def stage_heads(w, dst, src):
                for k in range(KC):
                    load(dst[:, k, :].rearrange("p (h d) -> p h d", h=H), src[:, k * P:(k + 1) * P, :].rearrange("h p d -> p h d"), w)

            a = "L0_xattn_a1_"
            stage_heads("a1_weights", W["a1"]["wq"], io[a + "wq"])
            stage_heads("a1_weights", W["a1"]["wk"], io[a + "wk"])
            stage_heads("a1_weights", W["a1"]["wv"], io[a + "wv"])
            load(W["a1"]["li1"], rows(io[a + "li1_w"]), "a1_weights")
            load(W["a1"]["li2"], rows(io[a + "li2_w"]), "a1_weights")
            load(W["a1"]["li3"], rows(io[a + "li3_w"]), "a1_weights")
            a = "L0_xattn_a2_"
            stage_heads("a2_weights", W["a2"]["wq"], io[a + "wq"])
            load(W["a2"]["wk"].rearrange("p (h d) -> p h d", h=H), io[a + "wk"].rearrange("h c d -> c h d"), "a2_weights")
            load(W["a2"]["wv"].rearrange("p (h d) -> p h d", h=H), io[a + "wv"].rearrange("h c d -> c h d"), "a2_weights")
            load(W["a2"]["li1"], rows(io[a + "li1_w"]), "a2_weights")
            load(W["a2"]["li2"], rows(io[a + "li2_w"]), "a2_weights")
            load(W["a2"]["li3"], rows(io[a + "li3_w"]), "a2_weights")
            for i, name in enumerate(HEADROWS):
                load(headrows[:, i * 16:(i + 1) * 16], io["L1_attn_" + name].rearrange("(h n) -> h n", h=H), "headrows_loaded")

            def load_batch(b, dst):
                load(dst[:, 0:NT - 1, :],
                     io["ctx_512"][ds(b, 1), 0:(NT - 1) * P, :].rearrange("o (p n) c -> p (o n) c", p=P), "ctx_loaded")
                load(dst[0:TAIL, NT - 1, :], io["ctx_512"][ds(b, 1), (NT - 1) * P:S_CTX, :].rearrange("o p c -> p (o c)"), "ctx_loaded")

            sp.wait_ge(sem("norm_out"), NORM["mid"] + 1)
            load(ctx_g, io["L0_xattn_a2_lny_g"].rearrange("(c a) -> c a", a=1), "ctx_affine")
            load(ctx_b, io["L0_xattn_a2_lny_b"].rearrange("(c a) -> c a", a=1), "ctx_affine")
            sp.wait_ge(sem("v_emptied"), v_done("a1_li3"))
            load(W["lin"]["wq"], rows(io["L0_attn_Wq"]), "lin_weights")
            load(W["lin"]["wk"], rows(io["L0_attn_Wk"]), "lin_weights")
            load(W["lin"]["wv"], rows(io["L0_attn_Wv"]), "lin_weights")
            load(W["lin"]["wo"], rows(io["L0_attn_Wo"]), "lin_weights")
            load(W["lin"]["wa"], rows(io["L0_attn_Wa"]), "lin_weights")
            sp.wait_ge(sem("tails_zeroed"), 1)
            load_batch(0, raw)
            with loop(sp, 1, NB) as b:
                sp.wait_ge(sem("ctx_centered"), b)
                load_batch(b, raw)

            sp.wait_ge(sem("ffn_zeroed"), 1)
            load(lin["ba"], io["L0_attn_ba"].rearrange("(a c) -> a c", a=1).to_broadcast([P, H]), "lin_bias")
            for k in range(KC):
                for n in ("q", "k", "v"):
                    load(W["ffn"]["w" + n][:, k, :].rearrange("p (h d) -> p h d", h=H)[:, :, 0:16],
                         io["L0_ffn_W" + n][k * P:(k + 1) * P, :].rearrange("p (h d) -> p h d", h=H), "ffn_weights")
            for m in range(4):
                for j in range(4):
                    hh = 4 * m + j
                    load(W["ffn"]["wo"][32 * j:32 * j + 16, m, :], io["L0_ffn_Wo"][hh * 16:(hh + 1) * 16, :], "ffn_weights")
            load(W["ffn"]["wff"], rows(io["L0_ffn_Wff"]), "ffn_weights")

            sp.wait_ge(sem("v_emptied"), v_done("lin_o"))
            load(W["x1"]["wq"], rows(io["L1_xattn_Wq"]), "x1_weights")
            load(W["x1"]["wk"], io["L1_xattn_Wk"], "x1_weights")
            load(W["x1"]["wv"], io["L1_xattn_Wv"], "x1_weights")
            load(W["x1"]["wo"], rows(io["L1_xattn_Wo"]), "x1_weights")
            sp.wait_ge(sem("ffn_added"), 1)
            for n in "rkvo":
                load(W["rw"][n + "W1"], rows(io[f"L1_attn_{n}W1"]), "rw_weights")
                for m, (e0, en) in enumerate(EC):
                    load(W["rw"][n + "W2"][0:en, m, :], io[f"L1_attn_{n}W2"][e0:e0 + en, :], "rw_weights")
            for n in "gad":
                load(W["rw"][n + "A"], rows(io[f"L1_attn_{n}A"]), "rw_weights")
                load(W["rw"][n + "B"], io[f"L1_attn_{n}B"], "rw_weights")
            load_batch(0, Y[0])
            sp.wait_ge(sem("ctx_loaded"), 32 * NB + 32)
            load_batch(1, Y[1])
            with loop(sp, 1, NB // 2) as i:
                for slot in range(2):
                    sp.wait_ge(sem("z_ready"), i * 16 + (NB * 8 + 8 * slot - 8))
                    load_batch(i * 2 + slot, Y[slot])

            def load_expert(e, slot):
                w = W["moe"][slot]
                load(w["w_in"], io["L1_ffn_W_in"][ds(e, 1), :, :].rearrange("o (k p) n -> p (o k) n", p=P), f"expert_loaded{slot}")
                load(w["w_out"], io["L1_ffn_W_out"][ds(e, 1), :, :].rearrange("o (k p) n -> p (o k) n", p=P), f"expert_loaded{slot}")

            sp.wait_ge(sem("v_emptied"), v_done("x1_out"))
            load_expert(0, 0)
            load_expert(1, 1)
            for i, n in enumerate("rkvad"):
                sp.wait_ge(sem("v_emptied"), v_done("rw_" + n + "2"))
                sp.dma_start(scratch[n].rearrange("(n p) c -> p n c", p=P),
                             rw_tm[:, i % 2, :].rearrange("p (n c) -> p n c", c=C)).then_inc(sem("scratch_written"), 16)
                sp.wait_ge(sem("scratch_written"), 16 * (i + 1))
                for b in range(NB):
                    load(hd[n][b * H:(b + 1) * H, :, :],
                         scratch[n][b * T:(b + 1) * T, :].rearrange("t (h n) -> h t n", h=H), "heads_loaded")
            sp.wait_ge(sem("rw_summed"), 1)
            for b in range(NB):
                sp.dma_start(scratch["o"][b * T:(b + 1) * T, :].rearrange("t (h n) -> h t n", h=H),
                             hd["v"][b * H:(b + 1) * H, :, :]).then_inc(sem("out_scratched"), 16)
            sp.wait_ge(sem("out_scratched"), 16 * NB)
            load(rw_tm[:, 0, :].rearrange("p (n c) -> p n c", c=C), scratch["o"].rearrange("(n p) c -> p n c", p=P), "rw_back_loaded")
            sp.wait_ge(sem("v_emptied"), v_done("rw_out"))
            load(W["gate"]["wg"], rows(io["L1_ffn_W_gate"]), "gate_weights")
            load(W["gate"]["b_out"], io["L1_ffn_b_out"], "gate_weights")
            with loop(sp, 1, NE // 2) as i:
                for slot in range(2):
                    sp.wait_ge(sem("v_emptied"), (i - 1) * (2 * PAIRS) + (v_done("moe_b") + (slot + 1) * PAIRS))
                    load_expert(i * 2 + slot, slot)
            sp.wait_ge(sem("v_emptied"), v_done("moe_y"))
            sp.dma_start(out.rearrange("b t c -> (b t) c").rearrange("(n p) c -> p n c", p=P), acc).then_inc(sem("stored"), 16)
            sp.wait_ge(sem("stored"), 16)

        @block.gpsimd
        def _(pool):
            settle = Settle(pool)
            chain = Chain(pool, sem("pool_order"))
            g = nc.gpsimd
            chain(g.memset(ident[:], 0.0))
            chain(g.affine_select(out=ident[:], in_=ident[:], compare_op=ALU.not_equal, fill=1.0, base=0,
                                  pattern=[[-1, P]], channel_multiplier=1))
            chain(g.memset(meanw[:], 1.0 / C))
            chain(g.memset(cst[:, 0:1], EPS))
            g.memset(cst[:, 1:2], 1e-6).then_inc(sem("constants"), 1)
            chain(g.memset(tri[:], 1.0))
            chain(g.memset(after_s[:], 1.0))
            chain(g.memset(upto_t[:], 1.0))
            chain(g.memset(above_q[:], 1.0))
            for b in range(2):
                q = slice(b * T, (b + 1) * T)
                chain(g.memset(tri[q, (1 - b) * T:(2 - b) * T], 0.0))
                chain(g.affine_select(out=tri[q, q], in_=tri[q, q], compare_op=ALU.is_ge, fill=0.0, base=0,
                                      pattern=[[1, T]], channel_multiplier=-1))
                chain(g.affine_select(out=after_s[q, :], in_=after_s[q, :], compare_op=ALU.is_ge, fill=0.0, base=-1,
                                      pattern=[[-1, T]], channel_multiplier=1))
                chain(g.affine_select(out=upto_t[q, :], in_=upto_t[q, :], compare_op=ALU.is_ge, fill=0.0, base=0,
                                      pattern=[[-1, T]], channel_multiplier=1))
                chain(g.affine_select(out=above_q[q, :], in_=above_q[q, :], compare_op=ALU.is_ge, fill=0.0, base=-1,
                                      pattern=[[1, T]], channel_multiplier=-1))
            chain(g.memset(rep[:], 0.0))
            rep3 = rep[:].rearrange("k (b h) -> k b h", h=H)
            g.affine_select(out=rep3, in_=rep3, compare_op=ALU.not_equal, fill=1.0, base=0,
                            pattern=[[0, NB], [-1, H]], channel_multiplier=1).then_inc(sem("masks"), 1)

            def stage_pairs(which, d):
                with loop(pool, 0, PAIRS, (chain.count, 2)) as p:
                    pool.wait_ge(sem("core_scores"), p + (which * PAIRS + 1))
                    chain(g.tensor_copy(d["QS"], d["QT"][:, :, ds(p * P, P)]))
                    chain(g.tensor_copy(d["KS"], d["KT"][:, :, ds(p * P, P)]))
                    pool.wait_ge(sem("core_o"), p + (which * PAIRS + 1))
                    src = d["V"][:, ds(p, 1), :].rearrange("p o n -> p (o n)") if which == 2 else d["V"][:, ds(p * 2, 2), :]
                    g.tensor_copy(d["VS"], src).then_inc(sem("core_staged"), 1)
                    pool.wait_ge(sem("core_staged"), p + (which * PAIRS + 1))

            pool.wait_ge(sem("s_emptied"), s_done("a1_v"))
            pool.wait_ge(sem("v_emptied"), v_done("a1_k"))
            stage_pairs(0, a1)

            full = [P, NT, CC]

            def normalize(b, slot, first):
                pool.wait_ge(sem("ctx_means"), b + 1)
                if not first:
                    pool.wait_ge(sem("z_ready"), b * 8 - 8)
                g.tensor_tensor(Y[slot], raw, bc(ctx_mean.unsqueeze(2), full), ALU.subtract).then_inc(sem("ctx_centered"), 1)
                pool.wait_ge(sem("ctx_centered"), b + 1)
                g.tensor_tensor(ctx_sq, Y[slot], Y[slot], ALU.mult).then_inc(sem("ctx_squared"), 1)
                pool.wait_ge(sem("ctx_rstds"), b + 1)
                g.tensor_tensor(Y[slot], Y[slot], bc(ctx_rstd.unsqueeze(2), full), ALU.mult).then_inc(sem("keys_made"), 1)

            pool.wait_ge(sem("norm_out"), NORM["a1_m"] + 1)
            g.memset(raw[:, NT - 1, :], 0.0).then_inc(sem("tails_zeroed"), 1)
            normalize(0, 0, True)
            normalize(1, 1, True)
            with loop(pool, 1, NB // 2) as i:
                normalize(i * 2, 0, False)
                normalize(i * 2 + 1, 1, False)
            pool.wait_ge(sem("norm_out"), NORM["lin"] + 1)
            for n in ("wq", "wk", "wv"):
                chain(g.memset(W["ffn"][n], 0.0))
            g.memset(W["ffn"]["wo"], 0.0).then_inc(sem("ffn_zeroed"), 1)
            pool.wait_ge(sem("s_emptied"), s_done("lin_v"))
            pool.wait_ge(sem("v_emptied"), v_done("lin_k"))
            stage_pairs(1, lin)
            pool.wait_ge(sem("s_emptied"), s_done("ffn_v"))
            pool.wait_ge(sem("v_emptied"), v_done("ffn_k"))
            stage_pairs(2, ffn)
            pool.wait_ge(sem("state"), 1)
            with loop(pool, 0, T, (chain.count, 2)) as t:
                v_j = hd["v"][:, ds(t, 1), :].rearrange("p o j -> p j o")
                rk_k = hd["rk"][:, ds(t, 1), :]
                d_j = hd["d"][:, ds(t, 1), :].rearrange("p o j -> p j o")
                w = hist[:, ds(t, 1), :, :].rearrange("p o j k -> p (o j) k")
                chain(g.tensor_tensor(s_new, bc(v_j, [P, 16, 16]), bc(rk_k, [P, 16, 16]), ALU.mult))
                pool.wait_ge(sem("state"), t + 1)
                chain(g.tensor_tensor(s_keep, w, bc(d_j, [P, 16, 16]), ALU.mult))
                g.tensor_tensor(s_keep, s_keep, s_new, ALU.add).then_inc(sem("state_kept"), 1)
                pool.wait_ge(sem("state_kept"), t + 1)
            pool.wait_ge(sem("norm_out"), NORM["moe"] + 1)
            g.iota(iota8, pattern=[[1, NE]], base=0, channel_multiplier=0, allow_small_or_imprecise_dtypes=True).then_inc(sem("iota"), 1)
            settle.finish(sem("constants"))

        @block.tensor
        def _(pe):
            settle = Settle(pe)
            pe.nop().then_inc(sem("core_scores"), 1)
            pe.nop().then_inc(sem("core_o"), 1)
            mm, tr = nc.tensor.matmul, nc.tensor.transpose
            sg = Groups(pe, (bank(0), bank(1)), sem("s_filled"), sem("s_emptied"), SCALAR_GROUPS)
            vg = Groups(pe, (bank(2), bank(3)), sem("v_filled"), sem("v_emptied"), VECTOR_GROUPS)

            def product(groups, name, n, lhs, rhs, k, outs=None):
                groups.layer(name)
                for i in range(n):
                    def emit(b):
                        for j in range(k):
                            left, right = lhs(i, j), rhs(i, j)
                            o = b[0:left.shape[-1], 0:right.shape[-1]]
                            ins = mm(o, lhsT=left, rhs=right, start=(j == 0), stop=(j == k - 1))
                        return ins
                    groups.fill(emit)

            def norm(name, src):
                i = NORM[name]
                for k in range(KC):
                    ins = mm(bank(4), lhsT=meanw[:], rhs=src[:, k, :], start=(k == 0), stop=(k == KC - 1))
                ins.then_inc(sem("norm_mean"), 1)
                pe.wait_ge(sem("norm_squared"), i + 1)
                for k in range(KC):
                    ins = mm(bank(5), lhsT=meanw[:], rhs=sq[:, k, :], start=(k == 0), stop=(k == KC - 1))
                ins.then_inc(sem("norm_var"), 1)

            def core(which, d, dk, dv):
                pe.wait_ge(sem("masks"), 1)
                with loop(pe, 0, PAIRS) as p:
                    done = p + which * PAIRS
                    left, right = (d["KS"], d["QS"]) if which == 2 else (d["QS"], d["KS"])
                    per = P // dk
                    pe.wait_ge(sem("core_staged"), done + 1)
                    settle()
                    for h in range(H):
                        rows = slice((h % per) * dk, (h % per + 1) * dk)
                        for b in range(2):
                            ins = mm(bank(h % per)[b * T:(b + 1) * T, (h // per) * T:(h // per + 1) * T],
                                     lhsT=left[rows, h // per, b * T:(b + 1) * T],
                                     rhs=right[rows, h // per, b * T:(b + 1) * T], start=True, stop=True)
                    ins.then_inc(sem("core_scores"), 1)
                    if which == 1:
                        pe.wait_ge(sem("lin_spread"), p + 1)
                        for i in range(2):
                            ins = mm(bank(2 + i), lhsT=tri[:],
                                     rhs=d["decay"][:, 8 * i:8 * i + 8, :].rearrange("p h s -> p (h s)"), start=True, stop=True)
                        ins.then_inc(sem("lin_sums"), 1)
                    pe.wait_ge(sem("core_probs"), done + 1)
                    settle()
                    if which < 2:
                        for h in range(H):
                            ins = tr(bank(2 + h // 4)[0:T, (h % 4) * P:(h % 4 + 1) * P], d["prob"][:, h, :], ident[:])
                        ins.then_inc(sem("core_pT"), 1)
                        pe.wait_ge(sem("core_pT_s"), done + 1)
                        pe.wait_ge(sem("core_pT_v"), done + 1)
                        settle()
                    pe.wait_ge(sem("core_stored"), done + 1)
                    settle()
                    perv = P // dv
                    for h in range(H):
                        for b in range(2):
                            q = slice(b * T, (b + 1) * T)
                            c0 = (h // perv) * P + b * T if which < 2 else b * BANK + (h // perv) * T
                            o = bank(6, 2)[(h % perv) * dv:(h % perv + 1) * dv, c0:c0 + T]
                            j = place(h, per)
                            if which == 2:
                                ins = mm(o, lhsT=d["VS"][q, h * dv:(h + 1) * dv], rhs=d["prob"][q, j, :], start=True, stop=True)
                            else:
                                ins = mm(o, lhsT=d["VS"][:, b, h * dv:(h + 1) * dv], rhs=d["probT"][:, j, q], start=True, stop=True)
                    ins.then_inc(sem("core_o"), 1)

            def cross(which, name, wk, n_chunk):
                D = n_chunk * P // H
                per = P // D
                sg.layer(name + "_wkT")
                for i in range(n_chunk // 4):
                    def emit(b):
                        for j in range(4):
                            c0 = (4 * i + j) * P
                            ins = tr(b[:, j * P:(j + 1) * P], wk[:, c0:c0 + P], ident[:])
                        return ins
                    sg.fill(emit)
                pe.wait_ge(sem("norm_out"), NORM["a2_x" if which == 0 else "x1"] + 1)
                product(sg, name + "_q", n_chunk, lambda i, j: W[name]["wq"][:, j, i * P:(i + 1) * P],
                        lambda i, j: x_xn[:, j, :], KC)
                pe.wait_ge(sem("s_emptied"), s_done(name + "_q"))

                def rows(h):
                    return slice((h % per) * D, (h % per + 1) * D)

                product(sg, name + "_qp", H, lambda h, j: x_WkT[rows(h), h // per, :],
                        lambda h, j: x_QT[rows(h), h // per, :], 1)
                pe.wait_ge(sem("s_emptied"), s_done(name + "_qp"))

                def turn_keys(b, slot, i):
                    if i == 0 and which == 0:
                        pe.wait_ge(sem("keys_made"), b + 1)
                    elif i == 0:
                        pe.wait_ge(sem("ctx_loaded"), b * 32 + (32 * NB + 32))
                    elif i >= 2:
                        pe.wait_ge(sem("keysT_" + "sv"[i % 2]), b * 2 + (which * NB * 2 + 1))
                    for j in range(min(4, NT - 4 * i)):
                        t = 4 * i + j
                        n = min(P, S_CTX - t * P)
                        ins = tr(bank(4 + i % 2)[:, j * P:j * P + n], Y[slot][0:n, t, :], ident[0:n, 0:n])
                    ins.then_inc(sem("keys_turned_" + "sv"[i % 2]), 1)

                def scores(n, k, slot, half, keys_of=None):
                    if half == 0:
                        pe.wait_ge(sem("q_staged"), n + (64 * which + 1))
                        if keys_of is not None:
                            pe.wait_ge(sem("keysT_s"), keys_of * 2 + (which * NB * 2 + 2))
                            pe.wait_ge(sem("keysT_v"), keys_of * 2 + (which * NB * 2 + 2))
                    for i in (2 * half, 2 * half + 1):
                        c = min(BANK, S_CTX - i * BANK)
                        ins = mm(bank(i)[:, 0:c], lhsT=q_stage[k], rhs=YT[slot][:, i * BANK:i * BANK + c], start=True, stop=True)
                    ins.then_inc(sem("scores" + "AB"[half]), 1)

                def turn_z(u):
                    pe.wait_ge(sem("z_scaled"), u + (64 * which + 1))
                    tr(bank(7)[:, 0:P], z_stage, ident[:]).then_inc(sem("zT_ready"), 1)

                def weigh(u, k, slot, first, nxt, keys=None):
                    g = u + 64 * which

                    def turn(i):
                        for j in range(min(4, NT - 4 * i)):
                            t = 4 * i + j
                            n = min(P, S_CTX - t * P)
                            ins = tr(bank(4 + i % 2)[0:n, j * P:(j + 1) * P], prob[k][:, t * P:t * P + n], ident[:])
                        ins.then_inc(sem("turned_" + "sv"[i // 2]), 1)

                    def add(i):
                        pe.wait_ge(sem("turned_out_" + "sv"[i // 2]), g * 2 + (i % 2 + 1))
                        for j in range(min(4, NT - 4 * i)):
                            t = 4 * i + j
                            n = min(P, S_CTX - t * P)
                            ins = mm(bank(6)[:, 0:CC], lhsT=probT[0:n, t, :], rhs=Y[slot][0:n, t, :], start=(t == 0), stop=(t == NT - 1))
                        return ins

                    pe.wait_ge(sem("expA"), g + 1)
                    if nxt:
                        scores(*nxt[0:3], 0, nxt[3])
                    turn(0)
                    pe.wait_ge(sem("expB"), g + 1)
                    if nxt:
                        scores(*nxt[0:3], 1)
                    turn(1)
                    if not first:
                        turn_z(u - 1)
                    add(0)
                    turn(2)
                    add(1)
                    turn(3)
                    add(2)
                    if keys:
                        turn_keys(*keys, 0)
                    add(3).then_inc(sem("z_ready"), 1)
                    if keys:
                        for i in (1, 2, 3):
                            turn_keys(*keys, i)

                def batch(b, slot, first, final):
                    pairs(pe, settle, first, 3, lambda h, k, f: weigh(b * 8 + h, k, slot, f, (b * 8 + h + 1, 1 - k, slot, None)))
                    weigh(b * 8 + 6, 0, slot, False, (b * 8 + 7, 1, slot, None), None if final else (b + 1, 1 - slot))
                    weigh(b * 8 + 7, 1, slot, False, None if final else (b * 8 + 8, 0, 1 - slot, b + 1))

                for i in range(4):
                    turn_keys(0, 0, i)
                scores(0, 0, 0, 0, 0)
                scores(0, 0, 0, 1)
                units(pe, batch)
                pe.wait_ge(sem("zT_stored"), 64 * which + 63)
                turn_z(8 * NB - 1)
                pe.wait_ge(sem("zT_stored"), 64 * (which + 1))
                sg.layer(name + "_o")
                for m in range(n_chunk):
                    def emit(b):
                        for j in range(per):
                            hh = m * per + j
                            ins = mm(b[j * D:(j + 1) * D, :], lhsT=W[name]["wv"][:, hh * D:(hh + 1) * D], rhs=head_rows(hh),
                                     start=True, stop=True)
                        return ins
                    sg.fill(emit)
                pe.wait_ge(sem("s_emptied"), s_done(name + "_o"))

            def mlp(name, src, hT):
                w = W[name]
                pe.wait_ge(sem("norm_out"), NORM[name + "_m"] + 1)
                product(sg, name + "_h", MC, lambda i, j: w["li2"][:, j, i * P:(i + 1) * P], lambda i, j: src[:, j, :], KC)
                pe.wait_ge(sem("s_emptied"), s_done(name + "_h"))
                product(vg, name + "_li3", KC, lambda i, j: w["li3"][:, j, i * P:(i + 1) * P], lambda i, j: hT[:, j, :], MC)

            pe.wait_ge(sem("constants"), 1)
            pe.wait_ge(sem("x_loaded"), 16)
            sg.layer("x_in")
            for k in range(KC):
                def emit(b):
                    for n in range(4):
                        ins = tr(b[:, n * P:(n + 1) * P], x_rows[:, n, k * P:(k + 1) * P], ident[:])
                    return ins
                sg.fill(emit)
            pe.wait_ge(sem("rows_loaded"), 16 * (len(ROWS) + len(EROWS)))
            sg.layer("params")

            def emit(b):
                for k in range(KC):
                    ins = tr(b[:, k * NROW:(k + 1) * NROW], par_rows[0:NROW, k * P:(k + 1) * P], ident[0:NROW, 0:NROW])
                return ins
            sg.fill(emit)
            ne = len(EROWS)
            for m, (e0, en) in enumerate(EC):
                sg.fill(lambda b: tr(b[0:en, 0:ne], epar_rows[0:ne, e0:e0 + en], ident[0:ne, 0:ne]))
            pe.wait_ge(sem("s_emptied"), s_done("params"))
            norm("x", X)
            pe.wait_ge(sem("norm_out"), NORM["x"] + 1)
            norm("h", hq)
            pe.wait_ge(sem("norm_out"), NORM["h"] + 1)
            norm("a1_x", h_in)
            pe.wait_ge(sem("norm_out"), NORM["a1_x"] + 1)
            pe.wait_ge(sem("a1_weights"), 16 * 9)
            w = W["a1"]
            product(sg, "a1_q", 4, lambda i, j: w["wq"][:, j, i * P:(i + 1) * P], lambda i, j: hq[:, j, :], KC)
            product(vg, "a1_k", 4, lambda i, j: w["wk"][:, j, i * P:(i + 1) * P], lambda i, j: hk[:, j, :], KC)
            product(sg, "a1_v", NB, lambda i, j: hk[:, j, i * T:(i + 1) * T], lambda i, j: w["wv"][:, j, :], KC)
            pe.wait_ge(sem("s_emptied"), s_done("a1_v"))
            pe.wait_ge(sem("v_emptied"), v_done("a1_k"))
            core(0, a1, 32, 32)
            pe.wait_ge(sem("core_stored"), PAIRS + 1)
            product(vg, "a1_li1", KC, lambda i, j: w["li1"][:, j, i * P:(i + 1) * P], lambda i, j: a1["OT"][:, j, :], 4)
            pe.wait_ge(sem("v_emptied"), v_done("a1_li1"))
            norm("a1_m", x_mid)
            mlp("a1", hq, a1["HT"])
            pe.wait_ge(sem("mid_ready"), 1)
            norm("mid", x_mid)
            pe.wait_ge(sem("norm_out"), NORM["mid"] + 1)
            norm("a2_x", w_in2)
            pe.wait_ge(sem("a2_weights"), 16 * 7)
            cross(0, "a2", W["a2"]["wk"], 4)
            w2 = W["a2"]
            product(vg, "a2_li1", KC, lambda i, j: w2["li1"][:, j, i * P:(i + 1) * P], lambda i, j: x_OT[:, j, :], 4)
            pe.wait_ge(sem("v_emptied"), v_done("a2_li1"))
            norm("a2_m", x_mid2)
            mlp("a2", x_m, x_HT)

            pe.wait_ge(sem("a2_added"), 1)
            norm("lin", X)
            pe.wait_ge(sem("norm_out"), NORM["lin"] + 1)
            pe.wait_ge(sem("lin_weights"), 16 * 5)
            wl = W["lin"]
            xn = lin["xn"]
            product(vg, "lin_q", 8, lambda i, j: wl["wq"][:, j, i * P:(i + 1) * P], lambda i, j: xn[:, j, :], KC)
            product(sg, "lin_v", 16, lambda i, j: xn[:, j, (i // 2) * T:(i // 2 + 1) * T],
                    lambda i, j: wl["wv"][:, j, (i % 2) * BANK:(i % 2 + 1) * BANK], KC)
            product(vg, "lin_k", 8, lambda i, j: wl["wk"][:, j, i * P:(i + 1) * P], lambda i, j: xn[:, j, :], KC)
            vg.layer("lin_a")

            def emit(b):
                for p in range(PAIRS):
                    for j in range(KC):
                        ins = mm(b[:, p * H:(p + 1) * H], lhsT=xn[:, j, p * P:(p + 1) * P], rhs=wl["wa"][:, j, :],
                                 start=(j == 0), stop=(j == KC - 1))
                return ins
            vg.fill(emit)
            pe.wait_ge(sem("s_emptied"), s_done("lin_v"))
            pe.wait_ge(sem("v_emptied"), v_done("lin_a"))
            core(1, lin, 64, 64)
            pe.wait_ge(sem("core_stored"), 2 * PAIRS + 1)
            product(vg, "lin_o", KC, lambda i, j: wl["wo"][:, j, i * P:(i + 1) * P], lambda i, j: lin["OT"][:, j, :], 8)

            pe.wait_ge(sem("v_emptied"), v_done("lin_o"))
            norm("ffn", X)
            pe.wait_ge(sem("norm_out"), NORM["ffn"] + 1)
            pe.wait_ge(sem("ffn_weights"), 16 * (3 * KC + 16 + 1))
            wf = W["ffn"]
            xf = ffn["xn"]
            product(sg, "ffn_q", 4, lambda i, j: wf["wq"][:, j, i * P:(i + 1) * P], lambda i, j: xf[:, j, :], KC)
            product(vg, "ffn_k", 4, lambda i, j: wf["wk"][:, j, i * P:(i + 1) * P], lambda i, j: xf[:, j, :], KC)
            product(sg, "ffn_v", PAIRS, lambda i, j: xf[:, j, i * P:(i + 1) * P], lambda i, j: wf["wv"][:, j, :], KC)
            pe.wait_ge(sem("s_emptied"), s_done("ffn_v"))
            pe.wait_ge(sem("v_emptied"), v_done("ffn_k"))
            core(2, ffn, 32, 32)
            pe.wait_ge(sem("core_stored"), 3 * PAIRS + 1)
            product(vg, "ffn_o", KC, lambda i, j: wf["wo"][:, j, i * P:(i + 1) * P], lambda i, j: ffn["OT"][:, j, :], 4)
            pe.wait_ge(sem("l2_squared"), 1)
            for k in range(KC):
                ins = mm(bank(4), lhsT=meanw[:], rhs=sq[:, k, :], start=(k == 0), stop=(k == KC - 1))
            ins.then_inc(sem("l2_sum"), 1)
            pe.wait_ge(sem("l2_out"), 1)
            product(vg, "ffn_f", KC, lambda i, j: wf["wff"][:, j, i * P:(i + 1) * P], lambda i, j: ffn["z"][:, j, :], KC)
            pe.wait_ge(sem("l2_squared"), 2)
            for k in range(KC):
                ins = mm(bank(4), lhsT=meanw[:], rhs=sq[:, k, :], start=(k == 0), stop=(k == KC - 1))
            ins.then_inc(sem("l2_sum"), 1)

            pe.wait_ge(sem("ffn_added"), 1)
            norm("x1", X)
            pe.wait_ge(sem("x1_weights"), 16 * 4)
            cross(1, "x1", W["x1"]["wk"], 8)
            product(vg, "x1_out", KC, lambda i, j: W["x1"]["wo"][:, j, i * P:(i + 1) * P], lambda i, j: x_OT[:, j, :], 8)

            settle.finish(sem("constants"))
            wr = W["rw"]
            pe.wait_ge(sem("v_emptied"), v_done("x1_out"))
            norm("rw", X)
            pe.wait_ge(sem("rw_weights"), 16 * (4 * 4 + 6))
            pe.wait_ge(sem("headrows_loaded"), 16 * len(HEADROWS))
            product(vg, "rw_heads", 1, lambda i, j: rep[:], lambda i, j: headrows[:], 1)
            for i, n in enumerate("rkv"):
                pe.wait_ge(sem("rw_shifted"), i + 1)
                sg.layer("rw_" + n)
                for m, (e0, en) in enumerate(EC):
                    def emit(b):
                        for j in range(KC):
                            ins = mm(b[0:en, :], lhsT=wr[n + "W1"][:, j, e0:e0 + en], rhs=rw_in[:, j, :], start=(j == 0), stop=(j == KC - 1))
                        return ins
                    sg.fill(emit)
                pe.wait_ge(sem("s_emptied"), s_done("rw_" + n))
                vg.layer("rw_" + n + "2")
                for p in range(4):
                    def emit(b):
                        for m, (e0, en) in enumerate(EC):
                            ins = mm(b[:, 0:C], lhsT=rw_HT[0:en, m, p * P:(p + 1) * P], rhs=wr[n + "W2"][0:en, m, :],
                                     start=(m == 0), stop=(m == 2))
                        return ins
                    vg.fill(emit)
            for i, n in enumerate("gad"):
                pe.wait_ge(sem("rw_shifted"), i + 4)
                sg.layer("rw_" + n)

                def emit(b):
                    for j in range(KC):
                        ins = mm(b[0:LORA, :], lhsT=wr[n + "A"][:, j, :], rhs=rw_in[:, j, :], start=(j == 0), stop=(j == KC - 1))
                    return ins
                sg.fill(emit)
                pe.wait_ge(sem("s_emptied"), s_done("rw_v") + 1 + (0, 3, 4)[i])
                if n == "g":
                    for m in range(KC):
                        sg.fill(lambda b: mm(b, lhsT=wr["gB"][:, m * P:(m + 1) * P], rhs=rw_lo, start=True, stop=True))
                else:
                    vg.layer("rw_" + n + "2")
                    for p in range(4):
                        vg.fill(lambda b: mm(b[:, 0:C], lhsT=rw_lo[:, p * P:(p + 1) * P], rhs=wr[n + "B"], start=True, stop=True))
            pe.wait_ge(sem("rw_back_loaded"), 16)
            sg.layer("rw_back")
            back = rw_tm[:, 0, :].rearrange("p (n c) -> p n c", c=C)
            for k in range(KC):
                def emit(b):
                    for n in range(4):
                        ins = tr(b[:, n * P:(n + 1) * P], back[:, n, k * P:(k + 1) * P], ident[:])
                    return ins
                sg.fill(emit)
            pe.wait_ge(sem("s_emptied"), s_done("rw_back"))
            norm("rw_o", rw_xn)
            pe.wait_ge(sem("rw_gated"), 1)
            sg.layer("rw_h")
            for m, (e0, en) in enumerate(EC):
                def emit(b):
                    for j in range(KC):
                        ins = mm(b[0:en, :], lhsT=wr["oW1"][:, j, e0:e0 + en], rhs=rw_in[:, j, :], start=(j == 0), stop=(j == KC - 1))
                    return ins
                sg.fill(emit)
            pe.wait_ge(sem("s_emptied"), s_done("rw_h"))
            vg.layer("rw_out")
            for i in range(KC):
                def emit(b):
                    for m, (e0, en) in enumerate(EC):
                        ins = mm(b, lhsT=wr["oW2"][0:en, m, i * P:(i + 1) * P], rhs=rw_HT[0:en, m, :], start=(m == 0), stop=(m == 2))
                    return ins
                vg.fill(emit)

            pe.wait_ge(sem("v_emptied"), v_done("rw_out"))
            norm("moe", X)
            pe.wait_ge(sem("norm_out"), NORM["moe"] + 1)
            pe.wait_ge(sem("gate_weights"), 32)
            vg.layer("moe_logits")

            def emit(b):
                for p in range(4):
                    for j in range(KC):
                        ins = mm(b[:, p * NE:(p + 1) * NE], lhsT=moe_xn[:, j, p * P:(p + 1) * P], rhs=W["gate"]["wg"][:, j, :],
                                 start=(j == 0), stop=(j == KC - 1))
                return ins
            vg.fill(emit)
            vg.layer("moe_xT")
            for p in range(4):
                def emit(b):
                    for k in range(KC):
                        ins = tr(b[:, k * P:(k + 1) * P], X[:, k, p * P:(p + 1) * P], ident[:])
                    return ins
                vg.fill(emit)
            pe.wait_ge(sem("combined"), 1)
            sg.layer("moe_ct")

            def emit(b):
                for p in range(4):
                    ins = tr(b[0:NE, p * P:(p + 1) * P], comb[:, p, :], ident[:])
                return ins
            sg.fill(emit)
            pe.wait_ge(sem("s_emptied"), s_done("moe_ct"))
            product(vg, "moe_b", 4, lambda i, j: combT[:, i * P:(i + 1) * P], lambda i, j: W["gate"]["b_out"], 1)
            sg.layer("moe_h")
            vg.layer("moe_y")
            with loop(pe, 0, NE // 2, (sg.count, 2 * MC), (vg.count, 2 * PAIRS)) as i:
                for slot in range(2):
                    w = W["moe"][slot]
                    pe.wait_ge(sem(f"expert_loaded{slot}"), i * 32 + 32)
                    for m in range(MC):
                        def emit(b):
                            for j in range(KC):
                                ins = mm(b, lhsT=w["w_in"][:, j, m * P:(m + 1) * P], rhs=moe_xn[:, j, :], start=(j == 0), stop=(j == KC - 1))
                            return ins
                        sg.fill(emit)
                    pe.wait_ge(sem("s_emptied"), sg.count.value)
                    for p in range(PAIRS):
                        def emit(b):
                            for m in range(MC):
                                ins = mm(b[:, 0:C], lhsT=moe_HT[slot][:, m, p * P:(p + 1) * P], rhs=w["w_out"][:, m, :],
                                         start=(m == 0), stop=(m == MC - 1))
                            return ins
                        vg.fill(emit)

        @block.scalar
        def _(act):
            settle = Settle(act)
            act.nop().then_inc(sem("core_stored"), 1)
            chain = Chain(act, sem("scalar_order"))
            f = nc.scalar.activation
            sg = Groups(act, (bank(0), bank(1)), sem("s_filled"), sem("s_emptied"), SCALAR_GROUPS)

            def norm(name, eps=0):
                i = NORM[name]
                act.wait_ge(sem("norm_centered"), i + 1)
                f(sq[:], xc[:], ACT.Square).then_inc(sem("norm_squared"), 1)
                act.wait_ge(sem("norm_squared"), i + 1)
                act.wait_ge(sem("norm_var"), i + 1)
                f(std[:], bank(5), ACT.Sqrt, bias=cst[:, eps:eps + 1]).then_inc(sem("norm_std"), 1)
                act.wait_ge(sem("norm_std"), i + 1)

            def copies(name, n, dst, func=ACT.Copy, bias=None, rows=slice(0, P), cols=slice(0, BANK)):
                sg.layer(name)
                for i in range(n):
                    b = sg.take()
                    if bias is None:
                        sg.release(f(dst(i), b[rows, cols], func))
                    else:
                        sg.release(f(dst(i), b[rows, cols], func, bias=bias(i)))

            def core(which, d, scale, nch):
                with loop(act, 0, PAIRS) as p:
                    done = p + which * PAIRS
                    if which == 1:
                        act.wait_ge(sem("lin_sums"), p + 1)
                        f(d["decay"], bank(2, 2).rearrange("p (h s) -> p h s", h=H), ACT.Exp).then_inc(sem("core_exp"), 1)
                    else:
                        act.wait_ge(sem("core_shifted"), p + (which // 2) * PAIRS + 1)
                        f(d["prob"], d["prob"], ACT.Exp, scale=scale).then_inc(sem("core_exp"), 1)
                    act.wait_ge(sem("core_exp"), done + 1)
                    if which < 2:
                        act.wait_ge(sem("core_pT"), done + 1)
                        f(d["probT"][:, 0:8, :], bank(2, 2)[0:T, :].rearrange("p (h s) -> p h s", h=8), ACT.Copy).then_inc(sem("core_pT_s"), 1)
                        act.wait_ge(sem("core_pT_s"), done + 1)
                    act.wait_ge(sem("core_o"), done + 2)
                    o = bank(6, 2)[:, 0:nch * P].rearrange("p (m t) -> p m t", t=P)
                    dst = d["OT"][:, :, ds(p * P, P)]
                    if which == 2:
                        o = bank(6, 2).rearrange("p (b m t) -> p b m t", b=2, t=T)[:, :, 0:nch, :]
                        dst = dst.rearrange("p m (b t) -> p b m t", b=2)
                    f(dst, o, ACT.Copy).then_inc(sem("core_stored"), 1)
                    act.wait_ge(sem("core_stored"), done + 2)

            def cross(which, name, n_chunk, scale):
                sg.layer(name + "_wkT")
                for i in range(n_chunk // 4):
                    b = sg.take()
                    sg.release(f(x_WkT[:, 4 * i:4 * i + 4, :], b.rearrange("p (m c) -> p m c", c=P), ACT.Copy))
                copies(name + "_q", n_chunk, lambda i: x_QT[:, i, :])
                sg.layer(name + "_qp")
                for i in range(H):
                    b = sg.take()
                    sg.release(f(head_rows(i), b.rearrange("p (b t) -> p b t", t=T), ACT.Copy))

                def affine(dst, src, name):
                    if which == 0:
                        f(dst, src, ACT.Identity, bias=ctx_b, scale=ctx_g).then_inc(sem(name), 1)
                    else:
                        f(dst, src, ACT.Copy).then_inc(sem(name), 1)

                def keys_out(b, slot):
                    for i in (0, 2):
                        at = b * 2 + (which * NB * 2 + i // 2 + 1)
                        act.wait_ge(sem("keys_turned_s"), at)
                        affine(YT[slot][:, i * BANK:(i + 1) * BANK], bank(4), "keysT_s")
                        act.wait_ge(sem("keysT_s"), at)

                def stage(n, k):
                    f(q_stage[k], unit_rows(n), ACT.Copy).then_inc(sem("q_staged"), 1)
                    act.wait_ge(sem("q_staged"), n + (64 * which + 1))

                def spread(n, k):
                    act.wait_ge(sem("biased"), n + (64 * which + 1))
                    for half in range(2):
                        lo, hi = (0, 2 * BANK) if half == 0 else (2 * BANK, S_CTX)
                        name = "exp" + "AB"[half]
                        f(prob[k][:, lo:hi], bank(0, 4)[:, lo:hi], ACT.Exp, bias=u_bias[k], scale=scale,
                          accum_out=u_sum[k][:, half:half + 1]).then_inc(sem(name), 1)
                        act.wait_ge(sem(name), n + (64 * which + 1))

                def z_out(u):
                    act.wait_ge(sem("zT_ready"), u + (64 * which + 1))
                    settle()
                    affine(unit_rows(u), bank(7)[:, 0:P], "zT_stored")
                    act.wait_ge(sem("zT_stored"), u + (64 * which + 1))

                def turned(u, k, first, nxt, after):
                    for i in range(2):
                        at = u * 2 + (128 * which + i + 1)
                        act.wait_ge(sem("turned_s"), at)
                        f(probT[:, 4 * i:4 * i + 4, :], bank(4 + i).rearrange("p (n c) -> p n c", c=P), ACT.Copy).then_inc(sem("turned_out_s"), 1)
                        act.wait_ge(sem("turned_out_s"), at)
                        if i == 0 and after:
                            stage(u + 2, k)
                    if not first:
                        z_out(u - 1)
                    if nxt:
                        spread(u + 1, 1 - k)

                def batch(b, slot, first, final):
                    pairs(act, settle, first, 2, lambda h, k, f: turned(b * 8 + h, k, f, True, True))
                    if which == 0 and not final:
                        keys_std(b + 1)
                    for h in range(4, 8):
                        turned(b * 8 + h, h % 2, False, h < 7 or not final, h < 6 or not final)
                        if h == 6 and not final:
                            keys_out(b + 1, 1 - slot)

                def keys_std(b):
                    act.wait_ge(sem("ctx_vars"), b + 1)
                    f(ctx_std, ctx_var, ACT.Sqrt, bias=cst[:, 0:1], scale=1.0 / CC).then_inc(sem("ctx_stds"), 1)
                    act.wait_ge(sem("ctx_stds"), b + 1)

                if which == 0:
                    keys_std(0)
                    act.wait_ge(sem("ctx_affine"), 32)
                keys_out(0, 0)
                stage(0, 0)
                stage(1, 1)
                spread(0, 0)
                units(act, batch)
                z_out(8 * NB - 1)
                copies(name + "_o", n_chunk, lambda i: x_OT[:, i, :])

            copies("x_in", 2, lambda i: X[:, i, :])
            sg.layer("params")
            b = sg.take()
            sg.release(f(par[:], b[:, 0:KC * NROW], ACT.Copy))
            ne = len(EROWS)
            for m, (e0, en) in enumerate(EC):
                b = sg.take()
                sg.release(f(epar[0:en, m * ne:(m + 1) * ne], b[0:en, 0:ne], ACT.Copy))
            act.wait_ge(sem("constants"), 1)
            norm("x")
            norm("h")
            norm("a1_x")
            copies("a1_q", 4, lambda i: a1["QT"][:, i, :])
            copies("a1_v", NB, lambda i: a1["V"][:, i, :], rows=slice(0, T))
            core(0, a1, 32 ** -0.5, 4)
            norm("a1_m")
            copies("a1_h", MC, lambda i: a1["HT"][:, i, :], ACT.Gelu, lambda i: col("L0_xattn_a1_li2_b", i))
            norm("mid")
            norm("a2_x")
            cross(0, "a2", 4, 32 ** -0.5)
            norm("a2_m")
            copies("a2_h", MC, lambda i: x_HT[:, i, :], ACT.Gelu, lambda i: col("L0_xattn_a2_li2_b", i))
            norm("lin")

            def elus(which, n):
                for i in range(n):
                    act.wait_ge(sem("elu_clamped"), which * 8 + i + 1)
                    f(elu[:, i % 2, :], elu[:, i % 2, :], ACT.Exp).then_inc(sem("elu_exp"), 1)
                    act.wait_ge(sem("elu_exp"), which * 8 + i + 1)

            elus(0, 8)
            copies("lin_v", 16, lambda i: lin["V"][:, i // 2, (i % 2) * BANK:(i % 2 + 1) * BANK], rows=slice(0, T))
            elus(1, 8)
            act.wait_ge(sem("lin_abs"), 1)
            chain(f(lin["la"], lin["la"], ACT.Exp, scale=-1.0))
            f(lin["la"], lin["la"], ACT.Ln, bias=1.0).then_inc(sem("lin_log"), 1)
            act.wait_ge(sem("lin_log"), 1)
            core(1, lin, 1.0, 8)
            norm("ffn")
            copies("ffn_q", 4, lambda i: ffn["QT"][:, i, :])
            copies("ffn_v", PAIRS, lambda i: ffn["V"][:, i, :])
            core(2, ffn, 1.0 / 16, 4)
            for i in range(2):
                act.wait_ge(sem("v_emptied"), v_done(("ffn_o", "ffn_f")[i]))
                f(sq[:], ffn[("z", "z2")[i]], ACT.Square).then_inc(sem("l2_squared"), 1)
                act.wait_ge(sem("l2_squared"), i + 1)
                act.wait_ge(sem("l2_sum"), i + 1)
                f(std[:], bank(4), ACT.Sqrt, scale=float(C)).then_inc(sem("l2_norm"), 1)
                act.wait_ge(sem("l2_norm"), i + 1)
            act.wait_ge(sem("l2_out"), 2)
            f(ffn["z2"], ffn["z2"], ACT.Gelu).then_inc(sem("ffn_gelu"), 1)
            act.wait_ge(sem("ffn_gelu"), 1)
            norm("x1")
            cross(1, "x1", 8, 64 ** -0.5)
            settle.finish(sem("constants"))
            norm("rw")
            for i, n in enumerate("rkv"):
                sg.layer("rw_" + n)
                for m, (e0, en) in enumerate(EC):
                    b = sg.take()
                    j = m * ne + EROWS.index("L1_attn_" + n + "b1")
                    if i and m == 0:
                        act.wait_ge(sem("v_filled"), v_done("rw_" + "rkv"[i - 1] + "2"))
                    sg.release(f(rw_HT[0:en, m, :], b[0:en, :], ACT.Gelu, bias=epar[0:en, j:j + 1]))
            copies("rw_g", 1, lambda i: rw_lo, rows=slice(0, LORA))
            for m in range(KC):
                b = sg.take()
                sg.release(f(gate[:, m, :], b, ACT.Sigmoid))
            for n in "ad":
                if n == "d":
                    act.wait_ge(sem("v_filled"), v_done("rw_a2"))
                copies("rw_" + n, 1, lambda i: rw_lo, rows=slice(0, LORA))
            act.wait_ge(sem("heads_biased"), 1)
            f(hd["a"], hd["a"], ACT.Sigmoid).then_inc(sem("heads_act"), 1)
            chain(f(hd["d"], hd["d"], ACT.Tanh))
            chain(f(hd["d"], hd["d"], ACT.Sigmoid))
            act.wait_ge(sem("heads_biased"), 2)
            f(nrm, nrm, ACT.Sqrt).then_inc(sem("heads_act"), 1)
            f(hd["d"], hd["d"], ACT.Exp, scale=-DECAY_C).then_inc(sem("heads_act"), 1)
            act.wait_ge(sem("heads_act"), 3)
            copies("rw_back", KC, lambda i: rw_xn[:, i, :])
            norm("rw_o", 1)
            sg.layer("rw_h")
            for m, (e0, en) in enumerate(EC):
                b = sg.take()
                j = m * ne + EROWS.index("L1_attn_ob1")
                sg.release(f(rw_HT[0:en, m, :], b[0:en, :], ACT.Gelu, bias=epar[0:en, j:j + 1]))
            norm("moe")
            act.wait_ge(sem("top_gap"), 1)
            f(dlt[:, 0:4], dlt[:, 0:4], ACT.Exp).then_inc(sem("top_exp"), 1)
            act.wait_ge(sem("top_exp"), 1)
            copies("moe_ct", 1, lambda i: combT, rows=slice(0, NE))
            sg.layer("moe_h")
            with loop(act, 0, NE // 2, (sg.count, 2 * MC)) as i:
                for slot in range(2):
                    act.wait_ge(sem("v_filled"), i * (2 * PAIRS) + (v_done("moe_b") + (slot - 2) * PAIRS + PAIRS))
                    for m in range(MC):
                        b = sg.take()
                        at = (m % KC) * NROW + ROW_AT["L1_ffn_b_in"] + m // KC + 4 * slot
                        sg.release(f(moe_HT[slot][:, m, :], b, ACT.Gelu, bias=par[:, ds(i * 8 + at, 1)]))

        @block.vector
        def _(dve):
            settle = Settle(dve)
            chain = Chain(dve, sem("vector_order"))
            v = nc.vector
            vg = Groups(dve, (bank(2), bank(3)), sem("v_filled"), sem("v_emptied"), VECTOR_GROUPS)

            def signal(ins, name, value=1):
                ins.then_inc(sem(name), 1)
                dve.wait_ge(sem(name), value)

            def norm(name, src, outs):
                i = NORM[name]
                dve.wait_ge(sem("norm_mean"), i + 1)
                chain(v.tensor_tensor(xc[:, 0, :], src[:, 0, :], bank(4), ALU.subtract))
                signal(v.tensor_tensor(xc[:, 1, :], src[:, 1, :], bank(4), ALU.subtract), "norm_centered", i + 1)
                dve.wait_ge(sem("norm_std"), i + 1)
                chain(v.reciprocal(rstd[:], std[:]))
                for n, (dst, g, b) in enumerate(outs):
                    for k in range(KC):
                        last_one = n == len(outs) - 1 and k == KC - 1
                        ins = v.tensor_tensor(dst[:, k, :], xc[:, k, :], rstd[:], ALU.mult)
                        if g is not None:
                            chain(ins)
                            ins = v.tensor_scalar(dst[:, k, :], dst[:, k, :], col(g, k), col(b, k), ALU.mult, ALU.add)
                        if last_one:
                            signal(ins, "norm_out", i + 1)
                        else:
                            chain(ins)

            def add_into(name, dst, bias, extra):
                vg.layer(name)
                for k in range(KC):
                    b = vg.take()
                    if bias is None:
                        vg.release(v.tensor_tensor(dst[:, k, :], b, extra[:, k, :], ALU.add))
                    else:
                        vg.release(v.scalar_tensor_tensor(out=dst[:, k, :], in0=b, scalar=col(bias, k), in1=extra[:, k, :],
                                                          op0=ALU.add, op1=ALU.add))

            def core(which, d):
                per, nch = (4, 4) if which != 1 else (2, 8)
                full = [P, per, nch, T]
                S = bank(0, per).rearrange("p (g c s) -> p g c s", g=per, s=T)[:, :, 0:nch, :]

                def heads(ap):
                    return ap.rearrange("p (g c) s -> p g c s", g=per)

                def spread(ap):
                    return bc(ap.rearrange("p (g c) -> p g c", g=per).unsqueeze(3), full)

                def over(mask):
                    return bc(mask[:].unsqueeze(1), [P, H, T])

                prob = d["prob"]
                steps = {0: 4, 1: 6, 2: 3}[which]
                with loop(dve, 0, PAIRS, (chain.count, steps)) as p:
                    done = p + which * PAIRS
                    if which == 1:
                        la = d["la"][:, ds(p, 1), :].rearrange("p o (c g) -> p g (o c)", g=per).unsqueeze(3)
                        for g in range(per):
                            ins = v.tensor_tensor(heads(d["decay"])[:, g, :, :], bc(la[:, g, :, :], [P, nch, T]),
                                                  bc(after_s[:].unsqueeze(1), [P, nch, T]), ALU.mult)
                            if g < per - 1:
                                chain(ins)
                        signal(ins, "lin_spread", p + 1)
                        dve.wait_ge(sem("core_scores"), done + 2)
                        dve.wait_ge(sem("core_exp"), done + 1)
                        chain(v.tensor_tensor(heads(prob), S, heads(d["decay"]), ALU.mult))
                        chain(v.tensor_tensor(prob, prob, over(upto_t), ALU.mult))
                        chain(v.tensor_reduce(sum16, prob, AX, ALU.add))
                        chain(v.tensor_scalar(sum16, sum16, 1e-6, None, ALU.add))
                        chain(v.reciprocal(rec16, sum16))
                        signal(v.tensor_tensor(heads(prob), heads(prob), spread(rec16), ALU.mult), "core_probs", done + 1)
                    else:
                        dve.wait_ge(sem("core_scores"), done + 2)
                        chain(v.tensor_reduce(mx16, S, AX, ALU.max))
                        signal(v.tensor_tensor(heads(prob), S, spread(mx16), ALU.subtract), "core_shifted",
                               p + ((which // 2) * PAIRS + 1))
                        dve.wait_ge(sem("core_exp"), done + 1)
                        chain(v.tensor_reduce(sum16, prob, AX, ALU.add))
                        chain(v.reciprocal(rec16, sum16))
                        ins = v.tensor_tensor(heads(prob), heads(prob), spread(rec16), ALU.mult)
                        if which == 0:
                            chain(ins)
                            ins = v.tensor_tensor(prob, prob, over(above_q), ALU.mult)
                        signal(ins, "core_probs", done + 1)
                    if which < 2:
                        dve.wait_ge(sem("core_pT"), done + 1)
                        signal(v.tensor_copy(d["probT"][:, 8:16, :], bank(4, 2)[0:T, :].rearrange("p (h s) -> p h s", h=8)),
                               "core_pT_v", done + 1)

            def cross(which, scale):
                full = [P, NT, CC]

                def keys_mean(b):
                    dve.wait_ge(sem("ctx_loaded"), b * 32 + 32)
                    signal(v.tensor_reduce(ctx_sum, raw, AX, ALU.add), "ctx_sums", b + 1)
                    signal(v.tensor_scalar(ctx_mean, ctx_sum, 1.0 / CC, None, ALU.mult), "ctx_means", b + 1)

                def keys_rstd(b):
                    dve.wait_ge(sem("ctx_squared"), b + 1)
                    signal(v.tensor_reduce(ctx_var, ctx_sq, AX, ALU.add), "ctx_vars", b + 1)
                    dve.wait_ge(sem("ctx_stds"), b + 1)
                    signal(v.reciprocal(ctx_rstd, ctx_std), "ctx_rstds", b + 1)

                def keys_out(b, slot):
                    for i, (lo, hi) in ((1, (BANK, 2 * BANK)), (3, (3 * BANK, S_CTX))):
                        at = b * 2 + (which * NB * 2 + i // 2 + 1)
                        dve.wait_ge(sem("keys_turned_v"), at)
                        src = bank(5)[:, 0:hi - lo]
                        if which == 0:
                            ins = v.tensor_scalar(YT[slot][:, lo:hi], src, ctx_g, ctx_b, ALU.mult, ALU.add)
                        else:
                            ins = v.tensor_copy(YT[slot][:, lo:hi], src)
                        signal(ins, "keysT_v", at)

                def peak(n, k):
                    g = n + 64 * which
                    for half in range(2):
                        dve.wait_ge(sem("scores" + "AB"[half]), g + 1)
                        lo, hi = (0, 2 * BANK) if half == 0 else (2 * BANK, S_CTX)
                        signal(v.tensor_reduce(u_max[:, half:half + 1], bank(0, 4)[:, lo:hi], AX, ALU.max), "peak" + "AB"[half], g + 1)
                    signal(v.tensor_scalar(u_bias[k], u_max[:, 0:1], u_max[:, 1:2], -scale, ALU.max, ALU.mult), "biased", g + 1)

                def weigh(u, k, nxt):
                    if nxt:
                        peak(u + 1, 1 - k)
                    for i in (2, 3):
                        n, tiles = (P, 4) if i == 2 else (TAIL, 1)
                        at = u * 2 + (128 * which + i - 1)
                        dve.wait_ge(sem("turned_v"), at)
                        signal(v.tensor_copy(probT[0:n, 4 * i:4 * i + tiles, :],
                                             bank(2 + i)[0:n, 0:tiles * P].rearrange("p (n c) -> p n c", c=P)),
                               "turned_out_v", at)
                    g = u + (64 * which + 1)
                    signal(v.tensor_tensor(u_total, u_sum[k][:, 0:1], u_sum[k][:, 1:2], ALU.add), "summed", g)
                    signal(v.reciprocal(u_rec, u_total), "sum_inverted", g)
                    dve.wait_ge(sem("z_ready"), g)
                    signal(v.tensor_scalar(z_stage, bank(6)[:, 0:CC], u_rec, None, ALU.mult), "z_scaled", g)

                def batch(b, slot, first, final):
                    if which == 0 and not final:
                        keys_mean(b + 1)
                    pairs(dve, settle, first, 2, lambda h, k, f: weigh(b * 8 + h, k, True))
                    if which == 0 and not final:
                        keys_rstd(b + 1)
                    for h in range(4, 8):
                        weigh(b * 8 + h, h % 2, h < 7 or not final)
                        if h == 6 and not final:
                            keys_out(b + 1, 1 - slot)

                if which == 0:
                    keys_mean(0)
                    keys_rstd(0)
                keys_out(0, 0)
                peak(0, 0)
                units(dve, batch)

            a = "L0_xattn_"
            norm("x", X, [(hq, None, None)])
            norm("h", hq, [(h_in, a + "ln1_g", a + "ln1_b")])
            norm("a1_x", h_in, [(hq, a + "a1_lnx_g", a + "a1_lnx_b"), (hk, a + "a1_lny_g", a + "a1_lny_b")])
            vg.layer("a1_k")
            for i in range(4):
                b = vg.take()
                vg.release(v.tensor_copy(a1["KT"][:, i, :], b))
            dve.wait_ge(sem("masks"), 1)
            core(0, a1)
            add_into("a1_li1", x_mid, a + "a1_li1_b", h_in)
            norm("a1_m", x_mid, [(hq, a + "a1_ln3_g", a + "a1_ln3_b")])
            add_into("a1_li3", x_mid, a + "a1_li3_b", x_mid)
            signal(v.tensor_tensor(x_mid, x_mid, h_in, ALU.add), "mid_ready")
            norm("mid", x_mid, [(w_in2, a + "ln2_g", a + "ln2_b")])
            norm("a2_x", w_in2, [(x_xn, a + "a2_lnx_g", a + "a2_lnx_b")])
            dve.wait_ge(sem("ctx_affine"), 32)
            cross(0, 32 ** -0.5)
            add_into("a2_li1", x_mid2, a + "a2_li1_b", w_in2)
            norm("a2_m", x_mid2, [(x_m, a + "a2_ln3_g", a + "a2_ln3_b")])
            add_into("a2_li3", x_mid2, a + "a2_li3_b", x_mid2)
            chain(v.tensor_tensor(x_mid2, x_mid2, w_in2, ALU.add))
            signal(v.tensor_tensor(X[:], X[:], x_mid2, ALU.add), "a2_added")

            norm("lin", X, [(lin["xn"], None, None)])

            def elus(which, name, dst):
                vg.layer(name)
                banks = {}

                def clamp(i):
                    banks[i] = vg.take()
                    signal(v.tensor_scalar(elu[:, i % 2, :], banks[i], 0.0, None, ALU.min), "elu_clamped", which * 8 + i + 1)

                clamp(0)
                for i in range(8):
                    if i < 7:
                        clamp(i + 1)
                    dve.wait_ge(sem("elu_exp"), which * 8 + i + 1)
                    vg.release(v.scalar_tensor_tensor(out=dst[:, i, :], in0=banks[i], scalar=0.0, in1=elu[:, i % 2, :],
                                                      op0=ALU.max, op1=ALU.add), int(i < 7))

            elus(0, "lin_q", lin["QT"])
            elus(1, "lin_k", lin["KT"])
            vg.layer("lin_a")
            dve.wait_ge(sem("lin_bias"), 16)
            b = vg.take()
            vg.release(v.tensor_tensor(lin["z"], b[:, 0:PAIRS * H].rearrange("p (n h) -> p n h", h=H),
                                       bc(lin["ba"].unsqueeze(1), [P, PAIRS, H]), ALU.add))
            chain(v.tensor_scalar(lin["z"], lin["z"], 2.0, None, ALU.add))
            signal(v.scalar_tensor_tensor(out=lin["la"], in0=lin["z"], scalar=-1.0, in1=lin["z"], op0=ALU.mult, op1=ALU.max), "lin_abs")
            dve.wait_ge(sem("lin_log"), 1)
            chain(v.scalar_tensor_tensor(out=lin["la"], in0=lin["z"], scalar=0.0, in1=lin["la"], op0=ALU.min, op1=ALU.subtract))
            core(1, lin)
            add_into("lin_o", X, None, X)

            norm("ffn", X, [(ffn["xn"], None, None)])
            vg.layer("ffn_k")
            for i in range(4):
                b = vg.take()
                vg.release(v.tensor_copy(ffn["KT"][:, i, :], b))
            core(2, ffn)
            for i in range(2):
                z = ffn[("z", "z2")[i]]
                vg.layer(("ffn_o", "ffn_f")[i])
                for k in range(KC):
                    b = vg.take()
                    vg.release(v.tensor_copy(z[:, k, :], b))
                dve.wait_ge(sem("l2_norm"), i + 1)
                chain(v.tensor_scalar(std[:], std[:], 1e-12, None, ALU.max))
                chain(v.reciprocal(rstd[:], std[:]))
                chain(v.tensor_tensor(z[:, 0, :], z[:, 0, :], rstd[:], ALU.mult))
                signal(v.tensor_tensor(z[:, 1, :], z[:, 1, :], rstd[:], ALU.mult), "l2_out", i + 1)
            dve.wait_ge(sem("ffn_gelu"), 1)
            signal(v.tensor_tensor(X[:], X[:], ffn["z2"], ALU.add), "ffn_added")

            norm("x1", X, [(x_xn, None, None)])
            cross(1, 64 ** -0.5)
            add_into("x1_out", X, "L1_xattn_bo", X)

            settle.finish(sem("constants"))
            norm("rw", X, [(rw_xn, None, None)])
            vg.layer("rw_heads")
            b = vg.take()
            vg.release(v.tensor_copy(headpar[:].rearrange("p i n -> p (i n)"), b[:, 0:P]))
            HP = {n: bc(headpar[:, i:i + 1, :], [P, T, 16]) for i, n in enumerate(HEADROWS)}

            def shift(i):
                n = "rkvgad"[i]
                if i:
                    dve.wait_ge(sem("s_filled"), s_done("rw_" + "rkvgad"[i - 1]) - (2 if i == 4 else 0))
                mu = "L1_attn_mu_" + n
                chain(v.tensor_scalar(rw_in[:, 0, :], rw_xn[:, 0, :], col(mu, 0), None, ALU.add))
                signal(v.tensor_scalar(rw_in[:, 1, :], rw_xn[:, 1, :], col(mu, 1), None, ALU.add), "rw_shifted", i + 1)

            def latents_out(i):
                n = "rkvad"[i]
                if i >= 2:
                    dve.wait_ge(sem("scratch_written"), 16 * (i - 1))
                vg.layer("rw_" + n + "2")
                for p in range(4):
                    b = vg.take()
                    vg.release(v.tensor_copy(rw_tm[:, i % 2, p * C:(p + 1) * C], b[:, 0:C]))

            shift(0)
            shift(1)
            latents_out(0)
            shift(2)
            latents_out(1)
            shift(3)
            latents_out(2)
            shift(4)
            shift(5)
            latents_out(3)
            latents_out(4)
            dve.wait_ge(sem("heads_loaded"), 16 * NB * 5)
            chain(v.tensor_tensor(hd["a"], hd["a"], HP["ab"], ALU.add))
            signal(v.tensor_tensor(hd["d"], hd["d"], HP["db"], ALU.add), "heads_biased", 1)
            for n in "rkv":
                chain(v.tensor_tensor(hd[n], hd[n], HP[n + "b2"], ALU.add))
            chain(v.tensor_tensor(hd["kn"], hd["k"], HP["rem_mult"], ALU.mult))
            chain(v.tensor_tensor(hd["akn"], hd["kn"], hd["kn"], ALU.mult))
            signal(v.tensor_reduce(nrm, hd["akn"], AX, ALU.add), "heads_biased", 2)
            dve.wait_ge(sem("heads_act"), 3)
            chain(v.tensor_scalar(nrm, nrm, 1e-12, None, ALU.max))
            chain(v.reciprocal(nrm2, nrm))
            t16 = [P, T, 16]
            chain(v.tensor_tensor(hd["kn"], hd["kn"], bc(nrm2.unsqueeze(2), t16), ALU.mult))
            chain(v.scalar_tensor_tensor(out=hd["akn"], in0=hd["a"], scalar=-1.0, in1=HP["iclr_mix"], op0=ALU.add, op1=ALU.mult))
            chain(v.scalar_tensor_tensor(out=hd["rk"], in0=hd["akn"], scalar=1.0, in1=hd["k"], op0=ALU.add, op1=ALU.mult))
            chain(v.tensor_tensor(hd["akn"], hd["a"], hd["kn"], ALU.mult))
            chain(v.tensor_tensor(hd["bonus"], hd["r"], hd["rk"], ALU.mult))
            chain(v.tensor_reduce(nrm, hd["bonus"], AX, ALU.add))
            chain(v.tensor_scalar(nrm, nrm, 0.2, None, ALU.mult))
            chain(v.tensor_tensor(hd["bonus"], hd["v"], HP["bonus_mult"], ALU.mult))
            chain(v.tensor_tensor(hd["bonus"], hd["bonus"], bc(nrm.unsqueeze(2), t16), ALU.mult))
            signal(v.memset(hist[:, 0, :, :], 0.0), "state", 1)
            jk = [P, 16, 16]
            with loop(dve, 0, T, (chain.count, 3)) as t:
                wT = hist[:, ds(t, 1), :, :].rearrange("p o j k -> p (o k) j")
                chain(v.tensor_tensor(s_tmp, wT, bc(hd["akn"][:, ds(t, 1), :], jk), ALU.mult))
                chain(v.tensor_reduce(s_row, s_tmp, AX, ALU.add))
                chain(v.tensor_tensor(s_tmp, bc(hd["kn"][:, ds(t, 1), :].rearrange("p o j -> p j o"), jk),
                                      bc(s_row.unsqueeze(1), jk), ALU.mult))
                dve.wait_ge(sem("state_kept"), t + 1)
                signal(v.tensor_tensor(hist[:, ds(t + 1, 1), :, :].rearrange("p o j k -> p (o j) k"), s_keep, s_tmp, ALU.subtract),
                       "state", t + 2)
            chain(v.tensor_tensor(hist[:, 1:T + 1, :, :], hist[:, 1:T + 1, :, :], bc(hd["r"].unsqueeze(2), [P, T, 16, 16]), ALU.mult))
            chain(v.tensor_reduce(hd["v"], hist[:, 1:T + 1, :, :], AX, ALU.add))
            signal(v.tensor_tensor(hd["v"], hd["v"], hd["bonus"], ALU.add), "rw_summed")
            norm("rw_o", rw_xn, [(rw_in, "L1_attn_ln_g", "L1_attn_ln_b")])
            signal(v.tensor_tensor(rw_in, rw_in, gate, ALU.mult), "rw_gated")
            add_into("rw_out", X, "L1_attn_ob2", X)

            norm("moe", X, [(moe_xn, None, None)])
            vg.layer("moe_logits")
            b = vg.take()
            vg.release(v.tensor_copy(logits, b[:, 0:4 * NE].rearrange("p (n e) -> p n e", e=NE)))
            vg.layer("moe_xT")
            for p in range(4):
                b = vg.take()
                vg.release(v.tensor_copy(acc[:, p, :], b[:, 0:C]))
            for p in range(4):
                chain(v.max(top8[:, p, :], logits[:, p, :]))
                chain(v.max_index(topi[:, p, :], top8[:, p, :], logits[:, p, :]))
            chain(v.tensor_copy(topf, topi[:]))
            signal(v.tensor_tensor(dlt[:, 0:4].unsqueeze(2), top8[:, :, 1:2], top8[:, :, 0:1], ALU.subtract), "top_gap")
            dve.wait_ge(sem("top_exp"), 1)
            chain(v.tensor_scalar(dlt[:, 4:8], dlt[:, 0:4], 1.0, None, ALU.add))
            chain(v.reciprocal(dlt[:, 4:8], dlt[:, 4:8]))
            chain(v.tensor_tensor(dlt[:, 0:4], dlt[:, 0:4], dlt[:, 4:8], ALU.mult))
            dve.wait_ge(sem("iota"), 1)
            for p in range(4):
                chain(v.tensor_scalar(hot, iota8, topf[:, p, 0:1], dlt[:, 4 + p:5 + p], ALU.is_equal, ALU.mult))
                chain(v.tensor_scalar(hot2, iota8, topf[:, p, 1:2], dlt[:, p:p + 1], ALU.is_equal, ALU.mult))
                ins = v.tensor_tensor(comb[:, p, :], hot, hot2, ALU.add)
                if p < 3:
                    chain(ins)
                else:
                    signal(ins, "combined")
            vg.layer("moe_b")
            for p in range(4):
                b = vg.take()
                vg.release(v.tensor_tensor(acc[:, p, :], b[:, 0:C], acc[:, p, :], ALU.add))
            vg.layer("moe_y")
            with loop(dve, 0, NE // 2, (vg.count, 2 * PAIRS)) as i:
                for slot in range(2):
                    for p in range(PAIRS):
                        b = vg.take()
                        vg.release(v.scalar_tensor_tensor(out=acc[:, p, :], in0=b[:, 0:C], scalar=comb[:, p, ds(i * 2 + slot, 1)],
                                                          in1=acc[:, p, :], op0=ALU.mult, op1=ALU.add))


_UNUSED = ("L1_attn_keys", "L1_attn_values", "L1_attn_attn_mask")
_OUT = (NB, T, C)


def kernel(**inputs):
    import numpy as _np
    import concourse.bacc as _bacc
    from concourse.bass_utils import run_bass_kernel_spmd as _run

    nc = _bacc.Bacc("TRN2", target_bir_lowering=False, num_devices=1)
    arrays, io = {}, {}
    for name, a in inputs.items():
        if name in _UNUSED:
            continue
        a = _np.ascontiguousarray(a)
        arrays[f"in_{name}"] = a
        io[name] = nc.dram_tensor(f"in_{name}", a.shape, mybir.dt.from_np(a.dtype), kind="ExternalInput").ap()
    out = nc.dram_tensor("out", _OUT, F32, kind="ExternalOutput").ap()
    perceiver_kernel(nc, io, out)
    r = _run(nc, [arrays], core_ids=[0])
    return r.results[0]["out"]
```

```python
from contextlib import ExitStack, contextmanager

import concourse.bass as bass
from concourse import mybir

F32 = mybir.dt.float32
F32R = mybir.dt.float32r
U32 = mybir.dt.uint32
ALU = mybir.AluOpType
ACT = mybir.ActivationFunctionType
AX = mybir.AxisListType.X
ds = bass.ds

P = 128
NB, T, C = 8, 64, 256
TOK = NB * T
KC = C // P
PAIRS = NB // 2
H = 16
S_CTX, CC = 1601, 128
S_EVEN = S_CTX + S_CTX % 2
NT = -(-S_CTX // P)
TAIL = S_CTX - (NT - 1) * P
HID = 1024
MC = HID // P
E1 = 307
EC = [(0, 128), (128, 128), (256, E1 - 256)]
LORA = 64
RW_SUMS = ((0, 32), (32, 56))
STEPS = 8
NE = 8
BANK = 512
DECAY_C = 0.7408182206817179
EPS = 1e-5

ROWS = [("L0_xattn_" + n, 1) for n in (
    "ln1_g", "ln1_b", "ln2_g", "ln2_b", "a1_li1_b", "a1_lnx_g", "a1_lnx_b", "a1_lny_g", "a1_lny_b", "a1_ln3_g",
    "a1_ln3_b", "a1_li3_b", "a2_li1_b", "a2_lnx_g", "a2_lnx_b", "a2_ln3_g", "a2_ln3_b", "a2_li3_b")]
ROWS += [("L0_xattn_a1_li2_b", 4), ("L0_xattn_a2_li2_b", 4), ("L1_xattn_bo", 1)]
ROWS += [("L1_attn_" + n, 1) for n in ("mu_r", "mu_k", "mu_v", "mu_g", "mu_a", "mu_d", "ob2", "ln_g", "ln_b")]
ROWS += [("L1_ffn_b_in", 32)]
NROW = sum(n for _, n in ROWS)
ROW_AT = {name: sum(n for _, n in ROWS[:i]) for i, (name, _) in enumerate(ROWS)}
EROWS = ["L1_attn_rb1", "L1_attn_kb1", "L1_attn_vb1", "L1_attn_ob1"]
HEADROWS = ["rem_mult", "iclr_mix", "bonus_mult", "rb2", "kb2", "vb2", "ab", "db"]

NORMS = ["x", "a1_x", "a1_m", "mid", "a2_x", "a2_m", "lin", "ffn", "x1", "rw", "rw_o", "moe"]
NORM = {n: i for i, n in enumerate(NORMS)}

SCALAR_GROUPS = [("x_in", 2), ("params", 4), ("a1_q", 4), ("a1_v", 8), ("a1_h", 8),
                 ("a2_wkT", 1), ("a2_q", 4), ("a2_qp", 16), ("a2_o", 4), ("a2_h", 8),
                 ("lin_v", 16), ("ffn_q", 4), ("ffn_v", 4),
                 ("x1_wkT", 2), ("x1_q", 8), ("x1_qp", 16), ("x1_o", 8),
                 ("rw_r", 3), ("rw_k", 3), ("rw_v", 3), ("rw_g", 3), ("rw_a", 1), ("rw_d", 1), ("rw_back", 2),
                 ("rw_h", 3), ("moe_ct", 1), ("moe_h", NE * MC)]
VECTOR_GROUPS = [("a1_k", 4), ("a1_li1", 2), ("a1_li3", 2), ("a2_li1", 2), ("a2_li3", 2),
                 ("lin_qk", 16), ("lin_a", 1), ("lin_o", 2), ("ffn_k", 4), ("ffn_o", 2), ("ffn_f", 2),
                 ("x1_out", 2), ("rw_heads", 1), ("rw_r2", 4), ("rw_k2", 4), ("rw_v2", 4), ("rw_a2", 4), ("rw_d2", 4),
                 ("rw_sums", 2),
                 ("rw_out", 2), ("moe_logits", 1), ("moe_xT", 4), ("moe_b", 4), ("moe_y", NE * PAIRS)]


def after(groups, name):
    n = 0
    for layer, count in groups:
        n += count
        if layer == name:
            return n
    raise KeyError(name)


def s_done(name):
    return after(SCALAR_GROUPS, name)


def v_done(name):
    return after(VECTOR_GROUPS, name)


class Count:

    def __init__(self):
        self.base, self.k, self.index = 0, 0, 0

    def step(self):
        self.k += 1
        self.index += 1

    @property
    def value(self):
        return self.base + self.k


class Settle:

    def __init__(self, eng):
        self.eng, self.one = eng, eng.alloc_register("settled")
        eng.reg_mov(self.one, 1)

    def __call__(self):
        self.eng.reg_alu(self.one, self.one, self.one, ALU.bitwise_or)

    def finish(self, done):
        self.eng.wait_ge(done, self.one)


@contextmanager
def loop(eng, start, end, *counts, settle=None):
    before = [(c.base, c.k, c.index) for c, _ in counts]
    if settle is not None:
        settle()
    with eng.Fori(start, end) as it:
        for (c, per), (base, k, _) in zip(counts, before):
            c.base, c.k = (it - start) * per + (base + k), 0
        yield it
        for c, per in counts:
            assert c.k == per, (c.k, per)
    for (c, per), (base, k, index) in zip(counts, before):
        c.base, c.k, c.index = base, k + per * (end - start), index + per * (end - start)


class Chain:

    def __init__(self, eng, sem):
        self.eng, self.sem, self.count = eng, sem, Count()

    def __call__(self, ins):
        self.beside(ins)
        self.eng.wait_ge(self.sem, self.count.value)

    def beside(self, ins):
        ins.then_inc(self.sem, 1)
        self.count.step()


class Groups:

    def __init__(self, eng, banks, filled, emptied, plan):
        self.eng, self.banks, self.filled, self.emptied, self.plan = eng, banks, filled, emptied, list(plan)
        self.count, self.left = Count(), 0

    def layer(self, name):
        assert self.left == 0 and self.plan[0][0] == name, (name, self.plan[0], self.left)
        self.left = self.plan.pop(0)[1]

    def fill(self, emit):
        if self.count.index >= 2:
            self.eng.wait_ge(self.emptied, self.count.value - 1)
        bank = self.banks[self.count.index % 2]
        self.count.step()
        self.left -= 1
        emit(bank).then_inc(self.filled, 1)

    def take(self):
        bank = self.banks[self.count.index % 2]
        self.count.step()
        self.left -= 1
        self.eng.wait_ge(self.filled, self.count.value)
        return bank

    def release(self, ins, taken_since=0):
        ins.then_inc(self.emptied, 1)
        self.eng.wait_ge(self.emptied, self.count.value - taken_since)


class Region:

    def __init__(self, tensor, at=0):
        self.tensor, self.at = tensor, at

    def take(self, *shape, parts=P):
        n = 1
        for s in shape:
            n *= s
        view = self.tensor[0:parts, self.at:self.at + n]
        self.at += n
        assert self.at <= self.tensor.shape[1], (self.at, self.tensor.shape)
        if len(shape) == 2:
            view = view.rearrange("p (a b) -> p a b", b=shape[1])
        elif len(shape) == 3:
            view = view.rearrange("p (a b c) -> p a b c", b=shape[1], c=shape[2])
        return view


def perceiver_kernel(nc, io, out):
    ctx = ExitStack()
    with ctx:
        def sb(name, shape, dt=F32):
            return ctx.enter_context(nc.sbuf_tensor(name, shape, dt))

        sems = {}

        def sem(name):
            if name not in sems:
                sems[name] = ctx.enter_context(nc.semaphore(name))
            return sems[name]

        psum = ctx.enter_context(nc.psum_tensor("psum", [P, 8 * BANK], F32))

        def bank(i, n=1):
            return psum[:, i * BANK:(i + n) * BANK]

        X = sb("X", [P, KC, TOK])
        xc = sb("xc", [P, KC, TOK])
        sq = sb("sq", [P, KC, TOK])
        fold = sb("fold", [P, TOK])
        ident = sb("ident", [P, P])
        meanw = sb("meanw", [P, P])
        lanes = sb("lanes", [P, 12])
        tri = sb("tri", [P, P])
        after_s = sb("after_s", [P, T])
        upto_t = sb("upto_t", [P, T])
        above_q = sb("above_q", [P, T])
        par = sb("par", [P, KC * NROW])
        epar = sb("epar", [P, 3 * len(EROWS)])
        small = sb("small", [P, 256])
        rep = sb("rep", [H, P])
        headrows = sb("headrows", [H, len(HEADROWS) * 16])
        headpar = sb("headpar", [P, len(HEADROWS), 16])
        weights = [sb("weights0", [P, 8224])]
        weights1_at = -(-nc.sbuf_base // 32) * 32
        weights.append(sb("weights1", [P, 7168]))
        work_at = -(-nc.sbuf_base // 32) * 32
        work = sb("work", [P, 25856])
        keysT = [sb(f"keysT_{n}", [P, 2, S_EVEN], F32R) for n in ("high", "low")]
        q_stage = [sb(f"q_{n}", [P, 2, P], F32R) for n in ("high", "low")]

        cst = small[:, 0:4]
        l_std, l_rstd = (lanes[:, 4 * i:4 * i + 4] for i in range(2))
        mx16, sum16, rec16 = small[:, 16:32], small[:, 32:48], small[:, 48:64]
        ctx_sum, ctx_mean, ctx_var = small[:, 64:64 + NT], small[:, 80:80 + NT], small[:, 96:96 + NT]
        ctx_std, ctx_rstd = small[:, 112:112 + NT], small[:, 128:128 + NT]
        u_max, u_total, u_rec = small[:, 144:146], small[:, 146:147], small[:, 147:148]
        u_bias = [small[:, 148 + k:149 + k] for k in range(2)]
        u_sum = [small[:, 150 + 2 * k:152 + 2 * k] for k in range(2)]
        warm = small[:, 156:157]
        ctx_g, ctx_b = small[:, 154:155], small[:, 155:156]

        def col(name, i=0):
            at = (i % KC) * NROW + ROW_AT[name] + i // KC
            return par[:, at:at + 1]

        W = {}
        r = Region(weights[0])
        W["a1"] = dict(wq=r.take(KC, 512), wk=r.take(KC, 512), wv=r.take(KC, 512), li1=r.take(4, C),
                       li2=r.take(KC, HID), li3=r.take(MC, C))
        r = Region(weights[1])
        W["a2"] = dict(wq=r.take(KC, 512), wk=r.take(512), wv=r.take(512), li1=r.take(4, C),
                       li2=r.take(KC, HID), li3=r.take(MC, C))
        r = Region(weights[0])
        W["lin"] = dict(wq=r.take(KC, 1024), wk=r.take(KC, 1024), wv=r.take(KC, 1024), wo=r.take(8, C), wa=r.take(KC, H))
        r = Region(weights[1])
        W["ffn"] = dict(wq=r.take(KC, 512), wk=r.take(KC, 512), wv=r.take(KC, 512), wo=r.take(4, C), wff=r.take(KC, C))
        r = Region(weights[0])
        W["x1"] = dict(wq=r.take(KC, 1024), wk=r.take(1024), wv=r.take(1024), wo=r.take(8, C))
        r = Region(weights[1])
        W["rw"] = {n + "W1": r.take(KC, E1) for n in "rkvo"}
        W["rw"].update({n + "W2": r.take(3, C) for n in "rkvo"})
        W["rw"].update({n + "A": r.take(KC, LORA) for n in "gad"})
        W["rw"].update({n + "B": r.take(C, parts=LORA) for n in "gad"})
        r = Region(weights[0])
        W["moe"] = [dict(w_in=r.take(KC, HID), w_out=r.take(MC, C)) for _ in range(2)]
        r = Region(weights[1])
        W["gate"] = dict(wg=r.take(KC, NE), b_out=r.take(C, parts=NE))

        r = Region(work, 16384)
        x_rows = r.take(4, C)
        par_rows = r.take(C)
        epar_rows = r.take(E1)
        r = Region(work)
        h_in = r.take(KC, TOK)
        hq = r.take(KC, TOK)
        hk = r.take(KC, TOK)
        x_mid = r.take(KC, TOK)
        a1 = dict(QT=r.take(4, TOK), KT=r.take(4, TOK), V=r.take(NB, 512, parts=T), OT=r.take(4, TOK),
                  prob=[r.take(H, T) for _ in range(2)], probT=r.take(H, P, parts=T))
        a1["HT"] = Region(work, 4096).take(MC, TOK)
        r = Region(work)
        w_in2 = r.take(KC, TOK)
        x_mid2 = r.take(KC, TOK)
        QZ = r.take(NB * H * T)
        phase_at = r.at
        x_QT = r.take(8, TOK)
        x_WkT = r.take(8, P)
        x_xn = r.take(KC, TOK)
        rq = Region(work, phase_at)
        keys_full = rq.take(S_CTX)
        prob = [rq.take(NT * P) for _ in range(2)]
        raw = r.take(NT, CC)
        Y = [r.take(NT, CC) for _ in range(2)]
        probT = r.take(NT, P)
        z_stage = r.take(P)
        ctx_sq = r.take(NT, CC)
        ro = Region(work, phase_at)
        x_OT = ro.take(8, TOK)
        x_HT = ro.take(MC, TOK)
        x_m = ro.take(KC, TOK)

        def unit_rows(u):
            return QZ[:, ds(u * P, P)]

        def head_rows(h):
            return QZ.rearrange("p (b h t) -> p b h t", h=H, t=T)[:, :, h, :]

        def units(eng, batch):
            batch(0, 0, True, False)
            with loop(eng, 0, (NB - 2) // 2) as p:
                batch(p * 2 + 1, 1, False, False)
                batch(p * 2 + 2, 0, False, False)
            batch(NB - 1, 1, False, True)

        def pairs(eng, settle, first, n, step):
            if first:
                step(0, 0, True)
                step(1, 1, False)
            with loop(eng, int(first), n, settle=settle) as j:
                step(j * 2, 0, False)
                step(j * 2 + 1, 1, False)
        r = Region(work)
        lin = dict(xn=r.take(KC, TOK), QT=r.take(8, TOK), KT=r.take(8, TOK), V=r.take(NB, 1024, parts=T), OT=r.take(8, TOK),
                   la=r.take(PAIRS, H), z=r.take(PAIRS, H), ba=r.take(H), decay=xc[:].rearrange("p k (h s) -> p (k h) s", s=T),
                   prob=[r.take(H, T) for _ in range(2)])
        elu_at = r.at
        lin["probT"] = r.take(H, P, parts=T)
        elu = Region(work, elu_at).take(2, TOK)
        r = Region(work)
        ffn = dict(xn=r.take(KC, TOK), QT=r.take(4, TOK), KT=r.take(4, TOK), V=r.take(PAIRS, 512), OT=r.take(4, TOK),
                   prob=[r.take(H, T) for _ in range(2)], z=r.take(KC, TOK), z2=r.take(KC, TOK))
        r = Region(work)
        hd = {n: r.take(T, 16) for n in ("k", "r", "v", "a", "d", "akn", "rk")}
        hd["kn"] = sq[:].rearrange("p k (t n) -> p (k t) n", n=16)
        hd["bonus"] = xc[:].rearrange("p k (t n) -> p (k t) n", n=16)
        gate = r.take(KC, TOK)
        rs = Region(fold)
        s_tmp = rs.take(16, 16)
        s_keep = rs.take(16, 16)
        s_new = [r.take(16, 16) for _ in range(2)]
        s_row = r.take(16)
        nrm = r.take(T)
        nrm2 = r.take(T)
        hist_at = r.at
        hist = r.take(T + 2, 16, 16)
        r = Region(work, hist_at)
        rw_xn = r.take(KC, TOK)
        rw_in = r.take(KC, TOK)
        rw_HT = r.take(3, TOK)
        rw_lo = r.take(TOK, parts=LORA)
        rw_tm = r.take(2, 4 * C)
        EXPERT = KC * HID + MC * C
        moe_w = nc.alloc_sbuf_tensor_at("moe_w", [P, 2, 2, EXPERT], F32R, offset=work_at)
        moe_h = nc.alloc_sbuf_tensor_at("moe_h", [P, 2, MC, TOK], F32R, offset=work_at + 4 * 4 * EXPERT)
        moe_x = nc.alloc_sbuf_tensor_at("moe_x", [P, 2, KC, TOK], F32R, offset=weights1_at + 4 * 2048)
        moe_part = [[moe_w[:, slot, half, :] for half in range(2)] for slot in range(2)]
        moe_in = [[w[:, 0:KC * HID].rearrange("p (k n) -> p k n", n=HID) for w in part] for part in moe_part]
        moe_out = [[w[:, KC * HID:EXPERT].rearrange("p (k n) -> p k n", n=C) for w in part] for part in moe_part]
        HALVES = ((0, 0), (0, 1), (1, 0))
        r = Region(weights[1], 272)
        moe_xn = r.take(KC, TOK)
        combT = r.take(TOK, parts=NE)
        assert r.at <= 2048
        r = Region(work, 4 * EXPERT + 2 * MC * TOK)
        acc = r.take(4, C)
        logits = r.take(4, NE)
        comb = r.take(4, NE)
        iota8 = r.take(NE)
        top8 = r.take(4, 8)
        topf = r.take(4, 8)
        hot = r.take(4, NE)
        hot2 = r.take(4, NE)
        dlt = r.take(8)
        topi = sb("topi", [P, 4, 8], U32)

        scratch = {n: nc.dram_tensor("scratch_" + n, (TOK, C), F32, kind="Internal").ap() for n in ("r", "k", "v", "a", "d", "o")}

        def place(h, per):
            return (h % per) * (H // per) + h // per

        def bc(ap, shape):
            return ap.to_broadcast(shape)

        block = ctx.enter_context(nc.Block())

        @block.sync
        def _(sp):
            def load(dst, src, name):
                sp.dma_start(dst, src).then_inc(sem(name), 16)

            def heads(ap):
                return ap.rearrange("h (k p) d -> p k h d", p=P)

            def rows(ap):
                return ap.rearrange("(k p) n -> p k n", p=P)

            load(x_rows, io["x"].rearrange("b t c -> (b t) c").rearrange("(n p) c -> p n c", p=P), "x_loaded")
            for name, n in ROWS:
                a = io[name]
                a = a.rearrange("e (k c) -> (e k) c", c=C) if name == "L1_ffn_b_in" else a.rearrange("(k c) -> k c", c=C)
                load(par_rows[ROW_AT[name]:ROW_AT[name] + n, :], a, "rows_loaded")
            for i, name in enumerate(EROWS):
                load(epar_rows[i:i + 1, :], io[name].rearrange("(a c) -> a c", a=1), "rows_loaded")

            def stage_heads(w, dst, src):
                for k in range(KC):
                    load(dst[:, k, :].rearrange("p (h d) -> p h d", h=H), src[:, k * P:(k + 1) * P, :].rearrange("h p d -> p h d"), w)

            a = "L0_xattn_a1_"
            stage_heads("a1_weights", W["a1"]["wq"], io[a + "wq"])
            stage_heads("a1_weights", W["a1"]["wk"], io[a + "wk"])
            stage_heads("a1_weights", W["a1"]["wv"], io[a + "wv"])
            load(W["a1"]["li1"], rows(io[a + "li1_w"]), "a1_weights")
            load(W["a1"]["li2"], rows(io[a + "li2_w"]), "a1_weights")
            load(W["a1"]["li3"], rows(io[a + "li3_w"]), "a1_weights")
            a = "L0_xattn_a2_"
            stage_heads("a2_weights", W["a2"]["wq"], io[a + "wq"])
            load(W["a2"]["wk"].rearrange("p (h d) -> p h d", h=H), io[a + "wk"].rearrange("h c d -> c h d"), "a2_weights")
            load(W["a2"]["wv"].rearrange("p (h d) -> p h d", h=H), io[a + "wv"].rearrange("h c d -> c h d"), "a2_weights")
            load(W["a2"]["li1"], rows(io[a + "li1_w"]), "a2_weights")
            load(W["a2"]["li2"], rows(io[a + "li2_w"]), "a2_weights")
            load(W["a2"]["li3"], rows(io[a + "li3_w"]), "a2_weights")
            for i, name in enumerate(HEADROWS):
                load(headrows[:, i * 16:(i + 1) * 16], io["L1_attn_" + name].rearrange("(h n) -> h n", h=H), "headrows_loaded")

            def load_batch(b, dst):
                load(dst[:, 0:NT - 1, :],
                     io["ctx_512"][ds(b, 1), 0:(NT - 1) * P, :].rearrange("o (p n) c -> p (o n) c", p=P), "ctx_loaded")
                load(dst[0:TAIL, NT - 1, :], io["ctx_512"][ds(b, 1), (NT - 1) * P:S_CTX, :].rearrange("o p c -> p (o c)"), "ctx_loaded")

            sp.wait_ge(sem("norm_out"), NORM["mid"] + 1)
            load(ctx_g, io["L0_xattn_a2_lny_g"].rearrange("(c a) -> c a", a=1), "ctx_affine")
            load(ctx_b, io["L0_xattn_a2_lny_b"].rearrange("(c a) -> c a", a=1), "ctx_affine")
            sp.wait_ge(sem("v_emptied"), v_done("a1_li3"))
            load(W["lin"]["wq"], rows(io["L0_attn_Wq"]), "lin_weights")
            load(W["lin"]["wk"], rows(io["L0_attn_Wk"]), "lin_weights")
            load(W["lin"]["wv"], rows(io["L0_attn_Wv"]), "lin_weights")
            load(W["lin"]["wo"], rows(io["L0_attn_Wo"]), "lin_weights")
            load(W["lin"]["wa"], rows(io["L0_attn_Wa"]), "lin_weights")
            sp.wait_ge(sem("tails_zeroed"), 1)
            load_batch(0, raw)
            with loop(sp, 1, NB) as b:
                sp.wait_ge(sem("ctx_centered"), b)
                load_batch(b, raw)

            sp.wait_ge(sem("ffn_zeroed"), 1)
            load(lin["ba"], io["L0_attn_ba"].rearrange("(a c) -> a c", a=1).to_broadcast([P, H]), "lin_bias")
            for k in range(KC):
                for n in ("q", "k", "v"):
                    load(W["ffn"]["w" + n][:, k, :].rearrange("p (h d) -> p h d", h=H)[:, :, 0:16],
                         io["L0_ffn_W" + n][k * P:(k + 1) * P, :].rearrange("p (h d) -> p h d", h=H), "ffn_weights")
            for m in range(4):
                for j in range(4):
                    hh = 4 * m + j
                    load(W["ffn"]["wo"][32 * j:32 * j + 16, m, :], io["L0_ffn_Wo"][hh * 16:(hh + 1) * 16, :], "ffn_weights")
            load(W["ffn"]["wff"], rows(io["L0_ffn_Wff"]), "ffn_weights")

            sp.wait_ge(sem("v_emptied"), v_done("lin_o"))
            load(W["x1"]["wq"], rows(io["L1_xattn_Wq"]), "x1_weights")
            load(W["x1"]["wk"], io["L1_xattn_Wk"], "x1_weights")
            load(W["x1"]["wv"], io["L1_xattn_Wv"], "x1_weights")
            load(W["x1"]["wo"], rows(io["L1_xattn_Wo"]), "x1_weights")
            sp.wait_ge(sem("ffn_added"), 1)
            for n in "rkvo":
                load(W["rw"][n + "W1"], rows(io[f"L1_attn_{n}W1"]), "rw_weights")
                for m, (e0, en) in enumerate(EC):
                    load(W["rw"][n + "W2"][0:en, m, :], io[f"L1_attn_{n}W2"][e0:e0 + en, :], "rw_weights")
            for n in "gad":
                load(W["rw"][n + "A"], rows(io[f"L1_attn_{n}A"]), "rw_weights")
                load(W["rw"][n + "B"], io[f"L1_attn_{n}B"], "rw_weights")
            load_batch(0, Y[0])
            sp.wait_ge(sem("ctx_loaded"), 32 * NB + 32)
            load_batch(1, Y[1])
            with loop(sp, 1, NB // 2) as i:
                for slot in range(2):
                    sp.wait_ge(sem("z_ready"), i * 16 + (NB * 8 + 8 * slot - 8))
                    load_batch(i * 2 + slot, Y[slot])

            def load_expert(e, slot):
                w = W["moe"][slot]
                load(w["w_in"], io["L1_ffn_W_in"][ds(e, 1), :, :].rearrange("o (k p) n -> p (o k) n", p=P), f"expert_loaded{slot}")
                load(w["w_out"], io["L1_ffn_W_out"][ds(e, 1), :, :].rearrange("o (k p) n -> p (o k) n", p=P), f"expert_loaded{slot}")

            sp.wait_ge(sem("v_emptied"), v_done("x1_out"))
            load_expert(0, 0)
            load_expert(1, 1)
            for i, n in enumerate("rkvad"):
                sp.wait_ge(sem("v_emptied"), v_done("rw_" + n + "2"))
                sp.dma_start(scratch[n].rearrange("(n p) c -> p n c", p=P),
                             rw_tm[:, i % 2, :].rearrange("p (n c) -> p n c", c=C)).then_inc(sem("scratch_written"), 16)
                sp.wait_ge(sem("scratch_written"), 16 * (i + 1))
                for b in range(NB):
                    load(hd[n][b * H:(b + 1) * H, :, :],
                         scratch[n][b * T:(b + 1) * T, :].rearrange("t (h n) -> h t n", h=H), "heads_loaded")
            sp.wait_ge(sem("v_emptied"), v_done("rw_sums"))
            for b in range(NB):
                sp.dma_start(scratch["o"][b * T:(b + 1) * T, :].rearrange("t (h n) -> h t n", h=H),
                             hd["v"][b * H:(b + 1) * H, :, :]).then_inc(sem("out_scratched"), 16)
            sp.wait_ge(sem("out_scratched"), 16 * NB)
            load(rw_tm[:, 0, :].rearrange("p (n c) -> p n c", c=C), scratch["o"].rearrange("(n p) c -> p n c", p=P), "rw_back_loaded")
            sp.wait_ge(sem("v_emptied"), v_done("rw_out"))
            load(W["gate"]["wg"], rows(io["L1_ffn_W_gate"]), "gate_weights")
            load(W["gate"]["b_out"], io["L1_ffn_b_out"], "gate_weights")
            with loop(sp, 1, NE // 2) as i:
                for slot in range(2):
                    sp.wait_ge(sem("w_low"), i * 4 + (2 * slot - 2))
                    load_expert(i * 2 + slot, slot)
            sp.wait_ge(sem("v_emptied"), v_done("moe_y"))
            sp.dma_start(out.rearrange("b t c -> (b t) c").rearrange("(n p) c -> p n c", p=P), acc).then_inc(sem("stored"), 16)
            sp.wait_ge(sem("stored"), 16)

        @block.gpsimd
        def _(pool):
            settle = Settle(pool)
            chain = Chain(pool, sem("pool_order"))
            g = nc.gpsimd
            chain(g.memset(ident[:], 0.0))
            chain(g.affine_select(out=ident[:], in_=ident[:], compare_op=ALU.not_equal, fill=1.0, base=0,
                                  pattern=[[-1, P]], channel_multiplier=1))
            chain(g.memset(meanw[:], 1.0 / C))
            chain(g.memset(cst[:, 0:1], EPS))
            chain(g.memset(cst[:, 2:3], EPS * EPS))
            g.memset(cst[:, 1:2], 1e-6).then_inc(sem("constants"), 1)
            for half in keysT:
                chain(g.memset(half[:, :, S_CTX:S_EVEN].bitcast(F32), 0.0))
            chain(g.memset(tri[:], 1.0))
            chain(g.memset(after_s[:], 1.0))
            chain(g.memset(upto_t[:], 1.0))
            chain(g.memset(above_q[:], 1.0))
            for b in range(2):
                q = slice(b * T, (b + 1) * T)
                chain(g.memset(tri[q, (1 - b) * T:(2 - b) * T], 0.0))
                chain(g.affine_select(out=tri[q, q], in_=tri[q, q], compare_op=ALU.is_ge, fill=0.0, base=0,
                                      pattern=[[1, T]], channel_multiplier=-1))
                chain(g.affine_select(out=after_s[q, :], in_=after_s[q, :], compare_op=ALU.is_ge, fill=0.0, base=-1,
                                      pattern=[[-1, T]], channel_multiplier=1))
                chain(g.affine_select(out=upto_t[q, :], in_=upto_t[q, :], compare_op=ALU.is_ge, fill=0.0, base=0,
                                      pattern=[[-1, T]], channel_multiplier=1))
                chain(g.affine_select(out=above_q[q, :], in_=above_q[q, :], compare_op=ALU.is_ge, fill=0.0, base=-1,
                                      pattern=[[1, T]], channel_multiplier=-1))
            chain(g.memset(rep[:], 0.0))
            rep3 = rep[:].rearrange("k (b h) -> k b h", h=H)
            g.affine_select(out=rep3, in_=rep3, compare_op=ALU.not_equal, fill=1.0, base=0,
                            pattern=[[0, NB], [-1, H]], channel_multiplier=1).then_inc(sem("masks"), 1)


            full = [P, NT, CC]

            def normalize(b, slot, first):
                pool.wait_ge(sem("ctx_means"), b + 1)
                if not first:
                    pool.wait_ge(sem("z_ready"), b * 8 - 8)
                g.tensor_tensor(Y[slot], raw, bc(ctx_mean.unsqueeze(2), full), ALU.subtract).then_inc(sem("ctx_centered"), 1)
                pool.wait_ge(sem("ctx_centered"), b + 1)
                g.tensor_tensor(ctx_sq, Y[slot], Y[slot], ALU.mult).then_inc(sem("ctx_squared"), 1)
                pool.wait_ge(sem("ctx_rstds"), b + 1)
                g.tensor_tensor(Y[slot], Y[slot], bc(ctx_rstd.unsqueeze(2), full), ALU.mult).then_inc(sem("keys_made"), 1)

            pool.wait_ge(sem("norm_out"), NORM["a1_m"] + 1)
            g.memset(raw[:, NT - 1, :], 0.0).then_inc(sem("tails_zeroed"), 1)
            normalize(0, 0, True)
            normalize(1, 1, True)
            with loop(pool, 1, NB // 2) as i:
                normalize(i * 2, 0, False)
                normalize(i * 2 + 1, 1, False)
            pool.wait_ge(sem("norm_out"), NORM["lin"] + 1)
            for n in ("wq", "wk", "wv"):
                chain(g.memset(W["ffn"][n], 0.0))
            g.memset(W["ffn"]["wo"], 0.0).then_inc(sem("ffn_zeroed"), 1)
            pool.wait_ge(sem("state"), 1)
            with loop(pool, 0, T // STEPS, (chain.count, 2 * STEPS)) as i:
                for step in range(STEPS):
                    t = i * STEPS + step
                    v_j = hd["v"][:, ds(t, 1), :].rearrange("p o j -> p j o")
                    rk_k = hd["rk"][:, ds(t, 1), :]
                    d_j = hd["d"][:, ds(t, 1), :].rearrange("p o j -> p j o")
                    w = hist[:, ds(t + 1, 1), :, :].rearrange("p o j k -> p (o j) k")
                    chain.beside(g.tensor_tensor(s_new[step % 2], bc(v_j, [P, 16, 16]), bc(rk_k, [P, 16, 16]), ALU.mult))
                    pool.wait_ge(sem("state"), t + 1)
                    chain(g.tensor_tensor(s_keep, w, bc(d_j, [P, 16, 16]), ALU.mult))
                    g.tensor_tensor(s_keep, s_keep, s_new[step % 2], ALU.add).then_inc(sem("state_kept"), 1)
            pool.wait_ge(sem("norm_out"), NORM["moe"] + 1)
            g.iota(iota8, pattern=[[1, NE]], base=0, channel_multiplier=0, allow_small_or_imprecise_dtypes=True).then_inc(sem("iota"), 1)

            def split(e, slot):
                for half in range(2):
                    at = slice(half * (EXPERT // 2), (half + 1) * (EXPERT // 2))
                    pool.wait_ge(sem("w_high"), e * MC + (half + 1) * (MC // 2))
                    g.tensor_tensor(moe_part[slot][1][:, at], weights[0][:, slot * EXPERT + at.start:slot * EXPERT + at.stop],
                                    moe_part[slot][0][:, at], ALU.subtract).then_inc(sem("w_low"), 1)

            split(0, 0)
            split(1, 1)
            with loop(pool, 1, NE // 2) as i:
                split(i * 2, 0)
                split(i * 2 + 1, 1)
            settle.finish(sem("constants"))

        @block.tensor
        def _(pe):
            settle = Settle(pe)
            mm, tr = nc.tensor.matmul, nc.tensor.transpose
            sg = Groups(pe, (bank(0), bank(1)), sem("s_filled"), sem("s_emptied"), SCALAR_GROUPS)
            vg = Groups(pe, (bank(2), bank(3)), sem("v_filled"), sem("v_emptied"), VECTOR_GROUPS)

            def product(groups, name, n, lhs, rhs, k, outs=None):
                groups.layer(name)
                for i in range(n):
                    def emit(b):
                        for j in range(k):
                            left, right = lhs(i, j), rhs(i, j)
                            o = b[0:left.shape[-1], 0:right.shape[-1]]
                            ins = mm(o, lhsT=left, rhs=right, start=(j == 0), stop=(j == k - 1))
                        return ins
                    groups.fill(emit)

            def means(b):
                for p in range(4):
                    for k in range(KC):
                        ins = mm(b[:, p:p + 1], lhsT=sq[:, k, p * P:(p + 1) * P], rhs=meanw[:, 0:1], start=(k == 0), stop=(k == KC - 1))
                return ins

            def over_features(b, column):
                for p in range(4):
                    ins = tr(b[:, p * P:(p + 1) * P], bc(column[:, p:p + 1], [P, P]), ident[:])
                return ins

            def norm(name, src, signal, value):
                i = NORM[name]
                for k in range(KC):
                    pe.wait_ge(sem(signal), value - (KC - 1 - k) if signal.endswith("emptied") else value)
                    ins = mm(bank(4), lhsT=meanw[:], rhs=src[:, k, :], start=(k == 0), stop=(k == KC - 1))
                ins.then_inc(sem("norm_mean"), 1)
                pe.wait_ge(sem("norm_squared"), 2 * i + 2)
                means(bank(5)).then_inc(sem("norm_var"), 1)
                pe.wait_ge(sem("norm_inverse"), i + 1)
                over_features(bank(5), l_rstd).then_inc(sem("norm_rstd"), 1)

            def l2(i):
                pe.wait_ge(sem("l2_squared"), i + 1)
                means(bank(4)).then_inc(sem("l2_sum"), 1)
                pe.wait_ge(sem("l2_inverse"), i + 1)
                over_features(bank(4), l_rstd).then_inc(sem("l2_factor"), 1)

            def core(which, d, dk, dv):
                per, perv = P // dk, P // dv
                nch = H // per
                left, right = (d["KT"], d["QT"]) if which == 2 else (d["QT"], d["KT"])

                def scores(p):
                    done = p + which * PAIRS
                    if which == 1:
                        pe.wait_ge(sem("lin_spread"), p + 1)
                        if p:
                            pe.wait_ge(sem("core_exp"), done)
                        for i in range(2):
                            ins = mm(bank(2 + i), lhsT=tri[:],
                                     rhs=d["decay"][:, 8 * i:8 * i + 8, :].rearrange("p h s -> p (h s)"), start=True, stop=True)
                        ins.then_inc(sem("lin_sums"), 1)
                    if p:
                        pe.wait_ge(sem("core_taken"), done)
                    for h in range(H):
                        rows = slice((h % per) * dk, (h % per + 1) * dk)
                        for b in range(2):
                            t = slice(p * P + b * T, p * P + (b + 1) * T)
                            ins = mm(bank(h % per)[b * T:(b + 1) * T, (h // per) * T:(h // per + 1) * T],
                                     lhsT=left[rows, h // per, t], rhs=right[rows, h // per, t], start=True, stop=True)
                    ins.then_inc(sem("core_scores"), 1)

                def turn(p, i):
                    for h in range(4 * i, 4 * i + 4):
                        ins = tr(bank(4 + i % 2)[0:T, (h % 4) * P:(h % 4 + 1) * P], d["prob"][p % 2][:, h, :], ident[:])
                    ins.then_inc(sem("core_turned_" + "sv"[i % 2]), 1)

                pe.wait_ge(sem("masks"), 1)
                scores(0)
                for p in range(PAIRS):
                    done = p + which * PAIRS
                    if which == 2 and p < PAIRS - 1:
                        scores(p + 1)
                    pe.wait_ge(sem("core_probs"), done + 1)
                    if which < 2:
                        turn(p, 0)
                        turn(p, 1)
                    if which < 2 and p < PAIRS - 1:
                        scores(p + 1)
                    if which < 2:
                        pe.wait_ge(sem("core_pT_s"), 2 * done + 1)
                        turn(p, 2)
                        pe.wait_ge(sem("core_pT_v"), 2 * done + 1)
                        turn(p, 3)
                    if done:
                        pe.wait_ge(sem("core_stored"), done)
                    for j in range(H):
                        h = (j % nch) * per + j // nch
                        assert place(h, per) == j
                        if which < 2 and j == 8:
                            pe.wait_ge(sem("core_pT_s"), 2 * done + 2)
                        if which < 2 and j == 12:
                            pe.wait_ge(sem("core_pT_v"), 2 * done + 2)
                        for b in range(2):
                            q = slice(b * T, (b + 1) * T)
                            c0 = (h // perv) * P + b * T if which < 2 else b * BANK + (h // perv) * T
                            o = bank(6, 2)[(h % perv) * dv:(h % perv + 1) * dv, c0:c0 + T]
                            if which == 2:
                                ins = mm(o, lhsT=d["V"][q, p, h * dv:(h + 1) * dv], rhs=d["prob"][p % 2][q, j, :], start=True, stop=True)
                            else:
                                ins = mm(o, lhsT=d["V"][:, 2 * p + b, h * dv:(h + 1) * dv], rhs=d["probT"][:, j, q], start=True, stop=True)
                    ins.then_inc(sem("core_o"), 1)

            def cross(which, name, wk, n_chunk):
                D = n_chunk * P // H
                per = P // D
                sg.layer(name + "_wkT")
                for i in range(n_chunk // 4):
                    def emit(b):
                        for j in range(4):
                            c0 = (4 * i + j) * P
                            ins = tr(b[:, j * P:(j + 1) * P], wk[:, c0:c0 + P], ident[:])
                        return ins
                    sg.fill(emit)
                pe.wait_ge(sem("norm_out"), NORM["a2_x" if which == 0 else "x1"] + 1)
                product(sg, name + "_q", n_chunk, lambda i, j: W[name]["wq"][:, j, i * P:(i + 1) * P],
                        lambda i, j: x_xn[:, j, :], KC)
                pe.wait_ge(sem("s_emptied"), s_done(name + "_q"))

                def rows(h):
                    return slice((h % per) * D, (h % per + 1) * D)

                product(sg, name + "_qp", H, lambda h, j: x_WkT[rows(h), h // per, :],
                        lambda h, j: x_QT[rows(h), h // per, :], 1)
                pe.wait_ge(sem("s_emptied"), s_done(name + "_qp"))

                def turn_keys(b, slot, i):
                    if i == 0 and which == 0:
                        pe.wait_ge(sem("keys_made"), b + 1)
                    elif i == 0:
                        pe.wait_ge(sem("ctx_loaded"), b * 32 + (32 * NB + 32))
                    elif i >= 2:
                        pe.wait_ge(sem("keys_out"), b * 4 + (which * NB * 4 + i - 1))
                    for j in range(min(4, NT - 4 * i)):
                        t = 4 * i + j
                        n = min(P, S_CTX - t * P)
                        ins = tr(bank(4 + i % 2)[:, j * P:j * P + n], Y[slot][0:n, t, :], ident[0:n, 0:n])
                    ins.then_inc(sem("keys_turned"), 1)

                def scores(n, k, slot, half, keys_of=None):
                    if half == 0:
                        pe.wait_ge(sem("q_staged"), n + (64 * which + 1))
                    if keys_of is not None:
                        pe.wait_ge(sem("keys_split"), keys_of * 4 + (which * NB * 4 + 2 * half + 2))
                    for i in (2 * half, 2 * half + 1):
                        c = min(BANK, S_EVEN - i * BANK)
                        for q, key in ((0, 0), (0, 1), (1, 0)):
                            ins = mm(bank(i)[:, 0:c], lhsT=q_stage[q][:, k, :], rhs=keysT[key][:, slot, i * BANK:i * BANK + c],
                                     start=(q + key == 0), stop=(q == 1))
                    ins.then_inc(sem("scores" + "AB"[half]), 1)

                def turn_z(u):
                    pe.wait_ge(sem("z_scaled"), u + (64 * which + 1))
                    tr(bank(7)[:, 0:P], z_stage, ident[:]).then_inc(sem("zT_ready"), 1)

                def weigh(u, k, slot, first, nxt, keys=None):
                    g = u + 64 * which

                    def turn(i):
                        for j in range(min(4, NT - 4 * i)):
                            t = 4 * i + j
                            n = min(P, S_CTX - t * P)
                            ins = tr(bank(4 + i % 2)[0:n, j * P:(j + 1) * P], prob[k][:, t * P:t * P + n], ident[:])
                        ins.then_inc(sem("turned_" + "sv"[i // 2]), 1)

                    def add(i):
                        pe.wait_ge(sem("turned_out_" + "sv"[i // 2]), g * 2 + (i % 2 + 1))
                        for j in range(min(4, NT - 4 * i)):
                            t = 4 * i + j
                            n = min(P, S_CTX - t * P)
                            ins = mm(bank(6)[:, 0:CC], lhsT=probT[0:n, t, :], rhs=Y[slot][0:n, t, :], start=(t == 0), stop=(t == NT - 1))
                        return ins

                    if keys:
                        turn_keys(*keys, 0)
                        turn_keys(*keys, 1)
                    pe.wait_ge(sem("expA"), g + 1)
                    if nxt:
                        scores(*nxt[0:3], 0, nxt[3])
                    if keys:
                        turn_keys(*keys, 2)
                        turn_keys(*keys, 3)
                        pe.wait_ge(sem("keys_out"), keys[0] * 4 + (which * NB * 4 + 3))
                    turn(0)
                    pe.wait_ge(sem("expB"), g + 1)
                    if nxt:
                        scores(*nxt[0:3], 1, nxt[3])
                    if keys:
                        pe.wait_ge(sem("keys_out"), keys[0] * 4 + (which * NB * 4 + 4))
                    turn(1)
                    if not first:
                        turn_z(u - 1)
                    add(0)
                    turn(2)
                    add(1)
                    turn(3)
                    add(2)
                    add(3).then_inc(sem("z_ready"), 1)

                def batch(b, slot, first, final):
                    pairs(pe, settle, first, 3, lambda h, k, f: weigh(b * 8 + h, k, slot, f, (b * 8 + h + 1, 1 - k, slot, None)))
                    weigh(b * 8 + 6, 0, slot, False, (b * 8 + 7, 1, slot, None), None if final else (b + 1, 1 - slot))
                    weigh(b * 8 + 7, 1, slot, False, None if final else (b * 8 + 8, 0, 1 - slot, b + 1))

                for i in range(4):
                    turn_keys(0, 0, i)
                scores(0, 0, 0, 0, 0)
                scores(0, 0, 0, 1, 0)
                units(pe, batch)
                pe.wait_ge(sem("zT_stored"), 64 * which + 63)
                turn_z(8 * NB - 1)
                pe.wait_ge(sem("zT_stored"), 64 * (which + 1))
                sg.layer(name + "_o")
                for m in range(n_chunk):
                    def emit(b):
                        for j in range(per):
                            hh = m * per + j
                            ins = mm(b[j * D:(j + 1) * D, :], lhsT=W[name]["wv"][:, hh * D:(hh + 1) * D], rhs=head_rows(hh),
                                     start=True, stop=True)
                        return ins
                    sg.fill(emit)
                pe.wait_ge(sem("s_emptied"), s_done(name + "_o"))

            def mlp(name, src, hT):
                w = W[name]
                pe.wait_ge(sem("norm_out"), NORM[name + "_m"] + 1)
                product(sg, name + "_h", MC, lambda i, j: w["li2"][:, j, i * P:(i + 1) * P], lambda i, j: src[:, j, :], KC)
                pe.wait_ge(sem("s_emptied"), s_done(name + "_h"))
                product(vg, name + "_li3", KC, lambda i, j: w["li3"][:, j, i * P:(i + 1) * P], lambda i, j: hT[:, j, :], MC)

            pe.wait_ge(sem("constants"), 1)
            pe.wait_ge(sem("x_loaded"), 16)
            sg.layer("x_in")
            for k in range(KC):
                def emit(b):
                    for n in range(4):
                        ins = tr(b[:, n * P:(n + 1) * P], x_rows[:, n, k * P:(k + 1) * P], ident[:])
                    return ins
                sg.fill(emit)
            norm("x", X, "s_emptied", s_done("x_in"))
            pe.wait_ge(sem("rows_loaded"), 16 * (len(ROWS) + len(EROWS)))
            sg.layer("params")

            def emit(b):
                for k in range(KC):
                    ins = tr(b[:, k * NROW:(k + 1) * NROW], par_rows[0:NROW, k * P:(k + 1) * P], ident[0:NROW, 0:NROW])
                return ins
            sg.fill(emit)
            ne = len(EROWS)
            for m, (e0, en) in enumerate(EC):
                sg.fill(lambda b: tr(b[0:en, 0:ne], epar_rows[0:ne, e0:e0 + en], ident[0:ne, 0:ne]))
            pe.wait_ge(sem("norm_out"), NORM["x"] + 1)
            norm("a1_x", h_in, "norm_out", NORM["x"] + 1)
            pe.wait_ge(sem("norm_out"), NORM["a1_x"] + 1)
            pe.wait_ge(sem("a1_weights"), 16 * 9)
            w = W["a1"]
            product(sg, "a1_q", 4, lambda i, j: w["wq"][:, j, i * P:(i + 1) * P], lambda i, j: hq[:, j, :], KC)
            product(vg, "a1_k", 4, lambda i, j: w["wk"][:, j, i * P:(i + 1) * P], lambda i, j: hk[:, j, :], KC)
            product(sg, "a1_v", NB, lambda i, j: hk[:, j, i * T:(i + 1) * T], lambda i, j: w["wv"][:, j, :], KC)
            pe.wait_ge(sem("s_emptied"), s_done("a1_v"))
            pe.wait_ge(sem("v_emptied"), v_done("a1_k"))
            core(0, a1, 32, 32)
            pe.wait_ge(sem("core_stored"), PAIRS)
            product(vg, "a1_li1", KC, lambda i, j: w["li1"][:, j, i * P:(i + 1) * P], lambda i, j: a1["OT"][:, j, :], 4)
            pe.wait_ge(sem("v_emptied"), v_done("a1_li1"))
            norm("a1_m", x_mid, "v_emptied", v_done("a1_li1"))
            mlp("a1", hq, a1["HT"])
            norm("mid", x_mid, "v_emptied", v_done("a1_li3"))
            pe.wait_ge(sem("norm_out"), NORM["mid"] + 1)
            norm("a2_x", w_in2, "norm_out", NORM["mid"] + 1)
            pe.wait_ge(sem("a2_weights"), 16 * 7)
            cross(0, "a2", W["a2"]["wk"], 4)
            w2 = W["a2"]
            product(vg, "a2_li1", KC, lambda i, j: w2["li1"][:, j, i * P:(i + 1) * P], lambda i, j: x_OT[:, j, :], 4)
            pe.wait_ge(sem("v_emptied"), v_done("a2_li1"))
            norm("a2_m", x_mid2, "v_emptied", v_done("a2_li1"))
            mlp("a2", x_m, x_HT)

            norm("lin", X, "v_emptied", v_done("a2_li3"))
            pe.wait_ge(sem("norm_out"), NORM["lin"] + 1)
            pe.wait_ge(sem("lin_weights"), 16 * 5)
            wl = W["lin"]
            xn = lin["xn"]
            vg.layer("lin_qk")
            sg.layer("lin_v")
            for i in range(16):
                def emit_qk(b):
                    w = wl["wq"] if i % 2 == 0 else wl["wk"]
                    for j in range(KC):
                        ins = mm(b, lhsT=w[:, j, (i // 2) * P:(i // 2 + 1) * P], rhs=xn[:, j, :], start=(j == 0), stop=(j == KC - 1))
                    return ins

                def emit_v(b):
                    for j in range(KC):
                        ins = mm(b[0:T, :], lhsT=xn[:, j, (i // 2) * T:(i // 2 + 1) * T],
                                 rhs=wl["wv"][:, j, (i % 2) * BANK:(i % 2 + 1) * BANK], start=(j == 0), stop=(j == KC - 1))
                    return ins
                vg.fill(emit_qk)
                sg.fill(emit_v)
            vg.layer("lin_a")

            def emit(b):
                for p in range(PAIRS):
                    for j in range(KC):
                        ins = mm(b[:, p * H:(p + 1) * H], lhsT=xn[:, j, p * P:(p + 1) * P], rhs=wl["wa"][:, j, :],
                                 start=(j == 0), stop=(j == KC - 1))
                return ins
            vg.fill(emit)
            pe.wait_ge(sem("s_emptied"), s_done("lin_v"))
            pe.wait_ge(sem("v_emptied"), v_done("lin_a"))
            core(1, lin, 64, 64)
            pe.wait_ge(sem("core_stored"), 2 * PAIRS)
            product(vg, "lin_o", KC, lambda i, j: wl["wo"][:, j, i * P:(i + 1) * P], lambda i, j: lin["OT"][:, j, :], 8)

            pe.wait_ge(sem("v_emptied"), v_done("lin_o"))
            norm("ffn", X, "v_emptied", v_done("lin_o"))
            pe.wait_ge(sem("norm_out"), NORM["ffn"] + 1)
            pe.wait_ge(sem("ffn_weights"), 16 * (3 * KC + 16 + 1))
            wf = W["ffn"]
            xf = ffn["xn"]
            product(sg, "ffn_q", 4, lambda i, j: wf["wq"][:, j, i * P:(i + 1) * P], lambda i, j: xf[:, j, :], KC)
            product(vg, "ffn_k", 4, lambda i, j: wf["wk"][:, j, i * P:(i + 1) * P], lambda i, j: xf[:, j, :], KC)
            product(sg, "ffn_v", PAIRS, lambda i, j: xf[:, j, i * P:(i + 1) * P], lambda i, j: wf["wv"][:, j, :], KC)
            pe.wait_ge(sem("s_emptied"), s_done("ffn_v"))
            pe.wait_ge(sem("v_emptied"), v_done("ffn_k"))
            core(2, ffn, 32, 32)
            pe.wait_ge(sem("core_stored"), 3 * PAIRS)
            product(vg, "ffn_o", KC, lambda i, j: wf["wo"][:, j, i * P:(i + 1) * P], lambda i, j: ffn["OT"][:, j, :], 4)
            l2(0)
            pe.wait_ge(sem("l2_out"), 1)
            product(vg, "ffn_f", KC, lambda i, j: wf["wff"][:, j, i * P:(i + 1) * P], lambda i, j: ffn["z"][:, j, :], KC)
            l2(1)

            pe.wait_ge(sem("ffn_added"), 1)
            norm("x1", X, "ffn_added", 1)
            pe.wait_ge(sem("x1_weights"), 16 * 4)
            cross(1, "x1", W["x1"]["wk"], 8)
            product(vg, "x1_out", KC, lambda i, j: W["x1"]["wo"][:, j, i * P:(i + 1) * P], lambda i, j: x_OT[:, j, :], 8)

            settle.finish(sem("constants"))
            wr = W["rw"]
            pe.wait_ge(sem("v_emptied"), v_done("x1_out"))
            norm("rw", X, "v_emptied", v_done("x1_out"))
            pe.wait_ge(sem("rw_weights"), 16 * (4 * 4 + 6))
            pe.wait_ge(sem("headrows_loaded"), 16 * len(HEADROWS))
            product(vg, "rw_heads", 1, lambda i, j: rep[:], lambda i, j: headrows[:], 1)
            for i, n in enumerate("rkv"):
                pe.wait_ge(sem("rw_shifted"), i + 1)
                sg.layer("rw_" + n)
                for m, (e0, en) in enumerate(EC):
                    def emit(b):
                        for j in range(KC):
                            ins = mm(b[0:en, :], lhsT=wr[n + "W1"][:, j, e0:e0 + en], rhs=rw_in[:, j, :], start=(j == 0), stop=(j == KC - 1))
                        return ins
                    sg.fill(emit)
                pe.wait_ge(sem("s_emptied"), s_done("rw_" + n))
                vg.layer("rw_" + n + "2")
                for p in range(4):
                    def emit(b):
                        for m, (e0, en) in enumerate(EC):
                            ins = mm(b[:, 0:C], lhsT=rw_HT[0:en, m, p * P:(p + 1) * P], rhs=wr[n + "W2"][0:en, m, :],
                                     start=(m == 0), stop=(m == 2))
                        return ins
                    vg.fill(emit)
            for i, n in enumerate("gad"):
                pe.wait_ge(sem("rw_shifted"), i + 4)
                sg.layer("rw_" + n)

                def emit(b):
                    for j in range(KC):
                        ins = mm(b[0:LORA, :], lhsT=wr[n + "A"][:, j, :], rhs=rw_in[:, j, :], start=(j == 0), stop=(j == KC - 1))
                    return ins
                sg.fill(emit)
                pe.wait_ge(sem("s_emptied"), s_done("rw_v") + 1 + (0, 3, 4)[i])
                if n == "g":
                    for m in range(KC):
                        sg.fill(lambda b: mm(b, lhsT=wr["gB"][:, m * P:(m + 1) * P], rhs=rw_lo, start=True, stop=True))
                else:
                    vg.layer("rw_" + n + "2")
                    for p in range(4):
                        vg.fill(lambda b: mm(b[:, 0:C], lhsT=rw_lo[:, p * P:(p + 1) * P], rhs=wr[n + "B"], start=True, stop=True))
            vg.layer("rw_sums")
            for lo, hi in RW_SUMS:
                pe.wait_ge(sem("state"), hi + 4)

                def emit(b):
                    for k in range(16):
                        ins = mm(b[:, 0:(hi - lo) * 16], lhsT=ident[:], rhs=hist[:, lo + 2:hi + 2, :, k],
                                 start=(k == 0), stop=(k == 15))
                    return ins
                vg.fill(emit)
            pe.wait_ge(sem("rw_back_loaded"), 16)
            sg.layer("rw_back")
            back = rw_tm[:, 0, :].rearrange("p (n c) -> p n c", c=C)
            for k in range(KC):
                def emit(b):
                    for n in range(4):
                        ins = tr(b[:, n * P:(n + 1) * P], back[:, n, k * P:(k + 1) * P], ident[:])
                    return ins
                sg.fill(emit)
            pe.wait_ge(sem("s_emptied"), s_done("rw_back"))
            norm("rw_o", rw_xn, "s_emptied", s_done("rw_back"))
            pe.wait_ge(sem("rw_gated"), 1)
            sg.layer("rw_h")
            for m, (e0, en) in enumerate(EC):
                def emit(b):
                    for j in range(KC):
                        ins = mm(b[0:en, :], lhsT=wr["oW1"][:, j, e0:e0 + en], rhs=rw_in[:, j, :], start=(j == 0), stop=(j == KC - 1))
                    return ins
                sg.fill(emit)
            pe.wait_ge(sem("s_emptied"), s_done("rw_h"))
            vg.layer("rw_out")
            for i in range(KC):
                def emit(b):
                    for m, (e0, en) in enumerate(EC):
                        ins = mm(b, lhsT=wr["oW2"][0:en, m, i * P:(i + 1) * P], rhs=rw_HT[0:en, m, :], start=(m == 0), stop=(m == 2))
                    return ins
                vg.fill(emit)

            pe.wait_ge(sem("v_emptied"), v_done("rw_out"))
            norm("moe", X, "v_emptied", v_done("rw_out"))
            pe.wait_ge(sem("norm_out"), NORM["moe"] + 1)
            pe.wait_ge(sem("gate_weights"), 32)
            vg.layer("moe_logits")

            def emit(b):
                for p in range(4):
                    for j in range(KC):
                        ins = mm(b[:, p * NE:(p + 1) * NE], lhsT=moe_xn[:, j, p * P:(p + 1) * P], rhs=W["gate"]["wg"][:, j, :],
                                 start=(j == 0), stop=(j == KC - 1))
                return ins
            vg.fill(emit)
            vg.layer("moe_xT")
            for p in range(4):
                def emit(b):
                    for k in range(KC):
                        ins = tr(b[:, k * P:(k + 1) * P], X[:, k, p * P:(p + 1) * P], ident[:])
                    return ins
                vg.fill(emit)
            pe.wait_ge(sem("combined"), 1)
            sg.layer("moe_ct")

            def emit(b):
                for p in range(4):
                    ins = tr(b[0:NE, p * P:(p + 1) * P], comb[:, p, :], ident[:])
                return ins
            sg.fill(emit)
            pe.wait_ge(sem("s_emptied"), s_done("moe_ct"))
            product(vg, "moe_b", 4, lambda i, j: combT[:, i * P:(i + 1) * P], lambda i, j: W["gate"]["b_out"], 1)
            sg.layer("moe_h")
            vg.layer("moe_y")
            pe.wait_ge(sem("x_split"), 2)
            with loop(pe, 0, NE // 2, (sg.count, 2 * MC), (vg.count, 2 * PAIRS)) as i:
                for slot in range(2):
                    e = i * 2 + slot
                    pe.wait_ge(sem("w_low"), e * 2 + 1)
                    for m in range(MC):
                        def emit(b):
                            for j in range(KC):
                                for wh, xh in HALVES:
                                    ins = mm(b, lhsT=moe_in[slot][wh][:, j, m * P:(m + 1) * P], rhs=moe_x[:, xh, j, :],
                                             start=(j + wh + xh == 0), stop=(j == KC - 1 and wh == 1))
                            return ins
                        sg.fill(emit)
                    pe.wait_ge(sem("w_low"), e * 2 + 2)
                    for p in range(PAIRS):
                        def emit(b):
                            for m in range(MC):
                                if p == 0:
                                    pe.wait_ge(sem("h_low"), e * MC + (m + 1))
                                for hh, wh in HALVES:
                                    ins = mm(b[:, 0:C], lhsT=moe_h[:, hh, m, p * P:(p + 1) * P], rhs=moe_out[slot][wh][:, m, :],
                                             start=(m + hh + wh == 0), stop=(m == MC - 1 and hh == 1))
                            return ins
                        vg.fill(emit)

        @block.scalar
        def _(act):
            settle = Settle(act)
            chain = Chain(act, sem("scalar_order"))
            f = nc.scalar.activation
            sg = Groups(act, (bank(0), bank(1)), sem("s_filled"), sem("s_emptied"), SCALAR_GROUPS)

            def ready(func):
                chain(f(warm, cst[:, 0:1], func))

            def norm(name, eps=0, twice=False):
                i = NORM[name]
                for k in range(KC):
                    act.wait_ge(sem("norm_centered"), 2 * i + k + 1)
                    f(sq[:, k, :], xc[:, k, :], ACT.Square).then_inc(sem("norm_squared"), 1)
                    act.wait_ge(sem("norm_squared"), 2 * i + k + 1)
                ready(ACT.Sqrt)
                act.wait_ge(sem("norm_var"), i + 1)
                if twice:
                    eps = 2
                f(l_std, bank(5)[:, 0:4], ACT.Sqrt, bias=cst[:, eps:eps + 1], scale=1.0 + EPS if twice else 1.0).then_inc(sem("norm_std"), 1)
                act.wait_ge(sem("norm_std"), i + 1)

            def copies(name, n, dst, func=ACT.Copy, bias=None, rows=slice(0, P), cols=slice(0, BANK)):
                sg.layer(name)
                for i in range(n):
                    b = sg.take()
                    if bias is None:
                        sg.release(f(dst(i), b[rows, cols], func))
                    else:
                        sg.release(f(dst(i), b[rows, cols], func, bias=bias(i)))

            def core(which, d, scale, nch):
                def weights(p):
                    done = p + which * PAIRS
                    if which == 1:
                        act.wait_ge(sem("lin_sums"), p + 1)
                        f(d["decay"], bank(2, 2).rearrange("p (h s) -> p h s", h=H), ACT.Exp).then_inc(sem("core_exp"), 1)
                    else:
                        act.wait_ge(sem("core_taken"), done + 1)
                        f(d["prob"][p % 2], d["prob"][p % 2], ACT.Exp, scale=scale).then_inc(sem("core_exp"), 1)
                    act.wait_ge(sem("core_exp"), done + 1)

                def turned(p, i):
                    at = 2 * (p + which * PAIRS) + i // 2 + 1
                    act.wait_ge(sem("core_turned_s"), at)
                    f(d["probT"][:, 4 * i:4 * i + 4, :], bank(4)[0:T, :].rearrange("p (h s) -> p h s", h=4),
                      ACT.Copy).then_inc(sem("core_pT_s"), 1)
                    act.wait_ge(sem("core_pT_s"), at)

                if which > 0:
                    ready(ACT.Exp)
                weights(0)
                for p in range(PAIRS):
                    done = p + which * PAIRS
                    if which < 2:
                        turned(p, 0)
                    if which == 1 and p < PAIRS - 1:
                        weights(p + 1)
                    if which < 2:
                        turned(p, 2)
                    if which != 1 and p < PAIRS - 1:
                        weights(p + 1)
                    act.wait_ge(sem("core_o"), done + 1)
                    o = bank(6, 2)[:, 0:nch * P].rearrange("p (m t) -> p m t", t=P)
                    dst = d["OT"][:, :, p * P:(p + 1) * P]
                    if which == 2:
                        o = bank(6, 2).rearrange("p (b m t) -> p b m t", b=2, t=T)[:, :, 0:nch, :]
                        dst = dst.rearrange("p m (b t) -> p b m t", b=2)
                    f(dst, o, ACT.Copy).then_inc(sem("core_stored"), 1)
                    act.wait_ge(sem("core_stored"), done + 1)

            def cross(which, name, n_chunk, scale):
                sg.layer(name + "_wkT")
                for i in range(n_chunk // 4):
                    b = sg.take()
                    sg.release(f(x_WkT[:, 4 * i:4 * i + 4, :], b.rearrange("p (m c) -> p m c", c=P), ACT.Copy))
                copies(name + "_q", n_chunk, lambda i: x_QT[:, i, :])
                sg.layer(name + "_qp")
                for i in range(H):
                    b = sg.take()
                    sg.release(f(head_rows(i), b.rearrange("p (b t) -> p b t", t=T), ACT.Copy))

                def affine(dst, src, name):
                    if which == 0:
                        f(dst, src, ACT.Identity, bias=ctx_b, scale=ctx_g).then_inc(sem(name), 1)
                    else:
                        f(dst, src, ACT.Copy).then_inc(sem(name), 1)

                def keys_out(b):
                    for i in range(4):
                        at = b * 4 + (which * NB * 4 + i + 1)
                        lo, hi = i * BANK, min((i + 1) * BANK, S_CTX)
                        act.wait_ge(sem("keys_turned"), at)
                        affine(keys_full[:, lo:hi], bank(4 + i % 2)[:, 0:hi - lo], "keys_out")
                        act.wait_ge(sem("keys_out"), at)

                def stage(n, k):
                    f(q_stage[0][:, k, :], unit_rows(n), ACT.Copy).then_inc(sem("q_high"), 1)
                    act.wait_ge(sem("q_high"), n + (64 * which + 1))

                def spread(n, k):
                    act.wait_ge(sem("biased"), n + (64 * which + 1))
                    for half in range(2):
                        lo, hi = (0, 2 * BANK) if half == 0 else (2 * BANK, S_CTX)
                        name = "exp" + "AB"[half]
                        f(prob[k][:, lo:hi], bank(0, 4)[:, lo:hi], ACT.Exp, bias=u_bias[k], scale=scale,
                          accum_out=u_sum[k][:, half:half + 1]).then_inc(sem(name), 1)
                        act.wait_ge(sem(name), n + (64 * which + 1))

                def z_out(u):
                    act.wait_ge(sem("zT_ready"), u + (64 * which + 1))
                    settle()
                    affine(unit_rows(u), bank(7)[:, 0:P], "zT_stored")
                    act.wait_ge(sem("zT_stored"), u + (64 * which + 1))

                def turned(u, k, first, nxt, after):
                    for i in range(2):
                        at = u * 2 + (128 * which + i + 1)
                        act.wait_ge(sem("turned_s"), at)
                        f(probT[:, 4 * i:4 * i + 4, :], bank(4 + i).rearrange("p (n c) -> p n c", c=P), ACT.Copy).then_inc(sem("turned_out_s"), 1)
                        act.wait_ge(sem("turned_out_s"), at)
                        if i == 0 and after:
                            stage(u + 2, k)
                    if not first:
                        z_out(u - 1)
                    if nxt:
                        spread(u + 1, 1 - k)

                def batch(b, slot, first, final):
                    pairs(act, settle, first, 2, lambda h, k, f: turned(b * 8 + h, k, f, True, True))
                    if which == 0 and not final:
                        keys_std(b + 1)
                    for h in range(4, 8):
                        if h == 6 and not final:
                            keys_out(b + 1)
                        turned(b * 8 + h, h % 2, False, h < 7 or not final, h < 6 or not final)

                def keys_std(b):
                    act.wait_ge(sem("ctx_vars"), b + 1)
                    f(ctx_std, ctx_var, ACT.Sqrt, bias=cst[:, 0:1], scale=1.0 / CC).then_inc(sem("ctx_stds"), 1)
                    act.wait_ge(sem("ctx_stds"), b + 1)

                if which == 0:
                    keys_std(0)
                    act.wait_ge(sem("ctx_affine"), 32)
                keys_out(0)
                stage(0, 0)
                stage(1, 1)
                ready(ACT.Exp)
                spread(0, 0)
                units(act, batch)
                z_out(8 * NB - 1)
                copies(name + "_o", n_chunk, lambda i: x_OT[:, i, :])

            copies("x_in", 2, lambda i: X[:, i, :])
            act.wait_ge(sem("constants"), 1)
            norm("x", twice=True)
            sg.layer("params")
            b = sg.take()
            sg.release(f(par[:], b[:, 0:KC * NROW], ACT.Copy))
            ne = len(EROWS)
            for m, (e0, en) in enumerate(EC):
                b = sg.take()
                sg.release(f(epar[0:en, m * ne:(m + 1) * ne], b[0:en, 0:ne], ACT.Copy))
            norm("a1_x")
            copies("a1_q", 4, lambda i: a1["QT"][:, i, :])
            copies("a1_v", NB, lambda i: a1["V"][:, i, :], rows=slice(0, T))
            core(0, a1, 32 ** -0.5, 4)
            norm("a1_m")
            ready(ACT.Gelu)
            copies("a1_h", MC, lambda i: a1["HT"][:, i, :], ACT.Gelu, lambda i: col("L0_xattn_a1_li2_b", i))
            norm("mid")
            norm("a2_x")
            cross(0, "a2", 4, 32 ** -0.5)
            norm("a2_m")
            ready(ACT.Gelu)
            copies("a2_h", MC, lambda i: x_HT[:, i, :], ACT.Gelu, lambda i: col("L0_xattn_a2_li2_b", i))
            norm("lin")

            ready(ACT.Exp)
            sg.layer("lin_v")
            for i in range(16):
                act.wait_ge(sem("elu_clamped"), i + 1)
                f(elu[:, i % 2, :], elu[:, i % 2, :], ACT.Exp).then_inc(sem("elu_exp"), 1)
                act.wait_ge(sem("elu_exp"), i + 1)
                b = sg.take()
                sg.release(f(lin["V"][:, i // 2, (i % 2) * BANK:(i % 2 + 1) * BANK], b[0:T, :], ACT.Copy))
            act.wait_ge(sem("lin_abs"), 1)
            chain(f(lin["la"], lin["la"], ACT.Exp, scale=-1.0))
            f(lin["la"], lin["la"], ACT.Ln, bias=1.0).then_inc(sem("lin_log"), 1)
            act.wait_ge(sem("lin_log"), 1)
            core(1, lin, 1.0, 8)
            norm("ffn")
            copies("ffn_q", 4, lambda i: ffn["QT"][:, i, :])
            copies("ffn_v", PAIRS, lambda i: ffn["V"][:, i, :])
            core(2, ffn, 1.0 / 16, 4)
            ready(ACT.Sqrt)
            for i in range(2):
                act.wait_ge(sem("v_emptied"), v_done(("ffn_o", "ffn_f")[i]))
                f(sq[:], ffn[("z", "z2")[i]], ACT.Square).then_inc(sem("l2_squared"), 1)
                act.wait_ge(sem("l2_squared"), i + 1)
                act.wait_ge(sem("l2_sum"), i + 1)
                f(l_std, bank(4)[:, 0:4], ACT.Sqrt, scale=float(C)).then_inc(sem("l2_norm"), 1)
                act.wait_ge(sem("l2_norm"), i + 1)
            ready(ACT.Gelu)
            act.wait_ge(sem("l2_out"), 2)
            f(ffn["z2"], ffn["z2"], ACT.Gelu).then_inc(sem("ffn_gelu"), 1)
            act.wait_ge(sem("ffn_gelu"), 1)
            norm("x1")
            cross(1, "x1", 8, 64 ** -0.5)
            settle.finish(sem("constants"))
            norm("rw")
            ready(ACT.Gelu)
            for i, n in enumerate("rkv"):
                sg.layer("rw_" + n)
                for m, (e0, en) in enumerate(EC):
                    b = sg.take()
                    j = m * ne + EROWS.index("L1_attn_" + n + "b1")
                    if i and m == 0:
                        act.wait_ge(sem("v_filled"), v_done("rw_" + "rkv"[i - 1] + "2"))
                    sg.release(f(rw_HT[0:en, m, :], b[0:en, :], ACT.Gelu, bias=epar[0:en, j:j + 1]))
            ready(ACT.Sigmoid)
            copies("rw_g", 1, lambda i: rw_lo, rows=slice(0, LORA))
            for m in range(KC):
                b = sg.take()
                sg.release(f(gate[:, m, :], b, ACT.Sigmoid))
            for n in "ad":
                if n == "d":
                    act.wait_ge(sem("v_filled"), v_done("rw_a2"))
                copies("rw_" + n, 1, lambda i: rw_lo, rows=slice(0, LORA))
            act.wait_ge(sem("heads_biased"), 1)
            f(hd["a"], hd["a"], ACT.Sigmoid).then_inc(sem("heads_act"), 1)
            chain(f(hd["d"], hd["d"], ACT.Tanh))
            chain(f(hd["d"], hd["d"], ACT.Sigmoid))
            ready(ACT.Sqrt)
            act.wait_ge(sem("heads_biased"), 2)
            f(nrm, nrm, ACT.Sqrt).then_inc(sem("heads_act"), 1)
            f(hd["d"], hd["d"], ACT.Exp, scale=-DECAY_C).then_inc(sem("heads_act"), 1)
            act.wait_ge(sem("heads_act"), 3)
            copies("rw_back", KC, lambda i: rw_xn[:, i, :])
            norm("rw_o", 1)
            ready(ACT.Gelu)
            sg.layer("rw_h")
            for m, (e0, en) in enumerate(EC):
                b = sg.take()
                j = m * ne + EROWS.index("L1_attn_ob1")
                sg.release(f(rw_HT[0:en, m, :], b[0:en, :], ACT.Gelu, bias=epar[0:en, j:j + 1]))
            def high(e, slot, m):
                if m == 0:
                    act.wait_ge(sem(f"expert_loaded{slot}"), (e - slot) * 16 + 32)
                at = m * (EXPERT // MC)
                f(moe_part[slot][0][:, at:at + EXPERT // MC], weights[0][:, slot * EXPERT + at:slot * EXPERT + at + EXPERT // MC],
                  ACT.Copy).then_inc(sem("w_high"), 1)

            norm("moe")
            ready(ACT.Exp)
            act.wait_ge(sem("norm_out"), NORM["moe"] + 1)
            f(moe_x[:, 0, :, :], moe_xn, ACT.Copy).then_inc(sem("x_split"), 1)
            for m in range(MC):
                high(0, 0, m)
            act.wait_ge(sem("top_gap"), 1)
            f(dlt[:, 0:4], dlt[:, 0:4], ACT.Exp).then_inc(sem("top_exp"), 1)
            act.wait_ge(sem("top_exp"), 1)
            ready(ACT.Gelu)
            copies("moe_ct", 1, lambda i: combT, rows=slice(0, NE))
            sg.layer("moe_h")

            def hidden(i, slot, then):
                e = i * 2 + slot
                for m in range(MC):
                    b = sg.take()
                    if m >= 2:
                        act.wait_ge(sem("h_low"), e * MC + (m - 1))
                    at = (m % KC) * NROW + ROW_AT["L1_ffn_b_in"] + m // KC + 4 * slot
                    sg.release(f(xc[:, m % 2, :], b, ACT.Gelu, bias=par[:, ds(i * 8 + at, 1)]))
                    if then:
                        high(e + 1, 1 - slot, m)

            with loop(act, 0, NE // 2 - 1, (sg.count, 2 * MC)) as i:
                hidden(i, 0, True)
                hidden(i, 1, True)
            hidden(NE // 2 - 1, 0, True)
            hidden(NE // 2 - 1, 1, False)

        @block.vector
        def _(dve):
            settle = Settle(dve)
            chain = Chain(dve, sem("vector_order"))
            v = nc.vector
            vg = Groups(dve, (bank(2), bank(3)), sem("v_filled"), sem("v_emptied"), VECTOR_GROUPS)

            def signal(ins, name, value=1):
                ins.then_inc(sem(name), 1)
                dve.wait_ge(sem(name), value)

            def v_affine(src, dst, g, b, k):
                return lambda: v.tensor_scalar(dst[:, k, :], src[:, k, :], col(g, k), col(b, k), ALU.mult, ALU.add)

            def norm(name, src, outs):
                i = NORM[name]
                dve.wait_ge(sem("norm_mean"), i + 1)
                for k in range(KC):
                    v.tensor_tensor(xc[:, k, :], src[:, k, :], bank(4), ALU.subtract).then_inc(sem("norm_centered"), 1)
                dve.wait_ge(sem("norm_centered"), 2 * i + KC)
                dve.wait_ge(sem("norm_std"), i + 1)
                signal(v.reciprocal(l_rstd, l_std), "norm_inverse", i + 1)
                dve.wait_ge(sem("norm_rstd"), i + 1)
                if i == 0:
                    dve.wait_ge(sem("s_emptied"), s_done("params"))
                shared = len(outs) > 1
                if shared:
                    chain.beside(v.tensor_tensor(xc[:, 0, :], xc[:, 0, :], bank(5), ALU.mult))
                    chain(v.tensor_tensor(xc[:, 1, :], xc[:, 1, :], bank(5), ALU.mult))
                    ops = [v_affine(xc, dst, g, b, k) for dst, g, b in outs for k in range(KC)]
                else:
                    dst, g, b = outs[0]
                    ops = [lambda k=k: v.tensor_tensor(dst[:, k, :], xc[:, k, :], bank(5), ALU.mult) for k in range(KC)]
                    if g is not None:
                        chain.beside(ops[0]())
                        chain(ops[1]())
                        ops = [v_affine(dst, dst, g, b, k) for k in range(KC)]
                for op in ops[:-2]:
                    chain.beside(op())
                chain(ops[-2]())
                signal(ops[-1](), "norm_out", i + 1)

            def add_into(name, dst, bias, extra):
                vg.layer(name)
                for k in range(KC):
                    b = vg.take()
                    if bias is None:
                        vg.release(v.tensor_tensor(dst[:, k, :], b, extra[:, k, :], ALU.add))
                    else:
                        vg.release(v.scalar_tensor_tensor(out=dst[:, k, :], in0=b, scalar=col(bias, k), in1=extra[:, k, :],
                                                          op0=ALU.add, op1=ALU.add))

            def core(which, d):
                per, nch = (4, 4) if which != 1 else (2, 8)
                full = [P, per, nch, T]
                S = bank(0, per).rearrange("p (g c s) -> p g c s", g=per, s=T)[:, :, 0:nch, :]

                def heads(ap):
                    return ap.rearrange("p (g c) s -> p g c s", g=per)

                def spread(ap):
                    return bc(ap.rearrange("p (g c) -> p g c", g=per).unsqueeze(3), full)

                def over(mask):
                    return bc(mask[:].unsqueeze(1), [P, H, T])

                def spread_decays(p):
                    la = d["la"][:, p, :].rearrange("p (c g) -> p g c", g=per)
                    for g in range(per):
                        ins = v.tensor_tensor(heads(d["decay"])[:, g, :, :], bc(la[:, g, :].unsqueeze(2), [P, nch, T]),
                                              bc(after_s[:].unsqueeze(1), [P, nch, T]), ALU.mult)
                        if g < per - 1:
                            chain(ins)
                    signal(ins, "lin_spread", p + 1)

                def take(p):
                    done, prob = p + which * PAIRS, d["prob"][p % 2]
                    dve.wait_ge(sem("core_scores"), done + 1)
                    if which == 1:
                        dve.wait_ge(sem("core_exp"), done + 1)
                        signal(v.tensor_tensor(heads(prob), S, heads(d["decay"]), ALU.mult), "core_taken", done + 1)
                    else:
                        chain(v.tensor_reduce(mx16, S, AX, ALU.max))
                        signal(v.tensor_tensor(heads(prob), S, spread(mx16), ALU.subtract), "core_taken", done + 1)

                def weights(p):
                    done, prob = p + which * PAIRS, d["prob"][p % 2]
                    if which == 1:
                        chain(v.tensor_tensor(prob, prob, over(upto_t), ALU.mult))
                        chain(v.tensor_reduce(sum16, prob, AX, ALU.add))
                        chain(v.tensor_scalar(sum16, sum16, 1e-6, None, ALU.add))
                    else:
                        dve.wait_ge(sem("core_exp"), done + 1)
                        chain(v.tensor_reduce(sum16, prob, AX, ALU.add))
                    chain(v.reciprocal(rec16, sum16))
                    ins = v.tensor_tensor(heads(prob), heads(prob), spread(rec16), ALU.mult)
                    if which == 0:
                        chain(ins)
                        ins = v.tensor_tensor(prob, prob, over(above_q), ALU.mult)
                    signal(ins, "core_probs", done + 1)

                def turned(p, i):
                    at = 2 * (p + which * PAIRS) + i // 2 + 1
                    dve.wait_ge(sem("core_turned_v"), at)
                    signal(v.tensor_copy(d["probT"][:, 4 * i:4 * i + 4, :], bank(5)[0:T, :].rearrange("p (h s) -> p h s", h=4)),
                           "core_pT_v", at)

                if which == 1:
                    spread_decays(0)
                take(0)
                if which == 1:
                    spread_decays(1)
                weights(0)
                for p in range(PAIRS):
                    if which < 2:
                        turned(p, 1)
                    if p < PAIRS - 1:
                        take(p + 1)
                    if which < 2:
                        turned(p, 3)
                    if which == 1 and p < PAIRS - 2:
                        spread_decays(p + 2)
                    if p < PAIRS - 1:
                        weights(p + 1)

            def cross(which, scale):
                full = [P, NT, CC]

                def keys_mean(b):
                    dve.wait_ge(sem("ctx_loaded"), b * 32 + 32)
                    signal(v.tensor_reduce(ctx_sum, raw, AX, ALU.add), "ctx_sums", b + 1)
                    signal(v.tensor_scalar(ctx_mean, ctx_sum, 1.0 / CC, None, ALU.mult), "ctx_means", b + 1)

                def keys_rstd(b):
                    dve.wait_ge(sem("ctx_squared"), b + 1)
                    signal(v.tensor_reduce(ctx_var, ctx_sq, AX, ALU.add), "ctx_vars", b + 1)
                    dve.wait_ge(sem("ctx_stds"), b + 1)
                    signal(v.reciprocal(ctx_rstd, ctx_std), "ctx_rstds", b + 1)

                def keys_out(b, slot, half):
                    for i in (2 * half, 2 * half + 1):
                        at = b * 4 + (which * NB * 4 + i + 1)
                        lo, hi = i * BANK, min((i + 1) * BANK, S_CTX)
                        dve.wait_ge(sem("keys_out"), at)
                        signal(v.tensor_copy(keysT[0][:, slot, lo:hi], keys_full[:, lo:hi]), "keys_high", at)
                        signal(v.tensor_tensor(keysT[1][:, slot, lo:hi], keys_full[:, lo:hi], keysT[0][:, slot, lo:hi], ALU.subtract), "keys_split", at)

                def stage(n, k):
                    dve.wait_ge(sem("q_high"), n + (64 * which + 1))
                    signal(v.tensor_tensor(q_stage[1][:, k, :], unit_rows(n), q_stage[0][:, k, :], ALU.subtract), "q_staged",
                           n + (64 * which + 1))

                def peak(n, k):
                    g = n + 64 * which
                    for half in range(2):
                        dve.wait_ge(sem("scores" + "AB"[half]), g + 1)
                        lo, hi = (0, 2 * BANK) if half == 0 else (2 * BANK, S_CTX)
                        signal(v.tensor_reduce(u_max[:, half:half + 1], bank(0, 4)[:, lo:hi], AX, ALU.max), "peak" + "AB"[half], g + 1)
                    signal(v.tensor_scalar(u_bias[k], u_max[:, 0:1], u_max[:, 1:2], -scale, ALU.max, ALU.mult), "biased", g + 1)

                def weigh(u, k, nxt, after):
                    if nxt:
                        peak(u + 1, 1 - k)
                    if after:
                        stage(u + 2, k)
                    for i in (2, 3):
                        n, tiles = (P, 4) if i == 2 else (TAIL, 1)
                        at = u * 2 + (128 * which + i - 1)
                        dve.wait_ge(sem("turned_v"), at)
                        signal(v.tensor_copy(probT[0:n, 4 * i:4 * i + tiles, :],
                                             bank(2 + i)[0:n, 0:tiles * P].rearrange("p (n c) -> p n c", c=P)),
                               "turned_out_v", at)
                    g = u + (64 * which + 1)
                    signal(v.tensor_tensor(u_total, u_sum[k][:, 0:1], u_sum[k][:, 1:2], ALU.add), "summed", g)
                    signal(v.reciprocal(u_rec, u_total), "sum_inverted", g)
                    dve.wait_ge(sem("z_ready"), g)
                    signal(v.tensor_scalar(z_stage, bank(6)[:, 0:CC], u_rec, None, ALU.mult), "z_scaled", g)

                def batch(b, slot, first, final):
                    if which == 0 and not final:
                        keys_mean(b + 1)
                    pairs(dve, settle, first, 2, lambda h, k, f: weigh(b * 8 + h, k, True, True))
                    if which == 0 and not final:
                        keys_rstd(b + 1)
                    for h in range(4, 8):
                        if h == 6 and not final:
                            keys_out(b + 1, 1 - slot, 0)
                        weigh(b * 8 + h, h % 2, h < 7 or not final, h < 6 or not final)
                        if h == 6 and not final:
                            keys_out(b + 1, 1 - slot, 1)

                if which == 0:
                    keys_mean(0)
                    keys_rstd(0)
                keys_out(0, 0, 0)
                keys_out(0, 0, 1)
                stage(0, 0)
                stage(1, 1)
                peak(0, 0)
                units(dve, batch)

            a = "L0_xattn_"
            dve.wait_ge(sem("s_emptied"), s_done("x_in"))
            norm("x", X, [(h_in, a + "ln1_g", a + "ln1_b")])
            norm("a1_x", h_in, [(hq, a + "a1_lnx_g", a + "a1_lnx_b"), (hk, a + "a1_lny_g", a + "a1_lny_b")])
            vg.layer("a1_k")
            for i in range(4):
                b = vg.take()
                vg.release(v.tensor_copy(a1["KT"][:, i, :], b))
            dve.wait_ge(sem("masks"), 1)
            core(0, a1)
            add_into("a1_li1", x_mid, a + "a1_li1_b", h_in)
            norm("a1_m", x_mid, [(hq, a + "a1_ln3_g", a + "a1_ln3_b")])
            chain(v.tensor_tensor(x_mid, x_mid, h_in, ALU.add))
            add_into("a1_li3", x_mid, a + "a1_li3_b", x_mid)
            norm("mid", x_mid, [(w_in2, a + "ln2_g", a + "ln2_b")])
            norm("a2_x", w_in2, [(x_xn, a + "a2_lnx_g", a + "a2_lnx_b")])
            dve.wait_ge(sem("ctx_affine"), 32)
            cross(0, 32 ** -0.5)
            add_into("a2_li1", x_mid2, a + "a2_li1_b", w_in2)
            norm("a2_m", x_mid2, [(x_m, a + "a2_ln3_g", a + "a2_ln3_b")])
            chain(v.tensor_tensor(x_mid2, x_mid2, w_in2, ALU.add))
            chain(v.tensor_tensor(x_mid2, x_mid2, X[:], ALU.add))
            add_into("a2_li3", X, a + "a2_li3_b", x_mid2)

            norm("lin", X, [(lin["xn"], None, None)])

            vg.layer("lin_qk")
            banks = {}

            def clamp(i):
                banks[i] = vg.take()
                signal(v.tensor_scalar(elu[:, i % 2, :], banks[i], 0.0, None, ALU.min), "elu_clamped", i + 1)

            clamp(0)
            for i in range(16):
                if i < 15:
                    clamp(i + 1)
                dve.wait_ge(sem("elu_exp"), i + 1)
                dst = lin["QT" if i % 2 == 0 else "KT"][:, i // 2, :]
                vg.release(v.scalar_tensor_tensor(out=dst, in0=banks[i], scalar=0.0, in1=elu[:, i % 2, :],
                                                  op0=ALU.max, op1=ALU.add), int(i < 15))
            vg.layer("lin_a")
            dve.wait_ge(sem("lin_bias"), 16)
            b = vg.take()
            vg.release(v.tensor_tensor(lin["z"], b[:, 0:PAIRS * H].rearrange("p (n h) -> p n h", h=H),
                                       bc(lin["ba"].unsqueeze(1), [P, PAIRS, H]), ALU.add))
            chain(v.tensor_scalar(lin["z"], lin["z"], 2.0, None, ALU.add))
            signal(v.scalar_tensor_tensor(out=lin["la"], in0=lin["z"], scalar=-1.0, in1=lin["z"], op0=ALU.mult, op1=ALU.max), "lin_abs")
            dve.wait_ge(sem("lin_log"), 1)
            chain(v.scalar_tensor_tensor(out=lin["la"], in0=lin["z"], scalar=0.0, in1=lin["la"], op0=ALU.min, op1=ALU.subtract))
            core(1, lin)
            add_into("lin_o", X, None, X)

            norm("ffn", X, [(ffn["xn"], None, None)])
            vg.layer("ffn_k")
            for i in range(4):
                b = vg.take()
                vg.release(v.tensor_copy(ffn["KT"][:, i, :], b))
            core(2, ffn)
            for i in range(2):
                z = ffn[("z", "z2")[i]]
                vg.layer(("ffn_o", "ffn_f")[i])
                for k in range(KC):
                    b = vg.take()
                    vg.release(v.tensor_copy(z[:, k, :], b))
                dve.wait_ge(sem("l2_norm"), i + 1)
                chain(v.tensor_scalar(l_std, l_std, 1e-12, None, ALU.max))
                signal(v.reciprocal(l_rstd, l_std), "l2_inverse", i + 1)
                dve.wait_ge(sem("l2_factor"), i + 1)
                chain(v.tensor_tensor(z[:, 0, :], z[:, 0, :], bank(4), ALU.mult))
                signal(v.tensor_tensor(z[:, 1, :], z[:, 1, :], bank(4), ALU.mult), "l2_out", i + 1)
            dve.wait_ge(sem("ffn_gelu"), 1)
            signal(v.tensor_tensor(X[:], X[:], ffn["z2"], ALU.add), "ffn_added")

            norm("x1", X, [(x_xn, None, None)])
            cross(1, 64 ** -0.5)
            add_into("x1_out", X, "L1_xattn_bo", X)

            settle.finish(sem("constants"))
            norm("rw", X, [(rw_xn, None, None)])
            vg.layer("rw_heads")
            b = vg.take()
            vg.release(v.tensor_copy(headpar[:].rearrange("p i n -> p (i n)"), b[:, 0:P]))
            HP = {n: bc(headpar[:, i:i + 1, :], [P, T, 16]) for i, n in enumerate(HEADROWS)}

            def shift(i):
                n = "rkvgad"[i]
                if i:
                    dve.wait_ge(sem("s_filled"), s_done("rw_" + "rkvgad"[i - 1]) - (2 if i == 4 else 0))
                mu = "L1_attn_mu_" + n
                chain(v.tensor_scalar(rw_in[:, 0, :], rw_xn[:, 0, :], col(mu, 0), None, ALU.add))
                signal(v.tensor_scalar(rw_in[:, 1, :], rw_xn[:, 1, :], col(mu, 1), None, ALU.add), "rw_shifted", i + 1)

            def latents_out(i):
                n = "rkvad"[i]
                if i >= 2:
                    dve.wait_ge(sem("scratch_written"), 16 * (i - 1))
                vg.layer("rw_" + n + "2")
                for p in range(4):
                    b = vg.take()
                    vg.release(v.tensor_copy(rw_tm[:, i % 2, p * C:(p + 1) * C], b[:, 0:C]))

            shift(0)
            shift(1)
            latents_out(0)
            shift(2)
            latents_out(1)
            shift(3)
            latents_out(2)
            shift(4)
            shift(5)
            latents_out(3)
            latents_out(4)
            t16 = [P, T, 16]
            chain(v.memset(hist[:, 0, :, :], 0.0))
            dve.wait_ge(sem("heads_loaded"), 16 * NB * 5)
            chain(v.tensor_tensor(hd["a"], hd["a"], HP["ab"], ALU.add))
            signal(v.tensor_tensor(hd["d"], hd["d"], HP["db"], ALU.add), "heads_biased", 1)
            for n in "rkv":
                chain(v.tensor_tensor(hd[n], hd[n], HP[n + "b2"], ALU.add))
            chain(v.tensor_tensor(hd["kn"], hd["k"], HP["rem_mult"], ALU.mult))
            chain(v.tensor_tensor(hd["akn"], hd["kn"], hd["kn"], ALU.mult))
            signal(v.tensor_reduce(nrm, hd["akn"], AX, ALU.add), "heads_biased", 2)
            dve.wait_ge(sem("heads_act"), 1)
            chain(v.scalar_tensor_tensor(out=hd["akn"], in0=hd["a"], scalar=-1.0, in1=HP["iclr_mix"], op0=ALU.add, op1=ALU.mult))
            chain(v.scalar_tensor_tensor(out=hd["rk"], in0=hd["akn"], scalar=1.0, in1=hd["k"], op0=ALU.add, op1=ALU.mult))
            chain(v.tensor_tensor(hd["bonus"], hd["r"], hd["rk"], ALU.mult))
            dve.wait_ge(sem("heads_act"), 2)
            chain(v.tensor_scalar(nrm, nrm, 1e-12, None, ALU.max))
            chain(v.reciprocal(nrm2, nrm))
            chain(v.tensor_tensor(hd["kn"], hd["kn"], bc(nrm2.unsqueeze(2), t16), ALU.mult))
            chain(v.tensor_tensor(hd["akn"], hd["a"], hd["kn"], ALU.mult))
            chain(v.tensor_reduce(nrm, hd["bonus"], AX, ALU.add))
            chain(v.tensor_scalar(nrm, nrm, 0.2, None, ALU.mult))
            chain(v.tensor_tensor(hd["bonus"], hd["v"], HP["bonus_mult"], ALU.mult))
            chain(v.tensor_tensor(hd["bonus"], hd["bonus"], bc(nrm.unsqueeze(2), t16), ALU.mult))
            dve.wait_ge(sem("heads_act"), 3)
            signal(v.memset(hist[:, 1, :, :], 0.0), "state", 1)
            jk = [P, 16, 16]
            r_at = hd["k"].shape[1] * 16
            with loop(dve, 0, T // STEPS, (chain.count, 4 * STEPS)) as i:
                for step in range(STEPS):
                    t = i * STEPS + step
                    wT = hist[:, ds(t + 1, 1), :, :].rearrange("p o j k -> p (o k) j")
                    chain(v.tensor_tensor(s_tmp, wT, bc(hd["akn"][:, ds(t, 1), :], jk), ALU.mult))
                    chain(v.tensor_reduce(s_row, s_tmp, AX, ALU.add))
                    chain.beside(v.tensor_tensor(s_tmp, bc(hd["kn"][:, ds(t, 1), :].rearrange("p o j -> p j o"), jk),
                                                 bc(s_row.unsqueeze(1), jk), ALU.mult))
                    seen = hist[:, ds(t, 1), :, :].rearrange("p o j k -> p (o j) k")
                    query = work[:, ds(t * 16 + (r_at - 32), 16)].unsqueeze(1)
                    chain.beside(v.tensor_tensor(seen, seen, bc(query, jk), ALU.mult))
                    dve.wait_ge(chain.sem, chain.count.value - 1)
                    dve.wait_ge(sem("state_kept"), t + 1)
                    signal(v.tensor_tensor(hist[:, ds(t + 2, 1), :, :].rearrange("p o j k -> p (o j) k"), s_keep, s_tmp, ALU.subtract),
                           "state", t + 2)
            chain(v.tensor_tensor(hist[:, T:T + 2, :, :], hist[:, T:T + 2, :, :],
                                  bc(hd["r"][:, T - 2:T, :].unsqueeze(2), [P, 2, 16, 16]), ALU.mult))
            rest = RW_SUMS[-1][1]
            chain(v.tensor_reduce(hd["v"][:, rest:T, :], hist[:, rest + 2:T + 2, :, :], AX, ALU.add))
            chain(v.tensor_tensor(hd["v"][:, rest:T, :], hd["v"][:, rest:T, :], hd["bonus"][:, rest:T, :], ALU.add))
            vg.layer("rw_sums")
            for lo, hi in RW_SUMS:
                b = vg.take()
                vg.release(v.tensor_tensor(hd["v"][:, lo:hi, :], b[:, 0:(hi - lo) * 16].rearrange("p (t j) -> p t j", j=16),
                                           hd["bonus"][:, lo:hi, :], ALU.add))
            dve.wait_ge(sem("s_emptied"), s_done("rw_back"))
            norm("rw_o", rw_xn, [(rw_in, "L1_attn_ln_g", "L1_attn_ln_b")])
            signal(v.tensor_tensor(rw_in, rw_in, gate, ALU.mult), "rw_gated")
            add_into("rw_out", X, "L1_attn_ob2", X)

            norm("moe", X, [(moe_xn, None, None)])
            vg.layer("moe_logits")
            b = vg.take()
            vg.release(v.tensor_copy(logits, b[:, 0:4 * NE].rearrange("p (n e) -> p n e", e=NE)))
            for p in range(4):
                ins = v.max(top8[:, p, :], logits[:, p, :])
                if p < 3:
                    chain.beside(ins)
                else:
                    chain(ins)
            chain.beside(v.tensor_tensor(dlt[:, 0:4].unsqueeze(2), top8[:, :, 1:2], top8[:, :, 0:1], ALU.subtract))
            for p in range(4):
                ins = v.max_index(topi[:, p, :], top8[:, p, :], logits[:, p, :])
                if p < 3:
                    chain.beside(ins)
                else:
                    chain(ins)
            signal(v.tensor_copy(topf, topi[:]), "top_gap")
            vg.layer("moe_xT")
            for p in range(4):
                b = vg.take()
                vg.release(v.tensor_copy(acc[:, p, :], b[:, 0:C]))
            dve.wait_ge(sem("top_exp"), 1)
            chain(v.tensor_scalar(dlt[:, 4:8], dlt[:, 0:4], 1.0, None, ALU.add))
            chain(v.reciprocal(dlt[:, 4:8], dlt[:, 4:8]))
            chain(v.tensor_tensor(dlt[:, 0:4], dlt[:, 0:4], dlt[:, 4:8], ALU.mult))
            dve.wait_ge(sem("iota"), 1)
            for p in range(4):
                chain.beside(v.tensor_scalar(hot[:, p, :], iota8, topf[:, p, 0:1], dlt[:, 4 + p:5 + p], ALU.is_equal, ALU.mult))
                ins = v.tensor_scalar(hot2[:, p, :], iota8, topf[:, p, 1:2], dlt[:, p:p + 1], ALU.is_equal, ALU.mult)
                if p < 3:
                    chain.beside(ins)
                else:
                    chain(ins)
            signal(v.tensor_tensor(comb, hot, hot2, ALU.add), "combined")
            dve.wait_ge(sem("x_split"), 1)
            signal(v.tensor_tensor(moe_x[:, 1, :, :], moe_xn, moe_x[:, 0, :, :], ALU.subtract), "x_split", 2)
            vg.layer("moe_b")
            for p in range(4):
                b = vg.take()
                vg.release(v.tensor_tensor(acc[:, p, :], b[:, 0:C], acc[:, p, :], ALU.add))
            vg.layer("moe_y")
            with loop(dve, 0, NE // 2, (vg.count, 2 * PAIRS)) as i:
                for slot in range(2):
                    for m in range(MC):
                        at = (i * 2 + slot) * MC + (m + 1)
                        dve.wait_ge(sem("s_emptied"), (i * 2 + slot) * MC + (s_done("moe_ct") + m + 1))
                        signal(v.tensor_copy(moe_h[:, 0, m, :], xc[:, m % 2, :]), "h_high", at)
                        signal(v.tensor_tensor(moe_h[:, 1, m, :], xc[:, m % 2, :], moe_h[:, 0, m, :], ALU.subtract), "h_low", at)
                    for p in range(PAIRS):
                        b = vg.take()
                        vg.release(v.scalar_tensor_tensor(out=acc[:, p, :], in0=b[:, 0:C], scalar=comb[:, p, ds(i * 2 + slot, 1)],
                                                          in1=acc[:, p, :], op0=ALU.mult, op1=ALU.add))


_UNUSED = ("L1_attn_keys", "L1_attn_values", "L1_attn_attn_mask")
_OUT = (NB, T, C)


def kernel(**inputs):
    import numpy as _np
    import concourse.bacc as _bacc
    from concourse.bass_utils import run_bass_kernel_spmd as _run

    nc = _bacc.Bacc("TRN2", target_bir_lowering=False, num_devices=1)
    arrays, io = {}, {}
    for name, a in inputs.items():
        if name in _UNUSED:
            continue
        a = _np.ascontiguousarray(a)
        arrays[f"in_{name}"] = a
        io[name] = nc.dram_tensor(f"in_{name}", a.shape, mybir.dt.from_np(a.dtype), kind="ExternalInput").ap()
    out = nc.dram_tensor("out", _OUT, F32, kind="ExternalOutput").ap()
    perceiver_kernel(nc, io, out)
    r = _run(nc, [arrays], core_ids=[0])
    return r.results[0]["out"]
```
